# Optimizing a Trainium2 kernel written in Bass

```python
import numpy as np
import jax
import jax.numpy as jnp

def _softmax(x, axis=-1):
    return jax.nn.softmax(x, axis=axis)

def _gelu(x):
    return jax.nn.gelu(x, approximate=True)

def _silu(x):
    return jax.nn.silu(x)

def _sigmoid(x):
    return jax.nn.sigmoid(x)

def _layernorm(x, axis=-1, eps=1e-05):
    m = jnp.mean(x, axis=axis, keepdims=True)
    v = jnp.var(x, axis=axis, keepdims=True)
    return (x - m) / jnp.sqrt(v + eps)

def _scatter_add(tgt, idx, src, axis=0):
    return tgt.at[idx].add(src)

def _segment_sum(src, seg, n):
    return jax.ops.segment_sum(src, seg, n)
kernel_name = 'mk_gnn_ffn_d1_gnn_r32_ab21f8'

def setup_inputs(seed: int=0):
    np.random.seed(seed)
    _w = jnp.asarray

    def _rec_inputs():
        import jax
        import jax.numpy as jnp
        _gk = jax.random.key(seed)
        x = -0.0002117 + 1 * jax.random.normal(jax.random.fold_in(_gk, 1), (3125, 256), jnp.float32)
        src = jax.random.randint(jax.random.fold_in(_gk, 2), (50000,), 0, 3125, jnp.int32)
        dst = jax.random.randint(jax.random.fold_in(_gk, 3), (50000,), 0, 3125, jnp.int32)
        _o = jnp.argsort(dst, stable=True)
        src = src[_o]
        dst = dst[_o]
        return (x, src, dst)
    x, src, dst = _rec_inputs()

    def _L0_gnn_setup():
        import jax, jax.numpy as jnp
        import numpy as np
        N = 3125
        E = 50000
        D = 256
        BN_EPS = 1e-05
        key = jax.random.key(seed)
        ks = jax.random.split(key, 6)
        node_feats = jax.random.normal(ks[0], (N, D), dtype=jnp.float32)
        src = jax.random.randint(ks[1], (E,), 0, N, dtype=jnp.int64)
        dst = jax.random.randint(ks[2], (E,), 0, N, dtype=jnp.int64)
        eps = jnp.zeros((1,), dtype=jnp.float32)
        W1 = jax.random.normal(ks[3], (D, 2 * D), dtype=jnp.float32) * (1.0 / np.sqrt(D))
        b1 = jnp.zeros((2 * D,), dtype=jnp.float32)
        W2 = jax.random.normal(ks[4], (2 * D, D), dtype=jnp.float32) * (1.0 / np.sqrt(2 * D))
        b2 = jnp.zeros((D,), dtype=jnp.float32)
        gamma = jnp.ones((D,), dtype=jnp.float32)
        beta = jnp.zeros((D,), dtype=jnp.float32)
        return {'node_feats': node_feats, 'src': src, 'dst': dst, 'eps': eps, 'W1': W1, 'b1': b1, 'W2': W2, 'b2': b2, 'gamma': gamma, 'beta': beta}
    _L0_gnn_all = _L0_gnn_setup()
    _L0_gnn_in = {k: v for k, v in _L0_gnn_all.items() if k in ('eps', 'W1', 'b1', 'W2', 'b2', 'gamma', 'beta')}
    del _L0_gnn_all

    def _L0_ffn_setup():
        import jax, jax.numpy as jnp
        import numpy as np
        B, K, D = (512, 16, 256)
        E = 32
        H = int(D * 0.25)
        key = jax.random.key(seed)
        ks = jax.random.split(key, 7)
        d_rs = D ** (-0.5)
        h_rs = H ** (-0.5)
        x = jax.random.normal(ks[0], (B, K, D), dtype=jnp.float32)
        router_w = jax.random.uniform(ks[1], (E, D), jnp.float32, -d_rs, d_rs)
        router_b = jax.random.uniform(ks[2], (E,), jnp.float32, -d_rs, d_rs)
        W1 = jax.random.uniform(ks[3], (E, D, H), jnp.float32, -h_rs, h_rs)
        b1 = jax.random.uniform(ks[4], (E, H), jnp.float32, -h_rs, h_rs)
        W2 = jax.random.uniform(ks[5], (E, H, D), jnp.float32, -d_rs, d_rs)
        b2 = jax.random.uniform(ks[6], (E, D), jnp.float32, -d_rs, d_rs)
        return {'x': x, 'router_w': router_w, 'router_b': router_b, 'W1': W1, 'b1': b1, 'W2': W2, 'b2': b2}
    _L0_ffn_all = _L0_ffn_setup()
    _L0_ffn_in = {k: v for k, v in _L0_ffn_all.items() if k in ('router_w', 'router_b', 'W1', 'b1', 'W2', 'b2')}
    del _L0_ffn_all
    return {'x': x, 'src': src, 'dst': dst, 'L0_gnn_eps': _L0_gnn_in['eps'], 'L0_gnn_W1': _L0_gnn_in['W1'], 'L0_gnn_b1': _L0_gnn_in['b1'], 'L0_gnn_W2': _L0_gnn_in['W2'], 'L0_gnn_b2': _L0_gnn_in['b2'], 'L0_gnn_gamma': _L0_gnn_in['gamma'], 'L0_gnn_beta': _L0_gnn_in['beta'], 'L0_ffn_router_w': _L0_ffn_in['router_w'], 'L0_ffn_router_b': _L0_ffn_in['router_b'], 'L0_ffn_W1': _L0_ffn_in['W1'], 'L0_ffn_b1': _L0_ffn_in['b1'], 'L0_ffn_W2': _L0_ffn_in['W2'], 'L0_ffn_b2': _L0_ffn_in['b2']}

def reference(x, src, dst, L0_gnn_eps, L0_gnn_W1, L0_gnn_b1, L0_gnn_W2, L0_gnn_b2, L0_gnn_gamma, L0_gnn_beta, L0_ffn_router_w, L0_ffn_router_b, L0_ffn_W1, L0_ffn_b1, L0_ffn_W2, L0_ffn_b2):
    import jax
    import jax.numpy as jnp

    def _L0_gnn_ref(node_feats, src, dst, eps, W1, b1, W2, b2, gamma, beta):
        import jax, jax.numpy as jnp
        import numpy as np
        N = 3125
        E = 50000
        D = 256
        BN_EPS = 1e-05
        n = node_feats.shape[0]
        neigh = jax.ops.segment_sum(node_feats[src], dst, num_segments=n)
        h = (1.0 + eps) * node_feats + neigh
        h = jax.nn.relu(h @ W1 + b1) @ W2 + b2
        mean = jnp.mean(h, axis=0)
        var = jnp.mean(jnp.square(h - mean), axis=0)
        h = (h - mean) * jax.lax.rsqrt(var + BN_EPS) * gamma + beta
        return h

    def _L0_ffn_ref(x, router_w, router_b, W1, b1, W2, b2):
        import jax, jax.numpy as jnp
        import numpy as np
        B, K, D = (512, 16, 256)
        E = 32
        H = int(D * 0.25)
        xf = x.reshape(-1, D)
        logits = xf @ router_w.T + router_b
        idx = jnp.argmax(logits, axis=-1)
        w1t = jnp.take(W1, idx, axis=0)
        h = jnp.einsum('nd,ndh->nh', xf, w1t) + jnp.take(b1, idx, axis=0)
        h = jax.nn.relu(h)
        w2t = jnp.take(W2, idx, axis=0)
        out = jnp.einsum('nh,nhd->nd', h, w2t) + jnp.take(b2, idx, axis=0)
        out = jax.nn.relu(out)
        return out.reshape(x.shape)
    x = x + _L0_gnn_ref(_layernorm(x, axis=-1), src, dst, L0_gnn_eps, L0_gnn_W1, L0_gnn_b1, L0_gnn_W2, L0_gnn_b2, L0_gnn_gamma, L0_gnn_beta)
    x = x + _L0_ffn_ref(_layernorm(x, axis=-1)[None], L0_ffn_router_w, L0_ffn_router_b, L0_ffn_W1, L0_ffn_b1, L0_ffn_W2, L0_ffn_b2)[0]
    return x

_drawn_inputs = setup_inputs


def setup_inputs(seed=0):
    import zlib

    import numpy as np

    out = dict(_drawn_inputs(seed))
    spreads = {'L0_gnn_b1': (0.0, 0.348),
     'L0_gnn_b2': (0.0, 0.8),
     'L0_gnn_gamma': (1.0, 0.2),
     'L0_gnn_beta': (0.0, 0.1)}
    factors = {'L0_ffn_b1': 8.0, 'L0_ffn_b2': 3.26}
    for name, (base, spread) in spreads.items():
        noise = np.random.default_rng([zlib.crc32(name.encode()), seed]).standard_normal(out[name].shape)
        drawn = base * np.exp(spread * noise) if base else spread * noise
        out[name] = jnp.asarray(drawn.astype(out[name].dtype))
    for name, factor in factors.items():
        out[name] = (out[name] * factor).astype(out[name].dtype)
    return out
```

```python
from contextlib import ExitStack

import concourse.bass as bass
from concourse import mybir

ALU = mybir.AluOpType
ACT = mybir.ActivationFunctionType
AX = mybir.AxisListType
F32 = mybir.dt.float32
F16 = mybir.dt.float16
I32 = mybir.dt.int32

P = 128
LN_EPS = 1e-5
BN_EPS = 1e-5
XSCALE = 2048.0

EPART = 125
STEP = 8
PAD_DST = 4095
SRC_BITS = 12

W = 5
QUAD = 4
BPS = 2 * QUAD
STEPS = 10
GN = STEPS * BPS * W


def ceil_div(a, b):
    return -(-a // b)


def chained(eng, sem):
    count = [0]

    def link(ins):
        count[0] += 1
        ins.then_inc(sem, 1)
        eng.wait_ge(sem, count[0])

    return link


def rsqrt(link, vec, r, root, var, t):
    link(vec.reciprocal(r, root))
    link(vec.tensor_tensor(t, r, r, ALU.mult))
    link(vec.tensor_tensor(t, t, var, ALU.mult))
    link(vec.tensor_scalar(t, t, -0.5, 1.5, ALU.mult, ALU.add))
    link(vec.tensor_tensor(r, r, t, ALU.mult))


def gnn_moe_kernel(nc, x, src, dst, eps, gw1, gb1, gw2, gb2, gamma, beta, rw, rb, ew1, eb1, ew2, eb2, out):
    N, D = x.shape
    E = src.shape[0]
    H = gw1.shape[1]
    NE, _, EH = ew1.shape
    T = ceil_div(N, P)
    LAST = N - (T - 1) * P
    KD = D // P
    KH = H // P
    EK = E // EPART
    ROWS = E // STEP
    GROUPS = ceil_div(N, GN)
    NP = GROUPS * GN
    BLOCKS = NP // W
    BC = ceil_div(BLOCKS, P)
    Z = T * W
    ZP = Z + 1
    CHUNKS = (N + NE * (P - 1)) // P
    XG = 5
    XT = T // XG
    assert NP == T * P and D == 2 * P and EPART * EK == E and T % XG == 0 and QUAD * ZP <= 512

    table = nc.dram_tensor("edge_rows", [ROWS, P], F32, kind="Internal").ap()
    slots_in = nc.dram_tensor("slots_in", [CHUNKS * P, D], F32, kind="Internal").ap()
    slots_out = nc.dram_tensor("slots_out", [CHUNKS * P, D], F32, kind="Internal").ap()

    top = ExitStack()

    def sb(name, shape, dt, ctx=top):
        return ctx.enter_context(nc.sbuf_tensor(name, shape, dt))

    def psum(name, shape, dt, ctx):
        return ctx.enter_context(nc.psum_tensor(name, shape, dt))

    def sem(name, ctx):
        return ctx.enter_context(nc.semaphore(name))

    with top:
        ident = sb("ident", [P, P], F32)
        iota16 = sb("iota16", [P, P], F16)
        ones16 = sb("ones16", [P, P], F16)
        xt = sb("xt", [P, T, D], F32)
        xs = sb("xs", [P, T, D], F32)
        xhl = sb("xhl", [P, T, 2, D], F16)
        hT = sb("hT", [P, KD, NP], F32)
        z2 = sb("z2", [P, BC * P, 2], F16)
        slo2 = sb("slo2", [P, BC * P, 2], F16)
        epsT = sb("epsT", [P, 1], F32)
        selfw = sb("selfw", [P, 1], F32)
        idx = sb("idx", [P, BC], I32)
        thr = sb("thr", [P, BC * P], F32)
        total = sb("total", [1, 1], I32)
        w1 = sb("w1", [P, KD, H], F32)
        w2 = sb("w2", [P, KH, D], F32)
        b1 = sb("b1", [P, KH], F32)
        b2 = sb("b2", [P, KD], F32)
        gam = sb("gam", [P, KD], F32)
        bet = sb("bet", [P, KD], F32)
        rwT = sb("rwT", [P, KD, NE], F32)
        rbT = sb("rbT", [NE, 1], F32)
        lneps = sb("lneps", [P, 1], F32)
        rows = sb("rows", [P, BC, P], F32)
        vi = sb("vi", [P, BC * P], I32)
        ti = sb("ti", [P, BC * P], I32)
        f0 = sb("f0", [P, BC * P], F32)
        f1 = sb("f1", [P, BC * P], F32)
        f2 = sb("f2", [P, BC * P], F32)
        found = sb("found", [P, 1], F32)

        dve, act_, pe_, pool_ = nc.vector, nc.scalar, nc.tensor, nc.gpsimd

        def gather_rows(pool, rows, gathered):
            for c in range(BC):
                pool_.indirect_dma_start(
                    rows[:, c, :], None, table, bass.IndirectOffsetOnAxis(ap=idx[:, c:c + 1], axis=0)
                ).then_inc(gathered, 16)

        def turn_rows(pe, rows, turned_ps, gathered, count, turned):
            pe.wait_ge(gathered, count)
            for c in range(BC):
                last = pe_.transpose(turned_ps[:, c * P:(c + 1) * P], rows[:, c, :], ident[:])
            last.then_inc(turned, 1)

        def unpack_rows(vec, link, turned_ps, turned, t):
            vi, ti, f0, f1, f2, found = t
            vec.wait_ge(turned, 1)
            link(dve.tensor_copy(vi[:], turned_ps[:, 0:BC * P]))
            link(dve.tensor_scalar(ti[:], vi[:], P - 1, None, ALU.bitwise_and))
            link(dve.tensor_copy(slo2[:], ti[:].unsqueeze(2).broadcast_to([P, BC * P, 2])))
            link(dve.tensor_scalar(ti[:], vi[:], 7, 31, ALU.arith_shift_right, ALU.bitwise_and))
            link(dve.tensor_copy(f0[:], ti[:]))
            link(dve.tensor_scalar(ti[:], vi[:], SRC_BITS, None, ALU.arith_shift_right))
            link(dve.tensor_tensor(f1[:], ti[:], thr[:], ALU.subtract))
            link(dve.tensor_scalar(f2[:], f1[:], 0.0, None, ALU.is_ge))
            link(dve.scalar_tensor_tensor(out=f2[:], in0=f1[:], scalar=float(W), in1=f2[:],
                                          op0=ALU.is_lt, op1=ALU.mult))
            link(dve.tensor_reduce(found[:], f2[:, 0:BLOCKS], AX.X, ALU.add))
            link(dve.scalar_tensor_tensor(out=f1[:], in0=f0[:], scalar=float(W), in1=f1[:],
                                          op0=ALU.mult, op1=ALU.add))
            link(dve.scalar_tensor_tensor(out=f1[:], in0=f1[:], scalar=1.0, in1=f2[:],
                                          op0=ALU.add, op1=ALU.mult))
            link(dve.tensor_scalar(z2[:], f1[:].unsqueeze(2).broadcast_to([P, BC * P, 2]), -1.0, None, ALU.add))

        BATCH = 4
        batches = [(t, min(BATCH, T - t)) for t in range(0, T, BATCH)]

        def turn_self(pe, selfT, xs_ready, self_turned, self_kept):
            for i, (t0, n) in enumerate(batches):
                if xs_ready is not None:
                    pe.wait_ge(xs_ready, t0 + n)
                if i >= 2:
                    pe.wait_ge(self_kept, KD * (i - 1))
                for k in range(KD):
                    for j in range(n):
                        last = pe_.transpose(selfT[:, i % 2, k, j * P:(j + 1) * P],
                                             xs[:, t0 + j, k * P:(k + 1) * P], ident[:])
                last.then_inc(self_turned, 1)

        def keep_self(act, i, selfT, self_turned, self_kept):
            t0, n = batches[i]
            act.wait_ge(self_turned, i + 1)
            for k in range(KD):
                act_.activation(hT[:, k, t0 * P:(t0 + n) * P], selfT[:, i % 2, k, 0:n * P], ACT.Copy,
                                scale=selfw[:]).then_inc(self_kept, 1)

        with ExitStack() as ctx:
            ed = sb("ed", [EPART, EK + P], I32, ctx)
            es = sb("es", [EPART, EK + P], I32, ctx)
            packed = sb("packed", [EPART, EK + P], F32, ctx)
            head = sb("head", [EPART, 1], F32, ctx)
            heads_below = sb("heads_below", [EPART, BC * P], F16, ctx)
            thrc = sb("thrc", [P, BC], F32, ctx)
            line = sb("line", [P, BC], F32, ctx)
            linei = sb("linei", [P, BC], I32, ctx)
            lines = sb("lines", [P, BC, EK], I32, ctx)
            junk = sb("junk", [P, EK], F32, ctx)
            below = sb("below", [P, BC], F32, ctx)
            start = sb("start", [P, BC], I32, ctx)
            ones32 = sb("ones32", [P, 1], F32, ctx)
            zero_row = sb("zero_row", [P, D], F32, ctx)
            stats = sb("stats", [P, T, 6], F32, ctx)
            mv = sb("mv", [P, T, 2], F32, ctx)
            var = sb("var", [P, T], F32, ctx)
            root = sb("root", [P, T], F32, ctx)
            rstd = sb("rstd", [P, T], F32, ctx)
            tmp = sb("tmp", [P, T], F32, ctx)
            counts_ps = psum("counts_ps", [P, 512], F32, ctx)
            turned_ps = psum("turned_ps", [P, 1024], F32, ctx)
            selfT = psum("selfT", [P, 2, KD, 512], F32, ctx)

            s_edges = sem("edges_in", ctx)
            s_halo = sem("halo_set", ctx)
            s_x = [sem(f"x_in{g}", ctx) for g in range(XG)]
            s_eps = sem("eps_in", ctx)
            s_w = sem("weights_in", ctx)
            s_tail = sem("tail_zeroed", ctx)
            s_const = sem("constants_made", ctx)
            s_zero = sem("zero_row_made", ctx)
            s_packed = sem("packed", ctx)
            s_table = sem("table_written", ctx)
            s_slots = sem("slots_zeroed", ctx)
            s_hb = sem("heads_compared", ctx)
            s_hc = sem("heads_counted", ctx)
            s_line = sem("lines_known", ctx)
            s_lines = sem("lines_gathered", ctx)
            s_idx = sem("rows_known", ctx)
            s_rows = sem("rows_gathered", ctx)
            s_turned = sem("rows_turned", ctx)
            s_found = sem("found_per_partition", ctx)
            s_sum = sem("found_summed", ctx)
            s_stats = sem("stats_done", ctx)
            s_dve = sem("vector_chain", ctx)
            s_var = sem("var_ready", ctx)
            s_root = sem("root_ready", ctx)
            s_xs = sem("xs_ready", ctx)
            s_hi = sem("hi_ready", ctx)
            s_lo = sem("lo_ready", ctx)
            s_selfw = sem("self_weight_ready", ctx)
            s_selfT = sem("self_turned", ctx)
            s_self = sem("self_kept", ctx)
            s_pool = sem("pool_chain", ctx)

            block = ctx.enter_context(nc.Block())

            @block.sync
            def _(sp):
                dl = dst.rearrange("(p k) -> p k", k=EK)
                sl = src.rearrange("(p k) -> p k", k=EK)
                sp.dma_start(ed[:, 0:EK], dl).then_inc(s_edges, 16)
                sp.dma_start(es[:, 0:EK], sl).then_inc(s_edges, 16)
                sp.wait_ge(s_halo, 2)
                sp.dma_start(ed[0:EPART - 1, EK:EK + P], dl[1:EPART, 0:P]).then_inc(s_edges, 16)
                sp.dma_start(es[0:EPART - 1, EK:EK + P], sl[1:EPART, 0:P]).then_inc(s_edges, 16)
                xv = x[0:(T - 1) * P, :].rearrange("(t p) d -> p t d", p=P)
                for g in range(XG):
                    a, b = g * XT, min((g + 1) * XT, T - 1)
                    sp.dma_start(xt[:, a:b, :], xv[:, a:b, :]).then_inc(s_x[g], 16)
                sp.wait_ge(s_tail, 1)
                sp.dma_start(xt[0:LAST, T - 1, :], x[(T - 1) * P:N, :]).then_inc(s_x[XG - 1], 16)
                sp.dma_start(epsT[:], eps.rearrange("(a b) -> a b", a=1).broadcast_to([P, 1])).then_inc(s_eps, 16)
                sp.wait_ge(s_packed, 1)
                overlapping = bass.AP(tensor=packed, offset=0,
                                      ap=[[EK + P, EPART], [STEP, EK // STEP], [1, P]])
                sp.dma_start(table.rearrange("(p j) e -> p j e", p=EPART), overlapping).then_inc(s_table, 16)
                for sbuf, dram in (
                    (w1[:], gw1.rearrange("(k p) h -> p k h", p=P)),
                    (w2[:], gw2.rearrange("(k p) h -> p k h", p=P)),
                    (b1[:], gb1.rearrange("(k p) -> p k", p=P)),
                    (b2[:], gb2.rearrange("(k p) -> p k", p=P)),
                    (gam[:], gamma.rearrange("(k p) -> p k", p=P)),
                    (bet[:], beta.rearrange("(k p) -> p k", p=P)),
                    (rbT[:], rb.rearrange("(e a) -> e a", a=1)),
                    (rwT[:, 0, :], rw[:, 0:P].rearrange("e p -> p e")),
                    (rwT[:, 1, :], rw[:, P:D].rearrange("e p -> p e")),
                ):
                    sp.dma_start(sbuf, dram, allow_slow_non_contiguous=True).then_inc(s_w, 16)
                sp.wait_ge(s_zero, 1)
                sp.dma_start(slots_in.rearrange("(c p) d -> p c d", p=P),
                             zero_row[:].unsqueeze(1).broadcast_to([P, CHUNKS, D])).then_inc(s_slots, 16)
                sp.wait_ge(s_w, 16 * 9)
                sp.wait_ge(s_slots, 16)
                sp.wait_ge(s_table, 16)

            @block.gpsimd
            def _(pool):
                link = chained(pool, s_pool)
                pool_.memset(ed[:, EK:EK + P], PAD_DST).then_inc(s_halo, 1)
                pool_.memset(es[:, EK:EK + P], 0).then_inc(s_halo, 1)
                pool_.memset(xt[:, T - 1, :], 0.0).then_inc(s_tail, 1)
                pool_.iota(thr[:], [[W, BC * P]], base=0, channel_multiplier=0,
                           allow_small_or_imprecise_dtypes=True).then_inc(s_const, 1)
                pool_.memset(ones16[:], 1.0).then_inc(s_const, 1)
                pool_.memset(lneps[:], LN_EPS).then_inc(s_const, 1)
                pool_.iota(thrc[:], [[W * P, BC]], base=0, channel_multiplier=W,
                           allow_small_or_imprecise_dtypes=True).then_inc(s_const, 1)
                pool_.iota(iota16[:], [[1, P]], base=0, channel_multiplier=0,
                           allow_small_or_imprecise_dtypes=True).then_inc(s_const, 1)
                link(pool_.memset(ident[:], 0.0))
                pool_.affine_select(out=ident[:], in_=ident[:], compare_op=ALU.not_equal, fill=1.0, base=0,
                                    pattern=[[-1, P]], channel_multiplier=1).then_inc(s_const, 1)
                pool_.memset(ones32[:], 1.0).then_inc(s_const, 1)
                pool_.memset(zero_row[:], 0.0).then_inc(s_zero, 1)
                pool.wait_ge(s_line, 1)
                dl = dst.rearrange("(p k) -> p k", k=EK)
                for c in range(BC):
                    pool_.indirect_dma_start(
                        lines[:, c, :], None, dl, bass.IndirectOffsetOnAxis(ap=linei[:, c:c + 1], axis=0)
                    ).then_inc(s_lines, 16)
                pool.wait_ge(s_idx, 1)
                pool.wait_ge(s_table, 16)
                gather_rows(pool, rows, s_rows)
                for i, (t, n) in enumerate(batches):
                    pool.wait_ge(s_hi, i + 1)
                    pool_.tensor_tensor(xhl[:, t:t + n, 1, :], xs[:, t:t + n, :], xhl[:, t:t + n, 0, :],
                                        ALU.subtract).then_inc(s_lo, 1)

            @block.tensor
            def _(pe):
                pe.wait_ge(s_hb, 1)
                pe.wait_ge(s_const, 7)
                for c in range(BC):
                    last = pe_.matmul(counts_ps[:, c:c + 1], heads_below[:, c * P:(c + 1) * P],
                                      ones16[0:EPART, 0:1], start=True, stop=True)
                last.then_inc(s_hc, 1)
                turn_self(pe, selfT, s_xs, s_selfT, s_self)
                turn_rows(pe, rows, turned_ps, s_rows, 16 * BC, s_turned)
                pe.wait_ge(s_found, 1)
                pe_.matmul(counts_ps[0:1, 8:9], found[:], ones32[:], start=True, stop=True).then_inc(s_sum, 1)

            @block.scalar
            def _(act):
                act.wait_ge(s_var, 1)
                act_.activation(root[:], var[:], ACT.Sqrt).then_inc(s_root, 1)
                for i, (t, n) in enumerate(batches):
                    act.wait_ge(s_xs, t + n)
                    act_.activation(xhl[:, t:t + n, 0, :], xs[:, t:t + n, :], ACT.Copy).then_inc(s_hi, 1)
                    if i == 1:
                        act.wait_ge(s_selfw, 1)
                    if i >= 1:
                        keep_self(act, i - 1, selfT, s_selfT, s_self)
                keep_self(act, len(batches) - 1, selfT, s_selfT, s_self)

            @block.vector
            def _(vec):
                link = chained(vec, s_dve)

                def group_stats(g):
                    vec.wait_ge(s_x[g], 16 if g < XG - 1 else 32)
                    with vec.Fori(g * XT, (g + 1) * XT) as t:
                        dve.bn_stats(stats[:, bass.ds(t, 1), :].rearrange("p a b -> p (a b)"),
                                     xt[:, bass.ds(t, 1), :].rearrange("p a b -> p (a b)")).then_inc(s_stats, 1)

                vec.wait_ge(s_edges, 64)
                vec.wait_ge(s_const, 7)
                dve.scalar_tensor_tensor(out=packed[:], in0=ed[:], scalar=float(1 << SRC_BITS), in1=es[:],
                                         op0=ALU.mult, op1=ALU.add).then_inc(s_packed, 1)
                link(dve.tensor_copy(head[:], ed[:, 0:1]))
                dve.tensor_scalar(heads_below[:], thr[0:EPART, :], head[:], None, ALU.is_gt).then_inc(s_hb, 1)
                group_stats(0)
                vec.wait_ge(s_hc, 1)
                link(dve.tensor_scalar(line[:], counts_ps[:, 0:BC], -1.0, 0.0, ALU.add, ALU.max))
                dve.tensor_copy(linei[:], line[:]).then_inc(s_line, 1)
                for g in range(1, XG):
                    group_stats(g)
                vec.wait_ge(s_lines, 16 * BC)
                for c in range(BC):
                    link(dve.tensor_scalar(junk[:], lines[:, c, :], thrc[:, c:c + 1], 0.0, ALU.is_lt, ALU.add,
                                           accum_out=below[:, c:c + 1]))
                link(dve.scalar_tensor_tensor(out=start[:], in0=line[:], scalar=float(EK), in1=below[:],
                                              op0=ALU.mult, op1=ALU.add))
                link(dve.tensor_scalar(start[:], start[:], STEP.bit_length() - 1, None, ALU.arith_shift_right))
                dve.tensor_scalar(idx[:], start[:], ROWS - 1, None, ALU.min).then_inc(s_idx, 1)
                vec.wait_ge(s_stats, T)
                for t in range(T):
                    last = dve.bn_aggr(mv[:, t, :], stats[:, t, :])
                link(last)
                link(dve.tensor_scalar(var[:], mv[:, :, 1], LN_EPS, None, ALU.add))
                vec.wait_ge(s_eps, 16)
                dve.tensor_scalar(selfw[:], epsT[:], 1.0, 1.0 / XSCALE, ALU.add, ALU.mult).then_inc(s_selfw, 1)
                link(dve.tensor_scalar(var[:], mv[:, :, 1], LN_EPS, None, ALU.add))
                dve.tensor_copy(tmp[:, 0:1], var[:, 0:1]).then_inc(s_var, 1)
                vec.wait_ge(s_var, 1)
                vec.wait_ge(s_root, 1)
                rsqrt(link, dve, rstd[:], root[:], var[:], tmp[:])
                link(dve.tensor_scalar(rstd[:], rstd[:], XSCALE, None, ALU.mult))
                for t in range(T):
                    dve.tensor_scalar(xs[:, t, :], xt[:, t, :], mv[:, t, 0:1], rstd[:, t:t + 1],
                                      ALU.subtract, ALU.mult).then_inc(s_xs, 1)
                unpack_rows(vec, link, turned_ps, s_turned, (vi, ti, f0, f1, f2, found))
                dve.tensor_copy(junk[:, 0:1], found[:]).then_inc(s_found, 1)
                vec.wait_ge(s_sum, 1)
                dve.tensor_copy(total[:], counts_ps[0:1, 8:9]).then_inc(s_sum, 1)
                vec.wait_ge(s_sum, 2)

        def one_pass(tag, clear):
            names = ("onehots_ready", "built", "at_ready", "ax_done", "h_added")
            with ExitStack() as ctx:
                zoh = sb(f"zoh{tag}", [P, 2, BPS, ZP], F16, ctx)
                soh = sb(f"soh{tag}", [P, 2, BPS, P], F16, ctx)
                at = sb(f"at{tag}", [P, 2, T, GN], F16, ctx)
                build_ps = psum(f"build_ps{tag}", [P, 2, 2, 512], F32, ctx)
                h_ps = psum(f"h_ps{tag}", [P, 2, KD, 512], F32, ctx)
                s_oh, s_built, s_at, s_ax, s_h = sems = [nc.alloc_semaphore(f"{n}{tag}") for n in names]
                with nc.Block() as block:

                    @block.vector
                    def _(vec):
                        def onehots(step, u, wait):
                            if wait:
                                vec.wait_ge(s_built, step - 1)
                            cols = z2[:, bass.ds(step * BPS, BPS), :]
                            dve.tensor_tensor(
                                zoh[:, u].rearrange("p b (i two) -> p b i two", two=2),
                                iota16[:, 0:ZP].rearrange("p (i two) -> p i two", two=2).unsqueeze(1)
                                .broadcast_to([P, BPS, ZP // 2, 2]),
                                cols.unsqueeze(2).broadcast_to([P, BPS, ZP // 2, 2]),
                                ALU.is_equal).then_inc(s_oh, 1)
                            srcs = slo2[:, bass.ds(step * BPS, BPS), :]
                            dve.tensor_tensor(
                                soh[:, u].rearrange("p b (i two) -> p b i two", two=2),
                                iota16[:].rearrange("p (i two) -> p i two", two=2).unsqueeze(1)
                                .broadcast_to([P, BPS, P // 2, 2]),
                                srcs.unsqueeze(2).broadcast_to([P, BPS, P // 2, 2]),
                                ALU.is_equal).then_inc(s_oh, 1)

                        def add(g):
                            vec.wait_ge(s_ax, g + 1)
                            for k in range(KD):
                                cols = hT[:, k, g * GN:(g + 1) * GN]
                                dve.scalar_tensor_tensor(out=cols, in0=h_ps[:, g % 2, k, 0:GN], scalar=1.0 / XSCALE,
                                                         in1=cols, op0=ALU.mult, op1=ALU.add).then_inc(s_h, 1)

                        for g in range(GROUPS):
                            onehots(g * STEPS, 0, g > 0)
                            onehots(g * STEPS + 1, 1, g > 0)
                            if g >= 2:
                                add(g - 2)
                            with vec.Fori(1, STEPS // 2) as i:
                                onehots(i * 2 + g * STEPS, 0, True)
                                onehots(i * 2 + g * STEPS + 1, 1, True)
                        add(GROUPS - 2)
                        add(GROUPS - 1)

                    @block.tensor
                    def _(pe):
                        def build(step, u, wait):
                            pe.wait_ge(s_oh, 2 * step + 2)
                            if wait:
                                pe.wait_ge(s_at, 2 * step - 2)
                            for b in range(BPS):
                                last = pe_.matmul(build_ps[:, u, b // QUAD, (b % QUAD) * ZP:(b % QUAD + 1) * ZP],
                                                  soh[:, u, b, :], zoh[:, u, b, :], start=True, stop=True)
                            last.then_inc(s_built, 1)

                        TPP = T // (STEPS // 2)

                        def sums(g, t, start, stop):
                            for k in range(KD):
                                for part in range(2):
                                    last = pe_.matmul(
                                        h_ps[:, g % 2, k, 0:GN],
                                        xhl[:, bass.ds(t, 1), part, k * P:(k + 1) * P].rearrange("p a b -> p (a b)"),
                                        at[:, g % 2, bass.ds(t, 1), :].rearrange("p a b -> p (a b)"),
                                        start=start and part == 0, stop=stop and part == 1, skip_group_check=True)
                            return last

                        def pair(g, i, first, final):
                            for u in range(2):
                                if g < GROUPS:
                                    build(g * STEPS + 2 * i + u, u, not (g == 0 and first))
                                if g >= 1:
                                    if first and u == 0:
                                        pe.wait_ge(s_at, 2 * STEPS * g)
                                        if g >= 3:
                                            pe.wait_ge(s_h, KD * (g - 2))
                                    for j in range(3 * u, 3 + 2 * u):
                                        last = sums(g - 1, i * TPP + j, first and j == 0, final and j == TPP - 1)
                            if g >= 1 and final:
                                last.then_inc(s_ax, 1)

                        for g in range(GROUPS + 1):
                            pair(g, 0, True, False)
                            with pe.Fori(1, STEPS // 2 - 1) as i:
                                pair(g, i, False, False)
                            pair(g, STEPS // 2 - 1, False, True)

                    @block.scalar
                    def _(act):
                        def keep(g, i, u):
                            act.wait_ge(s_built, g * STEPS + 2 * i + u + 1)
                            for q in range(2):
                                to = at[:, g % 2, :, bass.ds((2 * i + u) * BPS * W + q * QUAD * W, QUAD * W)]
                                fr = build_ps[:, u, q, 0:QUAD * ZP].rearrange("p (b z) -> p b z", z=ZP)[:, :, 0:Z]
                                act_.activation(to.rearrange("p t (b r) -> p b t r", r=W),
                                                fr.rearrange("p b (t r) -> p b t r", r=W),
                                                ACT.Copy).then_inc(s_at, 1)

                        for g in range(GROUPS):
                            if g >= 2:
                                act.wait_ge(s_ax, g - 1)
                            with act.Fori(0, STEPS // 2) as i:
                                keep(g, i, 0)
                                keep(g, i, 1)

                for s in sems:
                    if clear:
                        nc.all_engine_barrier(sems_to_clear=s)

        one_pass("", False)

        everything = nc.values_load(total[0:1, 0:1], min_val=0, max_val=E)
        with nc.If(everything != E):
            nc.all_engine_barrier()
            with ExitStack() as ctx:
                selfT = psum("selfT_again", [P, 2, KD, 512], F32, ctx)
                s_selfT = sem("self_turned_again", ctx)
                s_self = sem("self_kept_again", ctx)
                block = ctx.enter_context(nc.Block())

                @block.tensor
                def _(pe):
                    turn_self(pe, selfT, None, s_selfT, s_self)

                @block.scalar
                def _(act):
                    for i in range(len(batches)):
                        keep_self(act, i, selfT, s_selfT, s_self)

                @block.vector
                def _(vec):
                    dve.memset(idx[:], 0)

            s_rows = nc.alloc_semaphore("rows_gathered_g")
            with nc.Fori(0, ceil_div(E, P)) as i:
                with ExitStack() as ctx:
                    turned_ps = psum("turned_ps_g", [P, 1024], F32, ctx)
                    s_turned = nc.alloc_semaphore("rows_turned_g")
                    s_dve = nc.alloc_semaphore("vector_chain_g")
                    with nc.Block() as block:

                        @block.gpsimd
                        def _(pool):
                            gather_rows(pool, rows, s_rows)
                            pool.wait_ge(s_rows, (i + 1) * 16 * BC)

                        @block.tensor
                        def _(pe):
                            turn_rows(pe, rows, turned_ps, s_rows, (i + 1) * 16 * BC, s_turned)

                        @block.vector
                        def _(vec):
                            link = chained(vec, s_dve)
                            unpack_rows(vec, link, turned_ps, s_turned, (vi, ti, f0, f1, f2, found))
                            link(dve.tensor_scalar(idx[:], idx[:], P // STEP, None, ALU.add))

                    for s in (s_turned, s_dve):
                        nc.all_engine_barrier(sems_to_clear=s)
                one_pass("_g", True)

        bstats = sb("bstats", [P, KD, GROUPS, 6], F32)
        with ExitStack() as ctx:
            hid = sb("hid", [P, 2, KH, GN], F32, ctx)
            up_ps = psum("up_ps", [P, KH, 512], F32, ctx)
            down_ps = psum("down_ps", [P, 2, KD, 512], F32, ctx)
            s_up = sem("up_done", ctx)
            s_relu = sem("relu_done", ctx)
            s_down = sem("down_done", ctx)
            s_kept = sem("down_kept", ctx)
            s_stat = sem("bn_stats_done", ctx)
            block = ctx.enter_context(nc.Block())

            @block.tensor
            def _(pe):
                def up(g, wait):
                    for m in range(KH):
                        if wait:
                            pe.wait_ge(s_relu, (g - 1) * KH + m + 1)
                        for k in range(KD):
                            last = pe_.matmul(up_ps[:, m, 0:GN], w1[:, k, m * P:(m + 1) * P],
                                              hT[:, k, bass.ds(g * GN, GN)], start=(k == 0), stop=(k == KD - 1))
                        last.then_inc(s_up, 1)

                def down(g, u, wait):
                    if wait:
                        pe.wait_ge(s_kept, (g - 1) * KD)
                    for f in range(KD):
                        for m in range(KH):
                            if f == 0:
                                pe.wait_ge(s_relu, g * KH + m + 1)
                            last = pe_.matmul(down_ps[:, u, f, 0:GN], w2[:, m, f * P:(f + 1) * P],
                                              hid[:, u, m, :], start=(m == 0), stop=(m == KH - 1))
                        last.then_inc(s_down, 1)

                up(0, False)
                up(1, True)
                down(0, 0, False)
                up(2, True)
                down(1, 1, False)
                with pe.Fori(1, GROUPS // 2 - 1) as i:
                    up(i * 2 + 1, True)
                    down(i * 2, 0, True)
                    up(i * 2 + 2, True)
                    down(i * 2 + 1, 1, True)
                up(GROUPS - 1, True)
                down(GROUPS - 2, 0, True)
                down(GROUPS - 1, 1, True)

            @block.scalar
            def _(act):
                def relu(g, u, wait):
                    if wait:
                        act.wait_ge(s_down, (g - 1) * KD)
                    for m in range(KH):
                        act.wait_ge(s_up, g * KH + m + 1)
                        act_.activation(hid[:, u, m, :], up_ps[:, m, 0:GN], ACT.Relu,
                                        bias=b1[:, m:m + 1]).then_inc(s_relu, 1)

                relu(0, 0, False)
                relu(1, 1, False)
                with act.Fori(1, GROUPS // 2) as i:
                    relu(i * 2, 0, True)
                    relu(i * 2 + 1, 1, True)

            @block.vector
            def _(vec):
                def keep(g, u, n):
                    for f in range(KD):
                        vec.wait_ge(s_down, g * KD + f + 1)
                        dve.tensor_scalar(hT[:, f, bass.ds(g * GN, GN)], down_ps[:, u, f, 0:GN], b2[:, f:f + 1],
                                          None, ALU.add).then_inc(s_kept, 1)
                    for f in range(KD):
                        vec.wait_ge(s_kept, g * KD + f + 1)
                        dve.bn_stats(bstats[:, f, bass.ds(g, 1), :].rearrange("p a b -> p (a b)"),
                                     hT[:, f, bass.ds(g * GN, n)]).then_inc(s_stat, 1)

                with vec.Fori(0, GROUPS // 2 - 1) as i:
                    keep(i * 2, 0, GN)
                    keep(i * 2 + 1, 1, GN)
                keep(GROUPS - 2, 0, GN)
                keep(GROUPS - 1, 1, N - (GROUPS - 1) * GN)

        onehot = sb("onehot", [P, T, NE], F16)
        before = sb("before", [P, T + 1, NE], F16)
        pos = sb("pos", [P, T], I32)
        expert = sb("expert", [1, CHUNKS], I32)
        upper = sb("upper", [P, P], F16)
        upper_in = sb("upper_in", [NE, NE], F16)
        LB = 5
        NB = T // LB
        BN_ = LB * P
        HB = BN_ // 2
        with ExitStack() as ctx:
            mvB = sb("mvB", [P, KD, 2], F32, ctx)
            varB = sb("varB", [P, KD], F32, ctx)
            rootB = sb("rootB", [P, KD], F32, ctx)
            scaleB = sb("scaleB", [P, KD], F32, ctx)
            shiftB = sb("shiftB", [P, KD], F32, ctx)
            tmpB = sb("tmpB", [P, KD], F32, ctx)
            st2 = sb("st2", [P, T, 6], F32, ctx)
            mv2 = sb("mv2", [P, T, 2], F32, ctx)
            var2 = sb("var2", [P, T], F32, ctx)
            root2 = sb("root2", [P, T], F32, ctx)
            rstd2 = sb("rstd2", [P, T], F32, ctx)
            tmp2 = sb("tmp2", [P, T], F32, ctx)
            xT = sb("xT", [P, 2, KD, BN_], F32, ctx)
            lT = sb("lT", [NE, 2, BN_], F32, ctx)
            lmax = sb("lmax", [P, LB], F32, ctx)
            is_max = sb("is_max", [P, LB, NE], F32, ctx)
            first = sb("first", [P, LB], F32, ctx)
            iota32 = sb("iota32", [P, NE], F32, ctx)
            valid = sb("valid", [P, NE], F16, ctx)
            chunk_id = sb("chunk_id", [NE, CHUNKS], F32, ctx)
            ci = sb("ci", [NE, 1], I32, ctx)
            need = sb("need", [NE, 1], F16, ctx)
            needb = sb("needb", [NE, P], F16, ctx)
            ends = sb("ends", [NE, 1], F32, ctx)
            past = sb("past", [NE, CHUNKS], F16, ctx)
            base = sb("base", [P, NE], F32, ctx)
            rank = sb("rank", [P, T, NE], F32, ctx)
            posf = sb("posf", [P, T], F32, ctx)
            y_ps = psum("y_ps", [P, 2, 512], F32, ctx)
            x_ps = psum("x_ps", [P, 2, 512], F32, ctx)
            l_ps = psum("l_ps", [NE, 2, 512], F32, ctx)
            lt_ps = psum("lt_ps", [P, 512], F32, ctx)
            m_ps = psum("m_ps", [P, 512], F32, ctx)

            s_c = sem("router_constants", ctx)
            s_dve = sem("bn_chain", ctx)
            s_varB = sem("bn_var", ctx)
            s_rootB = sem("bn_root", ctx)
            s_scale = sem("bn_scale", ctx)
            s_bn = sem("bn_applied", ctx)
            s_yT = sem("y_turned", ctx)
            s_x1 = sem("x1_ready", ctx)
            s_st2 = sem("stats2", ctx)
            s_mv2 = sem("mv2_ready", ctx)
            s_var2 = sem("var2_ready", ctx)
            s_root2 = sem("root2_ready", ctx)
            s_xn = sem("xn2_ready", ctx)
            s_xT = sem("xn2_turned", ctx)
            s_xTk = sem("xn2_turned_kept", ctx)
            s_l = sem("logits_done", ctx)
            s_lk = sem("logits_kept", ctx)
            s_lT = sem("logits_turned", ctx)
            s_oh = sem("onehot_ready", ctx)
            s_bef = sem("before_ready", ctx)
            s_n = sem("counts_done", ctx)
            s_need = sem("need_ready", ctx)
            s_base = sem("bases_done", ctx)
            s_past = sem("past_ready", ctx)
            s_exp = sem("experts_done", ctx)
            s_rank = sem("ranks_done", ctx)
            s_pos = sem("pos_ready", ctx)
            s_disp = sem("dispatched", ctx)

            block = ctx.enter_context(nc.Block())
            BANK = 512 // NE
            T0 = min(ceil_div(T, 2), BANK)

            @block.gpsimd
            def _(pool):
                pool_.iota(iota32[:], [[1, NE]], base=0, channel_multiplier=0,
                           allow_small_or_imprecise_dtypes=True).then_inc(s_c, 1)
                pool_.iota(chunk_id[:], [[1, CHUNKS]], base=0, channel_multiplier=0,
                           allow_small_or_imprecise_dtypes=True).then_inc(s_c, 1)
                pool_.affine_select(out=valid[:], in_=ones16[:, 0:NE], compare_op=ALU.is_gt, fill=0.0, base=LAST,
                                    pattern=[[0, NE]], channel_multiplier=-1).then_inc(s_c, 1)
                pool_.affine_select(out=upper[:], in_=ones16[:], compare_op=ALU.is_gt, fill=0.0, base=0,
                                    pattern=[[1, P]], channel_multiplier=-1).then_inc(s_c, 1)
                pool_.affine_select(out=upper_in[:], in_=ones16[0:NE, 0:NE], compare_op=ALU.is_ge, fill=0.0,
                                    base=0, pattern=[[1, NE]], channel_multiplier=-1).then_inc(s_c, 1)
                pool_.memset(before[:, 0, :], 0.0).then_inc(s_bef, 1)
                for t in range(T):
                    pool.wait_ge(s_oh, t // LB + 1)
                    pool.wait_ge(s_bef, t + 1)
                    pool_.tensor_tensor(before[:, t + 1, :], before[:, t, :], onehot[:, t, :],
                                        ALU.add).then_inc(s_bef, 1)
                pool.wait_ge(s_pos, 1)
                for t in range(T):
                    n = P if t < T - 1 else LAST
                    pool_.indirect_dma_start(
                        slots_in, bass.IndirectOffsetOnAxis(ap=pos[0:n, t:t + 1], axis=0), xs[0:n, t, :], None
                    ).then_inc(s_disp, 16)
                pool.wait_ge(s_disp, 16 * T)

            @block.tensor
            def _(pe):
                def turn_y(b):
                    pe.wait_ge(s_bn, KD * (b + 1))
                    for t in range(b * LB, (b + 1) * LB):
                        if t >= 2:
                            pe.wait_ge(s_x1, t - 1)
                        for k in range(KD):
                            last = pe_.transpose(y_ps[:, t % 2, k * P:(k + 1) * P], hT[:, k, t * P:(t + 1) * P],
                                                 ident[:])
                        last.then_inc(s_yT, 1)

                def turn_x(b):
                    for t in range(b * LB, (b + 1) * LB):
                        pe.wait_ge(s_xn, t + 1)
                        if t >= 2:
                            pe.wait_ge(s_xTk, t - 1)
                        for k in range(KD):
                            last = pe_.transpose(x_ps[:, t % 2, k * P:(k + 1) * P], xs[:, t, k * P:(k + 1) * P],
                                                 ident[:])
                        last.then_inc(s_xT, 1)

                def logits(b):
                    pe.wait_ge(s_xTk, (b + 1) * LB)
                    if b >= 1:
                        pe.wait_ge(s_lk, b)
                    for i in range(2):
                        for k in range(KD):
                            last = pe_.matmul(l_ps[:, i, 0:HB], rwT[:, k, :], xT[:, b % 2, k, i * HB:(i + 1) * HB],
                                              start=(k == 0), stop=(k == KD - 1))
                    last.then_inc(s_l, 1)

                def turn_logits(b):
                    pe.wait_ge(s_lk, b + 1)
                    if b >= 1:
                        pe.wait_ge(s_oh, b)
                    for j in range(LB):
                        last = pe_.transpose(lt_ps[:, j * NE:(j + 1) * NE], lT[:, b % 2, j * P:(j + 1) * P],
                                             ident[0:NE, 0:NE])
                    last.then_inc(s_lT, 1)

                turn_y(0)
                turn_y(1)
                for b in range(NB):
                    turn_x(b)
                    if b + 2 < NB:
                        turn_y(b + 2)
                    logits(b)
                    turn_logits(b)
                pe.wait_ge(s_bef, T + 1)
                pe.wait_ge(s_c, 5)
                pe_.matmul(m_ps[0:NE, 0:1], before[:, T, :], ones16[:, 0:1], start=True, stop=True).then_inc(s_n, 1)
                pe.wait_ge(s_x1, T)
                for i, (a, b) in enumerate(((0, T0), (T0, T))):
                    r = y_ps[:, i, 0:(b - a) * NE]
                    pe_.matmul(r, upper[:], onehot[:, a:b, :].rearrange("p t e -> p (t e)"), start=True, stop=False)
                    pe_.matmul(r, ones16[:], before[:, a:b, :].rearrange("p t e -> p (t e)"), start=False,
                               stop=True).then_inc(s_rank, 1)
                pe.wait_ge(s_need, 1)
                pe_.matmul(m_ps[:, 64:64 + NE], needb[:], upper[0:NE, 0:NE], start=True, stop=True)\
                   .then_inc(s_base, 1)
                pe_.matmul(m_ps[0:NE, 128:129], upper_in[:], need[:], start=True, stop=True).then_inc(s_base, 1)
                pe.wait_ge(s_past, 1)
                pe_.matmul(m_ps[0:1, 192:192 + CHUNKS], ones16[0:NE, 0:1], past[:], start=True, stop=True)\
                   .then_inc(s_exp, 1)

            @block.scalar
            def _(act):
                act.wait_ge(s_varB, 1)
                act_.activation(rootB[:], varB[:], ACT.Sqrt).then_inc(s_rootB, 1)
                act.wait_ge(s_scale, 1)

                def apply_bn(b):
                    for k in range(KD):
                        cols = hT[:, k, b * BN_:(b + 1) * BN_]
                        act_.activation(cols, cols, ACT.Identity, bias=shiftB[:, k:k + 1],
                                        scale=scaleB[:, k:k + 1]).then_inc(s_bn, 1)

                def root(b):
                    act.wait_ge(s_var2, b + 1)
                    act_.activation(root2[:, b * LB:(b + 1) * LB], var2[:, b * LB:(b + 1) * LB],
                                    ACT.Sqrt).then_inc(s_root2, 1)

                def keep_x(b):
                    for t in range(b * LB, (b + 1) * LB):
                        act.wait_ge(s_xT, t + 1)
                        if b >= 2:
                            act.wait_ge(s_l, b - 1)
                        act_.activation(xT[:, b % 2, :, (t % LB) * P:(t % LB + 1) * P],
                                        x_ps[:, t % 2, 0:KD * P].rearrange("p (k n) -> p k n", k=KD),
                                        ACT.Copy).then_inc(s_xTk, 1)

                def keep_logits(b):
                    act.wait_ge(s_l, b + 1)
                    if b >= 2:
                        act.wait_ge(s_lT, b - 1)
                    act_.activation(lT[:, b % 2, :].rearrange("p (i n) -> p i n", i=2), l_ps[:, :, 0:HB],
                                    ACT.Identity, bias=rbT[:]).then_inc(s_lk, 1)

                for b in range(NB):
                    apply_bn(b)
                root(0)
                for b in range(NB):
                    if b + 1 < NB:
                        root(b + 1)
                    keep_x(b)
                    keep_logits(b)

            @block.vector
            def _(vec):
                link = chained(vec, s_dve)
                for k in range(KD):
                    last = dve.bn_aggr(mvB[:, k, :], bstats[:, k, :, :].rearrange("p g s -> p (g s)"))
                link(last)
                dve.tensor_scalar(varB[:], mvB[:, :, 1], BN_EPS, None, ALU.add).then_inc(s_varB, 1)
                vec.wait_ge(s_rootB, 1)
                rsqrt(link, dve, scaleB[:], rootB[:], varB[:], tmpB[:])
                link(dve.tensor_tensor(scaleB[:], scaleB[:], gam[:], ALU.mult))
                link(dve.tensor_tensor(tmpB[:], mvB[:, :, 0], scaleB[:], ALU.mult))
                dve.tensor_tensor(shiftB[:], bet[:], tmpB[:], ALU.subtract).then_inc(s_scale, 1)

                def residual(b):
                    for t in range(b * LB, (b + 1) * LB):
                        vec.wait_ge(s_yT, t + 1)
                        dve.tensor_tensor(xt[:, t, :], xt[:, t, :], y_ps[:, t % 2, 0:D], ALU.add)\
                           .then_inc(s_x1, 1)
                        if t > b * LB:
                            vec.wait_ge(s_x1, t)
                            dve.bn_stats(st2[:, t - 1, :], xt[:, t - 1, :]).then_inc(s_st2, 1)
                    t = (b + 1) * LB - 1
                    vec.wait_ge(s_x1, t + 1)
                    dve.bn_stats(st2[:, t, :], xt[:, t, :]).then_inc(s_st2, 1)
                    vec.wait_ge(s_st2, (b + 1) * LB)
                    for t in range(b * LB, (b + 1) * LB):
                        dve.bn_aggr(mv2[:, t, :], st2[:, t, :]).then_inc(s_mv2, 1)
                    vec.wait_ge(s_mv2, (b + 1) * LB)
                    ts = slice(b * LB, (b + 1) * LB)
                    dve.tensor_scalar(var2[:, ts], mv2[:, ts, 1], LN_EPS, None, ALU.add).then_inc(s_var2, 1)

                def normalise(b):
                    ts = slice(b * LB, (b + 1) * LB)
                    vec.wait_ge(s_root2, b + 1)
                    rsqrt(link, dve, rstd2[:, ts], root2[:, ts], var2[:, ts], tmp2[:, ts])
                    for t in range(b * LB, (b + 1) * LB):
                        dve.tensor_scalar(xs[:, t, :], xt[:, t, :], mv2[:, t, 0:1], rstd2[:, t:t + 1],
                                          ALU.subtract, ALU.mult).then_inc(s_xn, 1)

                def choose(b):
                    vec.wait_ge(s_lT, b + 1)
                    lg = lt_ps[:, 0:LB * NE].rearrange("p (t e) -> p t e", e=NE)
                    iota = iota32[:].unsqueeze(1).broadcast_to([P, LB, NE])
                    link(dve.tensor_reduce(lmax[:], lg, AX.X, ALU.max))
                    link(dve.tensor_tensor(is_max[:], lg, lmax[:].unsqueeze(2).broadcast_to([P, LB, NE]),
                                           ALU.is_ge))
                    link(dve.scalar_tensor_tensor(out=is_max[:], in0=is_max[:], scalar=-float(NE), in1=iota,
                                                  op0=ALU.mult, op1=ALU.add))
                    link(dve.tensor_reduce(first[:], is_max[:], AX.X, ALU.min))
                    link(dve.tensor_scalar(first[:], first[:], float(NE), None, ALU.add))
                    oh = onehot[:, b * LB:(b + 1) * LB, :]
                    if b < NB - 1:
                        dve.tensor_tensor(oh, iota, first[:].unsqueeze(2).broadcast_to([P, LB, NE]),
                                          ALU.is_equal).then_inc(s_oh, 1)
                    else:
                        link(dve.tensor_tensor(oh, iota, first[:].unsqueeze(2).broadcast_to([P, LB, NE]),
                                               ALU.is_equal))
                        dve.tensor_tensor(onehot[:, T - 1, :], onehot[:, T - 1, :], valid[:],
                                          ALU.mult).then_inc(s_oh, 1)

                vec.wait_ge(s_c, 5)
                residual(0)
                for b in range(NB):
                    if b + 1 < NB:
                        residual(b + 1)
                    normalise(b)
                    if b >= 1:
                        choose(b - 1)
                choose(NB - 1)
                vec.wait_ge(s_n, 1)
                link(dve.tensor_scalar(ci[:], m_ps[0:NE, 0:1], float(P - 1), None, ALU.add))
                link(dve.tensor_scalar(ci[:], ci[:], P.bit_length() - 1, None, ALU.arith_shift_right))
                link(dve.tensor_copy(need[:], ci[:]))
                dve.tensor_copy(needb[:], need[:].broadcast_to([NE, P])).then_inc(s_need, 1)
                vec.wait_ge(s_base, 2)
                link(dve.tensor_copy(ends[:], m_ps[0:NE, 128:129]))
                link(dve.tensor_scalar(base[:], m_ps[:, 64:64 + NE], float(P), None, ALU.mult))
                dve.tensor_scalar(past[:], chunk_id[:], ends[:], None, ALU.is_ge).then_inc(s_past, 1)
                vec.wait_ge(s_rank, 2)
                for i, (a, b) in enumerate(((0, T0), (T0, T))):
                    link(dve.tensor_tensor(rank[:, a:b, :],
                                           y_ps[:, i, 0:(b - a) * NE].rearrange("p (t e) -> p t e", e=NE),
                                           base[:].unsqueeze(1).broadcast_to([P, b - a, NE]), ALU.add))
                link(dve.tensor_tensor(rank[:], rank[:], onehot[:], ALU.mult))
                link(dve.tensor_reduce(posf[:], rank[:], AX.X, ALU.add))
                dve.tensor_copy(pos[:], posf[:]).then_inc(s_pos, 1)
                vec.wait_ge(s_exp, 1)
                dve.tensor_scalar(expert[:], m_ps[0:1, 192:192 + CHUNKS], float(NE - 1), None, ALU.min)

        SLOTS = 4
        assert CHUNKS % SLOTS == 0
        with ExitStack() as ctx:
            ew1s = sb("ew1s", [P, NE, KD, EH], F32, ctx)
            ew2s = sb("ew2s", [EH + 1, NE, D], F32, ctx)
            eb1s = sb("eb1s", [EH, NE], F32, ctx)
            xg = sb("xg", [P, SLOTS, D], F32, ctx)
            w1c = sb("w1c", [P, SLOTS, KD * EH], F32, ctx)
            w2c = sb("w2c", [EH + 1, SLOTS, D], F32, ctx)
            b1c = sb("b1c", [EH, SLOTS], F32, ctx)
            xgT = sb("xgT", [P, 2, KD, P], F32, ctx)
            hg = sb("hg", [EH + 1, 2, P], F32, ctx)
            og = sb("og", [P, SLOTS, D], F32, ctx)
            t_ps = psum("t_ps", [P, 2, 512], F32, ctx)
            u_ps = psum("u_ps", [P, 2, 512], F32, ctx)
            d_ps = psum("d_ps", [P, 2, 512], F32, ctx)
            s_w = sem("expert_weights_in", ctx)
            s_in = [sem(f"slot_in{i}", ctx) for i in range(SLOTS)]
            s_st = [sem(f"slot_out{i}", ctx) for i in range(SLOTS)]
            s_wc = sem("expert_copied", ctx)
            s_t = sem("slots_turned", ctx)
            s_tk = sem("slots_turned_kept", ctx)
            s_u = sem("expert_up", ctx)
            s_uk = sem("expert_relu", ctx)
            s_d = sem("expert_down", ctx)
            s_dk = sem("expert_kept", ctx)
            s_one = sem("ones_row", ctx)
            block = ctx.enter_context(nc.Block())

            def rounds(eng, body):
                for i in range(SLOTS):
                    body(i, i, False)
                with eng.Fori(1, CHUNKS // SLOTS) as r:
                    c = r * SLOTS
                    for i in range(SLOTS):
                        body(c + i, i, True)

            @block.sync
            def _(sp):
                sp.dma_start(ew1s[:], ew1.rearrange("e (p k) h -> p e (k h)", k=KD)
                             .rearrange("p e (k h) -> p e k h", k=KD)).then_inc(s_w, 16)
                sp.dma_start(ew2s[0:EH], ew2.rearrange("e h d -> h e d")).then_inc(s_w, 16)
                sp.dma_start(ew2s[EH:EH + 1], eb2.rearrange("(a e) d -> a e d", a=1)).then_inc(s_w, 16)
                sp.dma_start(eb1s[:], eb1.rearrange("e h -> h e"), allow_slow_non_contiguous=True)\
                  .then_inc(s_w, 16)
                vin = slots_in.rearrange("(c p) d -> c p d", p=P)

                def load(c, i, later):
                    if later:
                        sp.wait_ge(s_t, c - SLOTS + 1)
                    sp.dma_start(xg[:, i, :], slots_in[bass.ds(c * P, P), :]).then_inc(s_in[i], 16)

                rounds(sp, load)

            @block.gpsimd
            def _(pool):
                pool_.memset(hg[EH:EH + 1], 1.0).then_inc(s_one, 1)

                def store(c, i, later):
                    pool.wait_ge(s_dk, c + 1)
                    pool_.dma_start(slots_out[bass.ds(c * P, P), :], og[:, i, :]).then_inc(s_st[i], 16)

                rounds(pool, store)
                for s in s_st:
                    pool.wait_ge(s, 16 * (CHUNKS // SLOTS))

            @block.tensor
            def _(pe):
                def turn(c, i, later):
                    pe.wait_ge(s_in[i], (c - i) * (16 // SLOTS) + 16)
                    if later or i >= 2:
                        pe.wait_ge(s_tk, c - 1)
                    for k in range(KD):
                        last = pe_.transpose(t_ps[:, i % 2, k * P:(k + 1) * P],
                                             xg[:, i, :].rearrange("p (d k) -> p k d", k=KD)[:, k, :], ident[:])
                    last.then_inc(s_t, 1)

                def up(c, i, later):
                    pe.wait_ge(s_tk, c + 1)
                    pe.wait_ge(s_wc, 3 * c + 3)
                    if later or i >= 2:
                        pe.wait_ge(s_uk, c - 1)
                    for k in range(KD):
                        last = pe_.matmul(u_ps[0:EH, i % 2, 0:P], w1c[:, i, k * EH:(k + 1) * EH], xgT[:, i % 2, k, :],
                                          start=(k == 0), stop=(k == KD - 1))
                    last.then_inc(s_u, 1)

                def down(c, i, later):
                    pe.wait_ge(s_uk, c + 1)
                    if later or i >= 2:
                        pe.wait_ge(s_dk, c - 1)
                    pe_.matmul(d_ps[:, i % 2, 0:D], hg[:, i % 2, :], w2c[:, i, :], start=True, stop=True)\
                       .then_inc(s_d, 1)

                pe.wait_ge(s_one, 1)
                turn(0, 0, False)
                turn(1, 1, False)
                up(0, 0, False)
                for i in range(2, SLOTS):
                    turn(i, i, False)
                    up(i - 1, i - 1, False)
                    down(i - 2, i - 2, False)
                with pe.Fori(1, CHUNKS // SLOTS) as r:
                    c = r * SLOTS
                    for i in range(SLOTS):
                        turn(c + i, i, True)
                        up(c + i - 1, (i - 1) % SLOTS, True)
                        down(c + i - 2, (i - 2) % SLOTS, True)
                up(CHUNKS - 1, SLOTS - 1, True)
                down(CHUNKS - 2, SLOTS - 2, True)
                down(CHUNKS - 1, SLOTS - 1, True)

            @block.scalar
            def _(act):
                act.wait_ge(s_one, 1)

                def keep_turned(c, i, later):
                    act.wait_ge(s_t, c + 1)
                    if later or i >= 2:
                        act.wait_ge(s_u, c - 1)
                    act_.activation(xgT[:, i % 2].rearrange("p k n -> p (k n)"), t_ps[:, i % 2, 0:KD * P],
                                    ACT.Copy).then_inc(s_tk, 1)

                def relu(c, i, later):
                    act.wait_ge(s_u, c + 1)
                    if later or i >= 2:
                        act.wait_ge(s_d, c - 1)
                    act_.activation(hg[0:EH, i % 2, :], u_ps[0:EH, i % 2, 0:P], ACT.Relu,
                                    bias=b1c[:, i:i + 1]).then_inc(s_uk, 1)

                keep_turned(0, 0, False)
                for i in range(1, SLOTS):
                    keep_turned(i, i, False)
                    relu(i - 1, i - 1, False)
                with act.Fori(1, CHUNKS // SLOTS) as r:
                    c = r * SLOTS
                    for i in range(SLOTS):
                        keep_turned(c + i, i, True)
                        relu(c + i - 1, (i - 1) % SLOTS, True)
                relu(CHUNKS - 1, SLOTS - 1, True)

            @block.vector
            def _(vec):
                vec.wait_ge(s_w, 64)

                def fetch(c, i, later):
                    e = vec.value_load(expert[0:1, bass.ds(c, 1)], min_val=0, max_val=NE - 1)
                    if later:
                        vec.wait_ge(s_d, c - SLOTS + 1)
                    dve.tensor_copy(w1c[:, i, :], ew1s[:, bass.ds(e, 1)].rearrange("p a k h -> p (a k h)"))\
                       .then_inc(s_wc, 1)
                    dve.tensor_copy(w2c[:, i, :], ew2s[:, bass.ds(e, 1), :].rearrange("p a d -> p (a d)"))\
                       .then_inc(s_wc, 1)
                    dve.tensor_copy(b1c[:, i:i + 1], eb1s[:, bass.ds(e, 1)]).then_inc(s_wc, 1)

                def keep(c, i, later):
                    vec.wait_ge(s_d, c + 1)
                    if later:
                        vec.wait_ge(s_st[i], (c - i) * (16 // SLOTS))
                    dve.tensor_scalar(og[:, i, :], d_ps[:, i % 2, 0:D], 0.0, None, ALU.max).then_inc(s_dk, 1)

                fetch(0, 0, False)
                fetch(1, 1, False)
                for i in range(2, SLOTS):
                    fetch(i, i, False)
                    keep(i - 2, i - 2, False)
                keep(SLOTS - 2, SLOTS - 2, False)
                fetch(SLOTS, 0, True)
                keep(SLOTS - 1, SLOTS - 1, False)
                for i in range(1, SLOTS):
                    fetch(SLOTS + i, i, True)
                    keep(SLOTS + i - 1, i - 1, True)
                with vec.Fori(2, CHUNKS // SLOTS) as r:
                    c = r * SLOTS
                    for i in range(SLOTS):
                        fetch(c + i, i, True)
                        keep(c + i - 1, (i - 1) % SLOTS, True)
                keep(CHUNKS - 1, SLOTS - 1, True)

        R = 4
        with ExitStack() as ctx:
            og2 = sb("og2", [P, T, D], F32, ctx)
            s_g = [sem(f"taken{i}", ctx) for i in range(R)]
            s_add = sem("added", ctx)
            s_o = sem("stored", ctx)
            block = ctx.enter_context(nc.Block())

            @block.gpsimd
            def _(pool):
                for t in range(T):
                    n = P if t < T - 1 else LAST
                    pool_.indirect_dma_start(
                        og2[0:n, t, :], None, slots_out, bass.IndirectOffsetOnAxis(ap=pos[0:n, t:t + 1], axis=0)
                    ).then_inc(s_g[t % R], 16)
                    if t >= R - 1:
                        pool.wait_ge(s_g[(t + 1) % R], 16 * ((t + 1) // R))

            @block.vector
            def _(vec):
                for t in range(T):
                    n = P if t < T - 1 else LAST
                    vec.wait_ge(s_g[t % R], 16 * (t // R + 1))
                    dve.tensor_tensor(xt[0:n, t, :], xt[0:n, t, :], og2[0:n, t, :], ALU.add).then_inc(s_add, 1)

            @block.sync
            def _(sp):
                for t in range(T):
                    n = P if t < T - 1 else LAST
                    sp.wait_ge(s_add, t + 1)
                    sp.dma_start(out[t * P:t * P + n, :], xt[0:n, t, :]).then_inc(s_o, 16)
                sp.wait_ge(s_o, 16 * T)


_INS = ["x", "src", "dst", "L0_gnn_eps", "L0_gnn_W1", "L0_gnn_b1", "L0_gnn_W2", "L0_gnn_b2", "L0_gnn_gamma",
        "L0_gnn_beta", "L0_ffn_router_w", "L0_ffn_router_b", "L0_ffn_W1", "L0_ffn_b1", "L0_ffn_W2", "L0_ffn_b2"]


def kernel(**inputs):
    import numpy as _np
    import concourse.bacc as _bacc
    from concourse import mybir as _mybir
    from concourse.bass_utils import run_bass_kernel_spmd as _run

    nc = _bacc.Bacc("TRN2", target_bir_lowering=False, num_devices=1)
    arrays, args = {}, []
    for name in _INS:
        a = _np.ascontiguousarray(inputs[name])
        arrays[f"in_{name}_dram"] = a
        args.append(nc.dram_tensor(f"in_{name}_dram", a.shape, _mybir.dt.from_np(a.dtype), kind="ExternalInput").ap())
    args.append(nc.dram_tensor("out_dram", arrays["in_x_dram"].shape, _mybir.dt.float32, kind="ExternalOutput").ap())
    gnn_moe_kernel(nc, *args)
    r = _run(nc, [arrays], core_ids=[0])
    return r.results[0]["out_dram"]
```

```python
from contextlib import ExitStack

import concourse.bass as bass
from concourse import mybir

ALU = mybir.AluOpType
ACT = mybir.ActivationFunctionType
AX = mybir.AxisListType
F32 = mybir.dt.float32
F16 = mybir.dt.float16
I32 = mybir.dt.int32

P = 128
LN_EPS = 1e-5
BN_EPS = 1e-5
XSCALE = 2048.0

EPART = 125

W = 5
QUAD = 4
BPS = 2 * QUAD
STEPS = 10
GN = STEPS * BPS * W


def ceil_div(a, b):
    return -(-a // b)


def chained(eng, sem):
    count = [0]

    def link(ins):
        count[0] += 1
        ins.then_inc(sem, 1)
        eng.wait_ge(sem, count[0])

    return link


def rsqrt(link, vec, r, root, var, t):
    link(vec.reciprocal(r, root))
    link(vec.tensor_tensor(t, r, r, ALU.mult))
    link(vec.tensor_tensor(t, t, var, ALU.mult))
    link(vec.tensor_scalar(t, t, -0.5, 1.5, ALU.mult, ALU.add))
    link(vec.tensor_tensor(r, r, t, ALU.mult))


def gnn_moe_kernel(nc, x, src, dst, eps, gw1, gb1, gw2, gb2, gamma, beta, rw, rb, ew1, eb1, ew2, eb2, out):
    N, D = x.shape
    E = src.shape[0]
    H = gw1.shape[1]
    NE, _, EH = ew1.shape
    T = ceil_div(N, P)
    LAST = N - (T - 1) * P
    KD = D // P
    KH = H // P
    EK = E // EPART
    GROUPS = ceil_div(N, GN)
    NP = GROUPS * GN
    BLOCKS = NP // W
    BC = ceil_div(BLOCKS, P)
    Z = T * W
    ZP = Z + 1
    CHUNKS = (N + NE * (P - 1)) // P
    TPP = T // (STEPS // 2)
    XG = 5
    XT = T // XG
    assert NP == T * P and D == 2 * P and EPART * EK == E and T % XG == 0 and QUAD * ZP <= 512

    by_expert = nc.dram_tensor("by_expert", [CHUNKS * P, D], F32, kind="Internal").ap()
    slots_out = nc.dram_tensor("slots_out", [CHUNKS * P, D], F32, kind="Internal").ap()

    top = ExitStack()

    def sb(name, shape, dt, ctx=top):
        return ctx.enter_context(nc.sbuf_tensor(name, shape, dt))

    def psum(name, shape, dt, ctx):
        return ctx.enter_context(nc.psum_tensor(name, shape, dt))

    def sem(name, ctx):
        return ctx.enter_context(nc.semaphore(name))

    with top:
        ident = sb("ident", [P, P], F32)
        ones16 = sb("ones16", [P, P], F16)
        xt = sb("xt", [P, T, D], F32)
        xs = sb("xs", [P, T, D], F32)
        hT = sb("hT", [P, KD, NP], F32)
        total = sb("total", [1, 1], I32)
        w1 = sb("w1", [P, KD, H], F32)
        w2 = sb("w2", [P, KH, D], F32)
        b1 = sb("b1", [P, KH], F32)
        b2 = sb("b2", [P, KD], F32)
        gam = sb("gam", [P, KD], F32)
        bet = sb("bet", [P, KD], F32)
        rwT = sb("rwT", [P, KD, NE], F32)
        rbT = sb("rbT", [NE, 1], F32)
        agg = top.enter_context(ExitStack())
        iota16 = sb("iota16", [P, P], F16, agg)
        xhl = sb("xhl", [P, T, 2, D], F16, agg)
        z2 = sb("z2", [P, BC * P, 2], F16, agg)
        slo2 = sb("slo2", [P, BC * P, 2], F16, agg)
        epsT = sb("epsT", [P, 1], F32, agg)
        selfw = sb("selfw", [P, 1], F32, agg)
        idx = sb("idx", [P, BC], I32, agg)
        thr = sb("thr", [P, BC * P], F32, agg)
        rows = sb("rows", [P, BC, 2, P], I32, agg)
        rowsf = sb("rowsf", [P, BC, 2, P], F32, agg)
        dstT = sb("dstT", [P, BC * P], F32, agg)
        srcT = sb("srcT", [P, BC * P], I32, agg)
        ti = sb("ti", [P, BC * P], I32, agg)
        f1 = sb("f1", [P, BC * P], F32, agg)
        f2 = sb("f2", [P, BC * P], F32, agg)
        found = sb("found", [P, BC], F32, agg)

        dve, act_, pe_, pool_ = nc.vector, nc.scalar, nc.tensor, nc.gpsimd

        def gather_row(pool, c, gathered):
            for i, edges in enumerate((dst, src)):
                pool_.indirect_dma_start(
                    rows[:, c, i, :], None, edges.rearrange("(e a) -> e a", a=1),
                    bass.IndirectOffsetOnAxis(ap=idx[:, c:c + 1], axis=0)
                ).then_inc(gathered, 16)

        def turn_row(c, turned_ps):
            for i in range(2):
                last = pe_.transpose(turned_ps[:, i, c * P:(c + 1) * P], rowsf[:, c, i, :], ident[:])
            return last

        def unpack_rows(link, c0, c1, counted=None):
            n = (c1 - c0) * P
            s = slice(c0 * P, c1 * P)
            link(dve.tensor_scalar(ti[:, s], srcT[:, s], P - 1, None, ALU.bitwise_and))
            link(dve.tensor_copy(slo2[:, s], ti[:, s].unsqueeze(2).broadcast_to([P, n, 2])))
            link(dve.tensor_scalar(ti[:, s], srcT[:, s], P.bit_length() - 1, None, ALU.arith_shift_right))
            link(dve.tensor_tensor(f1[:, s], dstT[:, s], thr[:, s], ALU.subtract))
            link(dve.tensor_scalar(f2[:, s], f1[:, s], 0.0, None, ALU.is_ge))
            link(dve.scalar_tensor_tensor(out=f2[:, s], in0=f1[:, s], scalar=float(W), in1=f2[:, s],
                                          op0=ALU.is_lt, op1=ALU.mult))
            if counted is not None:
                link(dve.tensor_scalar(f2[:, s], f2[:, s], counted, None, ALU.mult))
            link(dve.tensor_reduce(found[:, c0:c1], f2[:, s].rearrange("p (c b) -> p c b", b=P), AX.X, ALU.add))
            link(dve.scalar_tensor_tensor(out=f1[:, s], in0=ti[:, s], scalar=float(W), in1=f1[:, s],
                                          op0=ALU.mult, op1=ALU.add))
            link(dve.scalar_tensor_tensor(out=f1[:, s], in0=f1[:, s], scalar=1.0, in1=f2[:, s],
                                          op0=ALU.add, op1=ALU.mult))
            link(dve.tensor_scalar(z2[:, s], f1[:, s].unsqueeze(2).broadcast_to([P, n, 2]), -1.0, None, ALU.add))

        BATCH = 4
        batches = [(t, min(BATCH, T - t)) for t in range(0, T, BATCH)]

        def turn_self(pe, i, selfT, self_turned, self_kept, xs_ready=None):
            t0, n = batches[i]
            if xs_ready is not None:
                pe.wait_ge(xs_ready, t0 + n)
            if i >= 1:
                pe.wait_ge(self_kept, KD * i)
            for k in range(KD):
                for j in range(n):
                    last = pe_.transpose(selfT[:, k, j * P:(j + 1) * P], xs[:, t0 + j, k * P:(k + 1) * P], ident[:])
            last.then_inc(self_turned, 1)

        def keep_self(act, i, selfT, self_turned, self_kept):
            t0, n = batches[i]
            act.wait_ge(self_turned, i + 1)
            for k in range(KD):
                act_.activation(hT[:, k, t0 * P:(t0 + n) * P], selfT[:, k, 0:n * P], ACT.Copy,
                                scale=selfw[:]).then_inc(self_kept, 1)

        class Pass:

            def __init__(self, tag, ctx):
                self.zoh = sb(f"zoh{tag}", [P, 2, BPS, ZP], F16, ctx)
                self.soh = sb(f"soh{tag}", [P, 2, BPS, P], F16, ctx)
                self.at = sb(f"at{tag}", [P, 2, T, GN], F16, ctx)
                self.build_ps = psum(f"build_ps{tag}", [P, 2, 2, 512], F32, ctx)
                self.h_ps = psum(f"h_ps{tag}", [P, 2, KD, 512], F32, ctx)
                names = ("onehots_ready", "built", "at_ready", "ax_done", "h_added")
                self.sems = [nc.alloc_semaphore(f"{n}{tag}") for n in names]
                self.s_oh, self.s_built, self.s_at, self.s_ax, self.s_h = self.sems

            def onehots(self, vec, step, u, wait):
                if wait:
                    vec.wait_ge(self.s_built, step - 1)
                for to, n, vals in ((self.zoh, ZP, z2), (self.soh, P, slo2)):
                    dve.tensor_tensor(
                        to[:, u].rearrange("p b (i two) -> p b i two", two=2),
                        iota16[:, 0:n].rearrange("p (i two) -> p i two", two=2).unsqueeze(1)
                        .broadcast_to([P, BPS, n // 2, 2]),
                        vals[:, bass.ds(step * BPS, BPS), :].unsqueeze(2).broadcast_to([P, BPS, n // 2, 2]),
                        ALU.is_equal).then_inc(self.s_oh, 1)

            def add(self, vec, g):
                vec.wait_ge(self.s_ax, g + 1)
                for k in range(KD):
                    cols = hT[:, k, g * GN:(g + 1) * GN]
                    dve.scalar_tensor_tensor(out=cols, in0=self.h_ps[:, g % 2, k, 0:GN], scalar=1.0 / XSCALE,
                                             in1=cols, op0=ALU.mult, op1=ALU.add).then_inc(self.s_h, 1)

            def vector_group(self, vec, g, self_kept=None):
                self.onehots(vec, g * STEPS, 0, g > 0)
                self.onehots(vec, g * STEPS + 1, 1, g > 0)
                if g == 2 and self_kept is not None:
                    vec.wait_ge(self_kept, KD * len(batches))
                if g >= 2:
                    self.add(vec, g - 2)
                with vec.Fori(1, STEPS // 2) as i:
                    self.onehots(vec, i * 2 + g * STEPS, 0, True)
                    self.onehots(vec, i * 2 + g * STEPS + 1, 1, True)

            def build(self, pe, step, u, wait):
                pe.wait_ge(self.s_oh, 2 * step + 2)
                if wait:
                    pe.wait_ge(self.s_at, 2 * step - 2)
                for b in range(BPS):
                    last = pe_.matmul(self.build_ps[:, u, b // QUAD, (b % QUAD) * ZP:(b % QUAD + 1) * ZP],
                                      self.soh[:, u, b, :], self.zoh[:, u, b, :], start=True, stop=True)
                last.then_inc(self.s_built, 1)

            def sums(self, g, t, start, stop):
                for k in range(KD):
                    for part in range(2):
                        last = pe_.matmul(
                            self.h_ps[:, g % 2, k, 0:GN],
                            xhl[:, bass.ds(t, 1), part, k * P:(k + 1) * P].rearrange("p a b -> p (a b)"),
                            self.at[:, g % 2, bass.ds(t, 1), :].rearrange("p a b -> p (a b)"),
                            start=start and part == 0, stop=stop and part == 1, skip_group_check=True)
                return last

            def pair(self, pe, g, i, first, final, split_ready=None, between=None):
                for u in range(2):
                    if g < GROUPS:
                        self.build(pe, g * STEPS + 2 * i + u, u, not (g == 0 and first))
                    if g >= 1:
                        if u == 0:
                            if first:
                                pe.wait_ge(self.s_at, 2 * STEPS * g)
                            if first and g >= 3:
                                pe.wait_ge(self.s_h, KD * (g - 2))
                            if g == 1 and split_ready is not None:
                                pe.wait_ge(split_ready, i + 1)
                        for j in range(3 * u, 3 + 2 * u):
                            last = self.sums(g - 1, i * TPP + j, first and j == 0, final and j == TPP - 1)
                    if between is not None:
                        between(2 * i + u)
                if g >= 1 and final:
                    last.then_inc(self.s_ax, 1)

            def tensor_group(self, pe, g, split_ready=None):
                self.pair(pe, g, 0, True, False, split_ready)
                with pe.Fori(1, STEPS // 2 - 1) as i:
                    self.pair(pe, g, i, False, False, split_ready)
                self.pair(pe, g, STEPS // 2 - 1, False, True, split_ready)

            def keep(self, act, g, i, u):
                act.wait_ge(self.s_built, g * STEPS + 2 * i + u + 1)
                for q in range(2):
                    to = self.at[:, g % 2, :, bass.ds((2 * i + u) * BPS * W + q * QUAD * W, QUAD * W)]
                    fr = self.build_ps[:, u, q, 0:QUAD * ZP].rearrange("p (b z) -> p b z", z=ZP)[:, :, 0:Z]
                    act_.activation(to.rearrange("p t (b r) -> p b t r", r=W),
                                    fr.rearrange("p b (t r) -> p b t r", r=W), ACT.Copy).then_inc(self.s_at, 1)

            def scalar_group(self, act, g):
                if g >= 2:
                    act.wait_ge(self.s_ax, g - 1)
                with act.Fori(0, STEPS // 2) as i:
                    self.keep(act, g, i, 0)
                    self.keep(act, g, i, 1)

        with ExitStack() as ctx:
            headi = sb("headi", [EPART, 1], I32, ctx)
            head = sb("head", [EPART, 1], F32, ctx)
            heads_below = sb("heads_below", [EPART, BC * P], F16, ctx)
            thrc = sb("thrc", [P, BC], F32, ctx)
            line = sb("line", [P, BC], F32, ctx)
            linei = sb("linei", [P, BC], I32, ctx)
            lines = sb("lines", [P, BC, EK], I32, ctx)
            junk = sb("junk", [P, BC, EK], F32, ctx)
            below = sb("below", [P, BC], F32, ctx)
            start = sb("start", [P, BC], F32, ctx)
            ones32 = sb("ones32", [P, 1], F32, ctx)
            foundp = sb("foundp", [P, 1], F32, ctx)
            stats = sb("stats", [P, T, 6], F32, ctx)
            mv = sb("mv", [P, T, 2], F32, ctx)
            var = sb("var", [P, T], F32, ctx)
            root = sb("root", [P, T], F32, ctx)
            rstd = sb("rstd", [P, T], F32, ctx)
            tmp = sb("tmp", [P, T], F32, ctx)
            one = Pass("", ctx)
            counts_ps = one.h_ps[:, 0, 1, 256:512]
            turned_ps = one.h_ps[:].rearrange("p i k n -> p i (k n)")
            selfT = one.h_ps[:, 1]

            s_heads = sem("heads_in", ctx)
            s_x = [sem(f"x_in{g}", ctx) for g in range(XG)]
            s_eps = sem("eps_in", ctx)
            s_w = sem("weights_in", ctx)
            s_tail = sem("tail_zeroed", ctx)
            s_const = sem("constants_made", ctx)
            s_hb = sem("heads_compared", ctx)
            s_hc = sem("heads_counted", ctx)
            s_line = sem("lines_known", ctx)
            s_lines = [sem(f"lines_gathered{c}", ctx) for c in range(BC)]
            s_late = sem("later_constants_made", ctx)
            s_cnt = sem("below_counted", ctx)
            s_idx = sem("rows_known", ctx)
            s_rows = [sem(f"rows_gathered{c}", ctx) for c in range(BC)]
            s_rowsf = sem("rows_as_float", ctx)
            s_turned = sem("rows_turned", ctx)
            s_turnedk = sem("turned_rows_kept", ctx)
            s_found = sem("found_per_partition", ctx)
            s_sum = sem("found_summed", ctx)
            s_totalled = sem("total_kept", ctx)
            s_stats = sem("stats_done", ctx)
            s_dve = sem("vector_chain", ctx)
            s_var = sem("var_ready", ctx)
            s_root = sem("root_ready", ctx)
            s_xs = sem("xs_ready", ctx)
            s_hi = sem("hi_ready", ctx)
            s_lo = sem("lo_ready", ctx)
            s_selfw = sem("self_weight_ready", ctx)
            s_selfT = sem("self_turned", ctx)
            s_self = sem("self_kept", ctx)
            s_pool = sem("pool_chain", ctx)

            block = ctx.enter_context(nc.Block())

            EARLY = 2

            def self_of(step):
                i = step - (STEPS - len(batches))
                return i if i >= 0 else None

            @block.sync
            def _(sp):
                sp.dma_start(headi[:], dst.rearrange("(p k) -> p k", k=EK)[:, 0:1], allow_slow_non_contiguous=True)\
                  .then_inc(s_heads, 16)
                xv = x[0:(T - 1) * P, :].rearrange("(t p) d -> p t d", p=P)
                for g in range(XG):
                    a, b = g * XT, min((g + 1) * XT, T - 1)
                    if g >= 2:
                        sp.wait_ge(s_lines[(g - 2) * 2], 16)
                    sp.dma_start(xt[:, a:b, :], xv[:, a:b, :]).then_inc(s_x[g], 16)
                sp.wait_ge(s_tail, 1)
                sp.dma_start(xt[0:LAST, T - 1, :], x[(T - 1) * P:N, :]).then_inc(s_x[XG - 1], 16)
                sp.dma_start(epsT[:], eps.rearrange("(a b) -> a b", a=1).broadcast_to([P, 1])).then_inc(s_eps, 16)
                for sbuf, dram in (
                    (w1[:], gw1.rearrange("(k p) h -> p k h", p=P)),
                    (w2[:], gw2.rearrange("(k p) h -> p k h", p=P)),
                    (b1[:], gb1.rearrange("(k p) -> p k", p=P)),
                    (b2[:], gb2.rearrange("(k p) -> p k", p=P)),
                    (gam[:], gamma.rearrange("(k p) -> p k", p=P)),
                    (bet[:], beta.rearrange("(k p) -> p k", p=P)),
                    (rbT[:], rb.rearrange("(e a) -> e a", a=1)),
                    (rwT[:, 0, :], rw[:, 0:P].rearrange("e p -> p e")),
                    (rwT[:, 1, :], rw[:, P:D].rearrange("e p -> p e")),
                ):
                    sp.dma_start(sbuf, dram, allow_slow_non_contiguous=True).then_inc(s_w, 16)
                sp.wait_ge(s_w, 16 * 9)

            @block.gpsimd
            def _(pool):
                link = chained(pool, s_pool)
                pool_.iota(thr[:], [[W, BC * P]], base=0, channel_multiplier=0,
                           allow_small_or_imprecise_dtypes=True).then_inc(s_const, 1)
                pool_.memset(ones16[:], 1.0).then_inc(s_const, 1)
                pool_.memset(xt[:, T - 1, :], 0.0).then_inc(s_tail, 1)
                pool_.iota(thrc[:], [[W * P, BC]], base=0, channel_multiplier=W,
                           allow_small_or_imprecise_dtypes=True).then_inc(s_const, 1)
                pool.wait_ge(s_line, 1)
                dl = dst.rearrange("(p k) -> p k", k=EK)
                for c in range(BC):
                    pool_.indirect_dma_start(
                        lines[:, c, :], None, dl, bass.IndirectOffsetOnAxis(ap=linei[:, c:c + 1], axis=0)
                    ).then_inc(s_lines[c], 16)
                pool_.iota(iota16[:], [[1, P]], base=0, channel_multiplier=0,
                           allow_small_or_imprecise_dtypes=True).then_inc(s_late, 1)
                link(pool_.memset(ident[:], 0.0))
                pool_.affine_select(out=ident[:], in_=ident[:], compare_op=ALU.not_equal, fill=1.0, base=0,
                                    pattern=[[-1, P]], channel_multiplier=1).then_inc(s_late, 1)
                pool_.memset(ones32[:], 1.0).then_inc(s_late, 1)
                for c in range(BC):
                    pool.wait_ge(s_idx, c + 1)
                    gather_row(pool, c, s_rows[c])
                for i in range(XG):
                    pool.wait_ge(s_hi, i + 1)
                    t, n = i * XT, XT
                    pool_.tensor_tensor(xhl[:, t:t + n, 1, :], xs[:, t:t + n, :], xhl[:, t:t + n, 0, :],
                                        ALU.subtract).then_inc(s_lo, 1)

            @block.tensor
            def _(pe):
                pe.wait_ge(s_hb, 1)
                pe.wait_ge(s_const, 3)
                for c in range(BC):
                    last = pe_.matmul(counts_ps[:, c:c + 1], heads_below[:, c * P:(c + 1) * P],
                                      ones16[0:EPART, 0:1], start=True, stop=True)
                last.then_inc(s_hc, 1)
                pe.wait_ge(s_late, 3)
                for c in range(BC):
                    pe.wait_ge(s_rowsf, c + 1)
                    turn_row(c, turned_ps).then_inc(s_turned, 1)
                one.tensor_group(pe, 0)
                pe.wait_ge(s_turnedk, 2 * BC)

                def between(step):
                    if self_of(step) is not None:
                        turn_self(pe, self_of(step), selfT, s_selfT, s_self, s_xs)

                for i in range(STEPS // 2):
                    one.pair(pe, 1, i, i == 0, i == STEPS // 2 - 1, s_lo, between)
                pe.wait_ge(s_self, KD * len(batches))
                for g in range(2, GROUPS):
                    one.tensor_group(pe, g)
                pe.wait_ge(s_found, 1)
                pe.wait_ge(one.s_at, 2 * STEPS * GROUPS)
                pe_.matmul(one.build_ps[0:1, 0, 0, 0:1], foundp[:], ones32[:], start=True, stop=True)\
                   .then_inc(s_sum, 1)
                one.tensor_group(pe, GROUPS)

            @block.scalar
            def _(act):
                def keep_row(c):
                    act.wait_ge(s_rows[c], 32)
                    act_.activation(rowsf[:, c], rows[:, c], ACT.Copy).then_inc(s_rowsf, 1)
                    act.wait_ge(s_turned, c + 1)
                    s = slice(c * P, (c + 1) * P)
                    act_.activation(dstT[:, s], turned_ps[:, 0, s], ACT.Copy).then_inc(s_turnedk, 1)
                    act_.activation(srcT[:, s], turned_ps[:, 1, s], ACT.Copy).then_inc(s_turnedk, 1)

                def split(g):
                    act.wait_ge(s_xs, (g + 1) * XT)
                    act_.activation(xhl[:, g * XT:(g + 1) * XT, 0, :], xs[:, g * XT:(g + 1) * XT, :],
                                    ACT.Copy).then_inc(s_hi, 1)

                keep_row(0)
                act.wait_ge(s_var, 1)
                act_.activation(root[:], var[:], ACT.Sqrt).then_inc(s_root, 1)
                keep_row(1)
                for g in range(EARLY):
                    split(g)
                for c in range(2, BC):
                    keep_row(c)
                one.scalar_group(act, 0)
                act.wait_ge(s_selfw, 1)
                for step in range(STEPS):
                    one.keep(act, 1, step // 2, step % 2)
                    if step % 2 == 1 and step // 2 + EARLY < XG:
                        split(step // 2 + EARLY)
                    if self_of(step) is not None:
                        keep_self(act, self_of(step), selfT, s_selfT, s_self)
                for g in range(2, GROUPS):
                    one.scalar_group(act, g)

            @block.vector
            def _(vec):
                link = chained(vec, s_dve)

                def group_stats(g):
                    vec.wait_ge(s_x[g], 16 if g < XG - 1 else 32)
                    for t in range(g * XT, (g + 1) * XT):
                        dve.bn_stats(stats[:, t, :], xt[:, t, :]).then_inc(s_stats, 1)

                vec.wait_ge(s_heads, 16)
                link(dve.tensor_copy(head[:], headi[:]))
                vec.wait_ge(s_const, 3)
                dve.tensor_scalar(heads_below[:], thr[0:EPART, :], head[:], None, ALU.is_gt).then_inc(s_hb, 1)
                vec.wait_ge(s_hc, 1)
                link(dve.tensor_scalar(line[:], counts_ps[:, 0:BC], -1.0, 0.0, ALU.add, ALU.max))
                dve.tensor_copy(linei[:], line[:]).then_inc(s_line, 1)
                group_stats(0)
                for c in range(BC):
                    vec.wait_ge(s_lines[c], 16)
                    dve.tensor_scalar(junk[:, c, :], lines[:, c, :], thrc[:, c:c + 1], 0.0, ALU.is_lt, ALU.add,
                                      accum_out=below[:, c:c + 1]).then_inc(s_cnt, 1)
                    vec.wait_ge(s_cnt, c + 1)
                    link(dve.scalar_tensor_tensor(out=start[:, c:c + 1], in0=line[:, c:c + 1], scalar=float(EK),
                                                  in1=below[:, c:c + 1], op0=ALU.mult, op1=ALU.add))
                    dve.tensor_scalar(idx[:, c:c + 1], start[:, c:c + 1], float(E - P), None, ALU.min)\
                       .then_inc(s_idx, 1)
                for g in range(1, XG):
                    group_stats(g)
                vec.wait_ge(s_stats, T)
                for t in range(T):
                    last = dve.bn_aggr(mv[:, t, :], stats[:, t, :])
                link(last)
                dve.tensor_scalar(var[:], mv[:, :, 1], LN_EPS, None, ALU.add).then_inc(s_var, 1)
                vec.wait_ge(s_eps, 16)
                dve.tensor_scalar(selfw[:], epsT[:], 1.0, 1.0 / XSCALE, ALU.add, ALU.mult).then_inc(s_selfw, 1)
                vec.wait_ge(s_root, 1)
                rsqrt(link, dve, rstd[:], root[:], var[:], tmp[:])
                link(dve.tensor_scalar(rstd[:], rstd[:], XSCALE, None, ALU.mult))

                def layernorm(a, b):
                    for t in range(a, b):
                        dve.tensor_scalar(xs[:, t, :], xt[:, t, :], mv[:, t, 0:1], rstd[:, t:t + 1],
                                          ALU.subtract, ALU.mult).then_inc(s_xs, 1)

                layernorm(0, EARLY * XT)
                vec.wait_ge(s_turnedk, 2)
                unpack_rows(link, 0, 1)
                vec.wait_ge(s_late, 3)
                one.vector_group(vec, 0)
                done = EARLY
                unpacked = 1
                for i in range(STEPS // 2):
                    for u in range(2):
                        step = STEPS + 2 * i + u
                        if (step + 1) * BPS > unpacked * P:
                            unpacked += 1
                            vec.wait_ge(s_turnedk, 2 * unpacked)
                            unpack_rows(link, unpacked - 1, unpacked)
                        one.onehots(vec, step, u, True)
                    if done < XG:
                        layernorm(done * XT, (done + 1) * XT)
                        done += 1
                vec.wait_ge(s_turnedk, 2 * BC)
                unpack_rows(link, unpacked, BC)
                dve.tensor_reduce(foundp[:], found[:], AX.X, ALU.add).then_inc(s_found, 1)
                for g in range(2, GROUPS):
                    one.vector_group(vec, g, s_self)
                vec.wait_ge(s_sum, 1)
                dve.tensor_copy(total[:], one.build_ps[0:1, 0, 0, 0:1]).then_inc(s_totalled, 1)
                one.add(vec, GROUPS - 2)
                one.add(vec, GROUPS - 1)

        wanted = sb("wanted", [P, 1], F32, agg)
        skipped = sb("skipped", [P, 1], F32, agg)
        counted = sb("counted", [P, 1], F32, agg)
        edge_id = sb("edge_id", [P, 1], F32, agg)
        everything = nc.values_load(total[0:1, 0:1], min_val=0, max_val=E)
        with nc.If(everything != E):
            nc.all_engine_barrier()
            with ExitStack() as ctx:
                selfT = psum("selfT_again", [P, KD, 512], F32, ctx)
                s_selfT = sem("self_turned_again", ctx)
                s_self = sem("self_kept_again", ctx)
                block = ctx.enter_context(nc.Block())

                @block.tensor
                def _(pe):
                    for i in range(len(batches)):
                        turn_self(pe, i, selfT, s_selfT, s_self)

                @block.scalar
                def _(act):
                    for i in range(len(batches)):
                        keep_self(act, i, selfT, s_selfT, s_self)

                @block.vector
                def _(vec):
                    dve.memset(wanted[:], 0.0)
                    dve.memset(idx[:], 0)
                    dve.memset(counted[:], 1.0)

                @block.gpsimd
                def _(pool):
                    pool_.iota(edge_id[:], [[0, 1]], base=0, channel_multiplier=1,
                               allow_small_or_imprecise_dtypes=True)

            s_rows = nc.alloc_semaphore("rows_gathered_g")
            with nc.Fori(0, ceil_div(E, P)) as i:
                with ExitStack() as ctx:
                    turned_ps = psum("turned_ps_g", [P, 2, 1024], F32, ctx)
                    s_rowsf = nc.alloc_semaphore("rows_as_float_g")
                    s_turned = nc.alloc_semaphore("rows_turned_g")
                    s_dve = nc.alloc_semaphore("vector_chain_g")
                    with nc.Block() as block:

                        @block.gpsimd
                        def _(pool):
                            for c in range(BC):
                                gather_row(pool, c, s_rows)
                            pool.wait_ge(s_rows, (i + 1) * 32 * BC)

                        @block.tensor
                        def _(pe):
                            pe.wait_ge(s_rowsf, 1)
                            for c in range(BC):
                                last = turn_row(c, turned_ps)
                            last.then_inc(s_turned, 1)

                        @block.vector
                        def _(vec):
                            link = chained(vec, s_dve)
                            vec.wait_ge(s_rows, (i + 1) * 32 * BC)
                            dve.tensor_copy(rowsf[:], rows[:]).then_inc(s_rowsf, 1)
                            vec.wait_ge(s_turned, 1)
                            link(dve.tensor_copy(dstT[:], turned_ps[:, 0, 0:BC * P]))
                            link(dve.tensor_copy(srcT[:], turned_ps[:, 1, 0:BC * P]))
                            unpack_rows(link, 0, BC, counted[:])
                            link(dve.tensor_scalar(wanted[:], wanted[:], float(P), None, ALU.add))
                            link(dve.tensor_scalar(idx[:], wanted[:].broadcast_to([P, BC]), float(E - P), None,
                                                   ALU.min))
                            link(dve.tensor_scalar(skipped[:], wanted[:], float(E - P), 0.0, ALU.subtract, ALU.max))
                            link(dve.tensor_tensor(counted[:], edge_id[:], skipped[:], ALU.is_ge))

                    for s in (s_rowsf, s_turned, s_dve):
                        nc.all_engine_barrier(sems_to_clear=s)
                with ExitStack() as ctx:
                    again = Pass("_g", ctx)
                    with nc.Block() as block:

                        @block.vector
                        def _(vec):
                            for g in range(GROUPS):
                                again.vector_group(vec, g)
                            again.add(vec, GROUPS - 2)
                            again.add(vec, GROUPS - 1)

                        @block.tensor
                        def _(pe):
                            for g in range(GROUPS + 1):
                                again.tensor_group(pe, g)

                        @block.scalar
                        def _(act):
                            for g in range(GROUPS):
                                again.scalar_group(act, g)

                    for s in again.sems:
                        nc.all_engine_barrier(sems_to_clear=s)
        agg.close()

        bstats = sb("bstats", [P, KD, GROUPS, 6], F32)
        EWC = KD * EH + D + 2
        ew = sb("ew", [P, NE, EWC], F32)
        C1, C2 = KD * EH, KD * EH + D
        with ExitStack() as ctx:
            hid = sb("hid", [P, 2, KH, GN], F32, ctx)
            up_ps = psum("up_ps", [P, KH, 512], F32, ctx)
            down_ps = psum("down_ps", [P, 2, KD, 512], F32, ctx)
            s_up = sem("up_done", ctx)
            s_relu = sem("relu_done", ctx)
            s_down = sem("down_done", ctx)
            s_kept = sem("down_kept", ctx)
            s_stat = sem("bn_stats_done", ctx)
            s_ew0 = sem("expert_padding_zeroed", ctx)
            s_ew = sem("expert_weights_in", ctx)
            zeros = sb("zeros", [P, D], F32, ctx)
            s_zeros = sem("zeros_made", ctx)
            s_zeroed = sem("pages_zeroed", ctx)
            block = ctx.enter_context(nc.Block())

            @block.gpsimd
            def _(pool):
                pool_.memset(zeros[:], 0.0).then_inc(s_zeros, 1)
                pool.wait_ge(s_zeros, 1)
                pool_.memset(ew[EH:P, :, C1:EWC], 0.0).then_inc(s_ew0, 1)
                pool.wait_ge(s_ew0, 1)
                pool_.memset(ew[0:EH, :, C2:EWC], 0.0).then_inc(s_ew0, 1)

            @block.sync
            def _(sp):
                sp.dma_start(ew[:, :, 0:C1], ew1.rearrange("e (p k) h -> p e (k h)", k=KD)).then_inc(s_ew, 16)
                sp.dma_start(ew[0:EH, :, C1:C2], ew2.rearrange("e h d -> h e d")).then_inc(s_ew, 16)
                sp.wait_ge(s_ew0, 2)
                sp.dma_start(ew[EH:EH + 1, :, C1:C2], eb2.rearrange("(a e) d -> a e d", a=1)).then_inc(s_ew, 16)
                sp.dma_start(ew[0:EH, :, C2], eb1.rearrange("e h -> h e"), allow_slow_non_contiguous=True)\
                  .then_inc(s_ew, 16)
                sp.wait_ge(s_zeros, 1)
                sp.dma_start(by_expert.rearrange("(c p) d -> p c d", p=P),
                             zeros[:].unsqueeze(1).broadcast_to([P, CHUNKS, D])).then_inc(s_zeroed, 16)
                sp.wait_ge(s_ew, 64)
                sp.wait_ge(s_zeroed, 16)

            @block.tensor
            def _(pe):
                def up(g, wait):
                    for m in range(KH):
                        if wait:
                            pe.wait_ge(s_relu, (g - 1) * KH + m + 1)
                        for k in range(KD):
                            last = pe_.matmul(up_ps[:, m, 0:GN], w1[:, k, m * P:(m + 1) * P],
                                              hT[:, k, bass.ds(g * GN, GN)], start=(k == 0), stop=(k == KD - 1))
                        last.then_inc(s_up, 1)

                def down(g, u, wait):
                    if wait:
                        pe.wait_ge(s_kept, (g - 1) * KD)
                    for f in range(KD):
                        for m in range(KH):
                            if f == 0:
                                pe.wait_ge(s_relu, g * KH + m + 1)
                            last = pe_.matmul(down_ps[:, u, f, 0:GN], w2[:, m, f * P:(f + 1) * P],
                                              hid[:, u, m, :], start=(m == 0), stop=(m == KH - 1))
                        last.then_inc(s_down, 1)

                up(0, False)
                up(1, True)
                down(0, 0, False)
                up(2, True)
                down(1, 1, False)
                with pe.Fori(1, GROUPS // 2 - 1) as i:
                    up(i * 2 + 1, True)
                    down(i * 2, 0, True)
                    up(i * 2 + 2, True)
                    down(i * 2 + 1, 1, True)
                up(GROUPS - 1, True)
                down(GROUPS - 2, 0, True)
                down(GROUPS - 1, 1, True)

            @block.scalar
            def _(act):
                def relu(g, u, wait):
                    if wait:
                        act.wait_ge(s_down, (g - 1) * KD)
                    for m in range(KH):
                        act.wait_ge(s_up, g * KH + m + 1)
                        act_.activation(hid[:, u, m, :], up_ps[:, m, 0:GN], ACT.Relu,
                                        bias=b1[:, m:m + 1]).then_inc(s_relu, 1)

                relu(0, 0, False)
                relu(1, 1, False)
                with act.Fori(1, GROUPS // 2) as i:
                    relu(i * 2, 0, True)
                    relu(i * 2 + 1, 1, True)

            @block.vector
            def _(vec):
                def keep(g, u, n):
                    for f in range(KD):
                        vec.wait_ge(s_down, g * KD + f + 1)
                        dve.tensor_scalar(hT[:, f, bass.ds(g * GN, GN)], down_ps[:, u, f, 0:GN], b2[:, f:f + 1],
                                          None, ALU.add).then_inc(s_kept, 1)
                    for f in range(KD):
                        vec.wait_ge(s_kept, g * KD + f + 1)
                        dve.bn_stats(bstats[:, f, bass.ds(g, 1), :].rearrange("p a b -> p (a b)"),
                                     hT[:, f, bass.ds(g * GN, n)]).then_inc(s_stat, 1)

                with vec.Fori(0, GROUPS // 2 - 1) as i:
                    keep(i * 2, 0, GN)
                    keep(i * 2 + 1, 1, GN)
                keep(GROUPS - 2, 0, GN)
                keep(GROUPS - 1, 1, N - (GROUPS - 1) * GN)

        onehot = sb("onehot", [P, T, NE], F16)
        row = sb("row", [P, T], I32)
        expert = sb("expert", [1, CHUNKS], I32)
        LB = 5
        NB = T // LB
        BN_ = LB * P
        HB = BN_ // 2
        UNITS = ceil_div(LB, 2)

        def unit_tiles(u):
            b, j = divmod(u, UNITS)
            return b * LB + 2 * j, min(2, LB - 2 * j)

        with ExitStack() as ctx:
            mvB = sb("mvB", [P, KD, 2], F32, ctx)
            varB = sb("varB", [P, KD], F32, ctx)
            rootB = sb("rootB", [P, KD], F32, ctx)
            scaleB = sb("scaleB", [P, KD], F32, ctx)
            shiftB = sb("shiftB", [P, KD], F32, ctx)
            tmpB = sb("tmpB", [P, KD], F32, ctx)
            st2 = sb("st2", [P, T, 6], F32, ctx)
            mv2 = sb("mv2", [P, T, 2], F32, ctx)
            var2 = sb("var2", [P, T], F32, ctx)
            root2 = sb("root2", [P, T], F32, ctx)
            rstd2 = sb("rstd2", [P, T], F32, ctx)
            tmp2 = sb("tmp2", [P, T], F32, ctx)
            xT = sb("xT", [P, 2, KD, BN_], F32, ctx)
            lT = sb("lT", [NE, 2, BN_], F32, ctx)
            lmax = sb("lmax", [P, LB], F32, ctx)
            is_max = sb("is_max", [P, LB, NE], F32, ctx)
            lfirst = sb("lfirst", [P, LB], F32, ctx)
            down32 = sb("down32", [P, NE], F32, ctx)
            valid = sb("valid", [P, NE], F16, ctx)
            upper = sb("upper", [P, P], F16, ctx)
            before = sb("before", [P, T + 1, NE], F16, ctx)
            picked = sb("picked", [P, 3, LB, NE], F32, ctx)
            per_token = sb("per_token", [P, 3, LB], F32, ctx)
            beyond = sb("beyond", [P, LB], F32, ctx)
            nmr2 = sb("nmr2", [P, T], F32, ctx)
            page_id = sb("page_id", [NE, CHUNKS], F32, ctx)
            first_new = sb("first_new", [NE, NB], F32, ctx)
            new_end = sb("new_end", [NE, NB], F32, ctx)
            from_first = sb("from_first", [NE, NB, CHUNKS], F32, ctx)
            to_end = sb("to_end", [NE, NB, CHUNKS], F32, ctx)
            owned = sb("owned", [NE, CHUNKS], F32, ctx)
            eid = sb("eid", [NE, 1], F32, ctx)
            full_at = sb("full_at", [NE, T + 1], F32, ctx)
            full = sb("full", [NE, T + 1], F32, ctx)
            pages = sb("pages", [NE, NB + 1], F32, ctx)
            new = sb("new", [NE, NB], F32, ctx)
            new_shift = sb("new_shift", [NE, NB], F32, ctx)
            moved = sb("moved", [NE, NB], F32, ctx)
            shifts = sb("shifts", [NE, NB + 1, 3], F32, ctx)
            shift_diag = sb("shift_diag", [NE, 3, NE], F16, ctx)
            upper32 = sb("upper32", [NE, NE], F32, ctx)
            ones_e = sb("ones_e", [NE, NE], F32, ctx)
            page_e = sb("page_e", [NE, P], F16, ctx)
            y_ps = psum("y_ps", [P, 2, 512], F32, ctx)
            x_ps = psum("x_ps", [P, 2, 512], F32, ctx)
            l_ps = psum("l_ps", [NE, 2, 512], F32, ctx)
            lt_ps = psum("lt_ps", [P, 512], F32, ctx)
            m_ps = psum("m_ps", [P, 512], F32, ctx)
            pick_ps = m_ps[:, 0:3 * LB * NE].rearrange("p (a t e) -> p a t e", a=3, e=NE)
            count_ps = m_ps[0:NE, 480:481]
            page_ps = m_ps[0:NE, 484:485]
            expert_ps = m_ps[0:1, 0:CHUNKS]

            s_c = sem("router_constants", ctx)
            s_dve = sem("bn_chain", ctx)
            s_varB = sem("bn_var", ctx)
            s_rootB = sem("bn_root", ctx)
            s_scale = sem("bn_scale", ctx)
            s_bn = sem("bn_applied", ctx)
            s_yT = sem("y_turned", ctx)
            s_x1 = sem("x1_ready", ctx)
            s_st2 = sem("stats2", ctx)
            s_mv2 = sem("mv2_ready", ctx)
            s_var2 = sem("var2_ready", ctx)
            s_root2 = sem("root2_ready", ctx)
            s_r2 = sem("rstd2_ready", ctx)
            s_xn = sem("xn2_ready", ctx)
            s_xT = sem("xn2_turned", ctx)
            s_xTk = sem("xn2_turned_kept", ctx)
            s_l = sem("logits_done", ctx)
            s_lk = sem("logits_kept", ctx)
            s_lT = sem("logits_turned", ctx)
            s_oh = sem("onehot_ready", ctx)
            s_bef = sem("before_ready", ctx)
            s_count = sem("tokens_counted", ctx)
            s_new = sem("new_pages_known", ctx)
            s_first = sem("first_new_page_done", ctx)
            s_shift = sem("shifts_ready", ctx)
            s_shiftb = sem("shifts_broadcast", ctx)
            s_owned = sem("owned_ready", ctx)
            s_exp = sem("experts_done", ctx)
            s_row = sem("rows_ready", ctx)
            s_disp = sem("dispatched", ctx)

            block = ctx.enter_context(nc.Block())

            @block.gpsimd
            def _(pool):
                for to, pattern, base, mult in (
                    (down32[:], [[-1, NE]], NE, 0),
                    (full_at[:], [[P, T + 1]], 0, 0),
                    (page_id[:], [[1, CHUNKS]], 0, 0),
                    (eid[:], [[0, 1]], 0, 1),
                ):
                    pool_.iota(to, pattern, base=base, channel_multiplier=mult,
                               allow_small_or_imprecise_dtypes=True).then_inc(s_c, 1)
                pool_.affine_select(out=valid[:], in_=ones16[:, 0:NE], compare_op=ALU.is_gt, fill=0.0, base=LAST,
                                    pattern=[[0, NE]], channel_multiplier=-1).then_inc(s_c, 1)
                pool_.affine_select(out=upper[:], in_=ones16[:], compare_op=ALU.is_gt, fill=0.0, base=0,
                                    pattern=[[1, P]], channel_multiplier=-1).then_inc(s_c, 1)
                pool_.memset(ones_e[:], 1.0).then_inc(s_c, 1)
                pool_.memset(pages[:, 0:1], 0.0).then_inc(s_c, 1)
                pool_.memset(shifts[:, 0, 0:1], 0.0).then_inc(s_c, 1)
                pool_.memset(page_e[:], float(P)).then_inc(s_c, 1)
                pool.wait_ge(s_c, 10)
                pool_.affine_select(out=upper32[:], in_=ones_e[:], compare_op=ALU.is_gt, fill=0.0,
                                    base=0, pattern=[[1, NE]], channel_multiplier=-1).then_inc(s_c, 1)
                pool_.memset(before[:, 0, :], 0.0).then_inc(s_bef, 1)

                def count(b):
                    pool.wait_ge(s_oh, b + 1)
                    for t in range(b * LB, (b + 1) * LB):
                        pool.wait_ge(s_bef, t + 1)
                        pool_.tensor_tensor(before[:, t + 1, :], before[:, t, :], onehot[:, t, :],
                                            ALU.add).then_inc(s_bef, 1)

                def dispatch(b):
                    pool.wait_ge(s_row, b + 1)
                    for t in range(b * LB, (b + 1) * LB):
                        n = P if t < T - 1 else LAST
                        pool_.indirect_dma_start(
                            by_expert, bass.IndirectOffsetOnAxis(ap=row[0:n, t:t + 1], axis=0),
                            xs[0:n, t, :], None).then_inc(s_disp, 16)

                for b in range(NB):
                    count(b)
                    if b >= 1:
                        dispatch(b - 1)
                dispatch(NB - 1)
                pool.wait_ge(s_disp, 16 * T)

            @block.tensor
            def _(pe):
                def turn_y(u):
                    t0, n = unit_tiles(u)
                    pe.wait_ge(s_bn, KD * (u // UNITS + 1))
                    if u >= 2:
                        pe.wait_ge(s_x1, u - 1)
                    for i in range(n):
                        for k in range(KD):
                            last = pe_.transpose(y_ps[:, u % 2, (i * KD + k) * P:(i * KD + k + 1) * P],
                                                 hT[:, k, (t0 + i) * P:(t0 + i + 1) * P], ident[:])
                    last.then_inc(s_yT, 1)

                def turn_x(u):
                    t0, n = unit_tiles(u)
                    pe.wait_ge(s_xn, t0 + n)
                    if u >= 2:
                        pe.wait_ge(s_xTk, u - 1)
                    for i in range(n):
                        for k in range(KD):
                            last = pe_.transpose(x_ps[:, u % 2, (i * KD + k) * P:(i * KD + k + 1) * P],
                                                 xs[:, t0 + i, k * P:(k + 1) * P], ident[:])
                    last.then_inc(s_xT, 1)

                def logits(b, i):
                    pe.wait_ge(s_xTk, b * UNITS + ceil_div((i + 1) * HB, 2 * P))
                    if b >= 1:
                        pe.wait_ge(s_lk, b)
                    for k in range(KD):
                        last = pe_.matmul(l_ps[:, i, 0:HB], rwT[:, k, :], xT[:, b % 2, k, i * HB:(i + 1) * HB],
                                          start=(k == 0), stop=(k == KD - 1))
                    if i == 1:
                        last.then_inc(s_l, 1)

                def turn_logits(b):
                    pe.wait_ge(s_lk, b + 1)
                    if b >= 1:
                        pe.wait_ge(s_oh, b)
                    for j in range(LB):
                        last = pe_.transpose(lt_ps[:, j * NE:(j + 1) * NE], lT[:, b % 2, j * P:(j + 1) * P],
                                             ident[0:NE, 0:NE])
                    last.then_inc(s_lT, 1)

                def count_tokens(b):
                    pe.wait_ge(s_oh, b + 1)
                    pe.wait_ge(s_bef, b * LB + 1)
                    if b >= 1:
                        pe.wait_ge(s_row, b)
                    pe_.matmul(count_ps, before[:, b * LB, :], ones16[:, 0:1], start=True, stop=False,
                               skip_group_check=True)
                    for t in range(b * LB, (b + 1) * LB):
                        last = pe_.matmul(count_ps, onehot[:, t, :], ones16[:, 0:1], start=False,
                                          stop=(t == (b + 1) * LB - 1), skip_group_check=True)
                    last.then_inc(s_count, 1)

                def first_new_page(b):
                    pe.wait_ge(s_new, b + 1)
                    pe_.matmul(page_ps, ones_e[:], pages[:, b:b + 1], start=True, stop=False, skip_group_check=True)
                    pe_.matmul(page_ps, upper32[:], new[:, b:b + 1], start=False, stop=True,
                               skip_group_check=True).then_inc(s_first, 1)

                def rank_and_shifts(b):
                    ts = slice(b * LB, (b + 1) * LB)
                    pe.wait_ge(s_bef, (b + 1) * LB)
                    pe.wait_ge(s_shift, b + 1)
                    pe_.matmul(pick_ps[:, 0], upper[:], onehot[:, ts, :], start=True, stop=False,
                               skip_group_check=True)
                    pe_.matmul(pick_ps[:, 0], ones16[:], before[:, ts, :], start=False, stop=False,
                               skip_group_check=True)
                    for i in range(3):
                        last = pe_.matmul(pick_ps[:, i], page_e[:],
                                          shift_diag[:, i, :].unsqueeze(1).broadcast_to([NE, LB, NE]),
                                          start=(i > 0), stop=True, skip_group_check=True)
                    last.then_inc(s_shiftb, 1)

                pe.wait_ge(s_c, 11)
                for u in range(UNITS):
                    turn_y(u)
                for b in range(NB):
                    ahead = range((b + 1) * UNITS, (b + 2) * UNITS) if b + 1 < NB else ()
                    for u in ahead[:-1]:
                        turn_y(u)
                    for u in range(b * UNITS, (b + 1) * UNITS):
                        turn_x(u)
                    if b >= 1:
                        count_tokens(b - 1)
                    logits(b, 0)
                    for u in ahead[-1:]:
                        turn_y(u)
                    logits(b, 1)
                    turn_logits(b)
                    if b >= 1:
                        first_new_page(b - 1)
                        rank_and_shifts(b - 1)
                count_tokens(NB - 1)
                first_new_page(NB - 1)
                rank_and_shifts(NB - 1)
                pe.wait_ge(s_row, NB)
                pe.wait_ge(s_owned, 1)
                pe_.matmul(expert_ps, eid[:], owned[:], start=True, stop=True, skip_group_check=True)\
                   .then_inc(s_exp, 1)

            @block.scalar
            def _(act):
                act.wait_ge(s_varB, 1)
                act_.activation(rootB[:], varB[:], ACT.Sqrt).then_inc(s_rootB, 1)
                act.wait_ge(s_scale, 1)

                def apply_bn(b):
                    for k in range(KD):
                        cols = hT[:, k, b * BN_:(b + 1) * BN_]
                        act_.activation(cols, cols, ACT.Identity, bias=shiftB[:, k:k + 1],
                                        scale=scaleB[:, k:k + 1]).then_inc(s_bn, 1)

                def root(b):
                    act.wait_ge(s_var2, b + 1)
                    act_.activation(root2[:, b * LB:(b + 1) * LB], var2[:, b * LB:(b + 1) * LB],
                                    ACT.Sqrt).then_inc(s_root2, 1)

                def normalise(b):
                    act.wait_ge(s_r2, b + 1)
                    for t in range(b * LB, (b + 1) * LB):
                        act_.activation(xs[:, t, :], xt[:, t, :], ACT.Identity, bias=nmr2[:, t:t + 1],
                                        scale=rstd2[:, t:t + 1]).then_inc(s_xn, 1)

                def keep_x(b):
                    for u in range(b * UNITS, (b + 1) * UNITS):
                        t0, n = unit_tiles(u)
                        act.wait_ge(s_xT, u + 1)
                        if b >= 2:
                            act.wait_ge(s_l, b - 1)
                        cols = xT[:, b % 2, :, (t0 - b * LB) * P:(t0 - b * LB + n) * P]
                        act_.activation(cols.rearrange("p k (i n) -> p i k n", n=P),
                                        x_ps[:, u % 2, 0:n * D].rearrange("p (i k n) -> p i k n", k=KD, n=P),
                                        ACT.Copy).then_inc(s_xTk, 1)

                def keep_logits(b):
                    act.wait_ge(s_l, b + 1)
                    if b >= 2:
                        act.wait_ge(s_lT, b - 1)
                    act_.activation(lT[:, b % 2, :].rearrange("p (i n) -> p i n", i=2), l_ps[:, :, 0:HB],
                                    ACT.Identity, bias=rbT[:]).then_inc(s_lk, 1)

                apply_bn(0)
                apply_bn(1)
                root(0)
                apply_bn(2)
                normalise(0)
                for b in range(NB):
                    keep_x(b)
                    if b + 3 < NB:
                        apply_bn(b + 3)
                    if b + 1 < NB:
                        root(b + 1)
                    keep_logits(b)
                    if b + 1 < NB:
                        normalise(b + 1)

            @block.vector
            def _(vec):
                link = chained(vec, s_dve)
                for k in range(KD):
                    last = dve.bn_aggr(mvB[:, k, :], bstats[:, k, :, :].rearrange("p g s -> p (g s)"))
                link(last)
                dve.tensor_scalar(varB[:], mvB[:, :, 1], BN_EPS, None, ALU.add).then_inc(s_varB, 1)
                vec.wait_ge(s_rootB, 1)
                rsqrt(link, dve, scaleB[:], rootB[:], varB[:], tmpB[:])
                link(dve.tensor_tensor(scaleB[:], scaleB[:], gam[:], ALU.mult))
                link(dve.tensor_tensor(tmpB[:], mvB[:, :, 0], scaleB[:], ALU.mult))
                dve.tensor_tensor(shiftB[:], bet[:], tmpB[:], ALU.subtract).then_inc(s_scale, 1)

                def residual(b):
                    def stats_of(u):
                        t0, n = unit_tiles(u)
                        vec.wait_ge(s_x1, u + 1)
                        for t in range(t0, t0 + n):
                            dve.bn_stats(st2[:, t, :], xt[:, t, :]).then_inc(s_st2, 1)

                    for u in range(b * UNITS, (b + 1) * UNITS):
                        t0, n = unit_tiles(u)
                        vec.wait_ge(s_yT, u + 1)
                        dve.tensor_tensor(xt[:, t0:t0 + n, :], xt[:, t0:t0 + n, :],
                                          y_ps[:, u % 2, 0:n * D].rearrange("p (t d) -> p t d", d=D), ALU.add)\
                           .then_inc(s_x1, 1)
                        if u > b * UNITS:
                            stats_of(u - 1)
                    stats_of((b + 1) * UNITS - 1)
                    vec.wait_ge(s_st2, (b + 1) * LB)
                    for t in range(b * LB, (b + 1) * LB):
                        dve.bn_aggr(mv2[:, t, :], st2[:, t, :]).then_inc(s_mv2, 1)
                    vec.wait_ge(s_mv2, (b + 1) * LB)
                    ts = slice(b * LB, (b + 1) * LB)
                    dve.tensor_scalar(var2[:, ts], mv2[:, ts, 1], LN_EPS, None, ALU.add).then_inc(s_var2, 1)

                def rstd_of(b):
                    ts = slice(b * LB, (b + 1) * LB)
                    vec.wait_ge(s_root2, b + 1)
                    rsqrt(link, dve, rstd2[:, ts], root2[:, ts], var2[:, ts], tmp2[:, ts])
                    dve.scalar_tensor_tensor(out=nmr2[:, ts], in0=mv2[:, ts, 0], scalar=-1.0, in1=rstd2[:, ts],
                                             op0=ALU.mult, op1=ALU.mult).then_inc(s_r2, 1)

                def choose_start(b):
                    vec.wait_ge(s_lT, b + 1)
                    lg = lt_ps[:, 0:LB * NE].rearrange("p (t e) -> p t e", e=NE)
                    link(dve.tensor_reduce(lmax[:], lg, AX.X, ALU.max))
                    link(dve.tensor_tensor(is_max[:], lg, lmax[:].unsqueeze(2).broadcast_to([P, LB, NE]),
                                           ALU.is_ge))

                def choose(b):
                    down = down32[:].unsqueeze(1).broadcast_to([P, LB, NE])
                    link(dve.tensor_tensor(is_max[:], is_max[:], down, ALU.mult))
                    link(dve.tensor_reduce(lfirst[:], is_max[:], AX.X, ALU.max))
                    hits = dve.tensor_tensor(onehot[:, b * LB:(b + 1) * LB, :], down,
                                             lfirst[:].unsqueeze(2).broadcast_to([P, LB, NE]), ALU.is_equal)
                    if b < NB - 1:
                        hits.then_inc(s_oh, 1)
                    else:
                        link(hits)
                        dve.tensor_tensor(onehot[:, T - 1, :], onehot[:, T - 1, :], valid[:],
                                          ALU.mult).then_inc(s_oh, 1)

                def new_pages(b):
                    vec.wait_ge(s_count, b + 1)
                    link(dve.tensor_scalar(full[:], full_at[:], count_ps, 0.0, ALU.is_lt, ALU.add,
                                           accum_out=pages[:, b + 1:b + 2]))
                    dve.tensor_tensor(new[:, b:b + 1], pages[:, b + 1:b + 2], pages[:, b:b + 1],
                                      ALU.subtract).then_inc(s_new, 1)

                def shifts_of(b):
                    vec.wait_ge(s_first, b + 1)
                    old, limit, change = (shifts[:, b, i:i + 1] for i in range(3))
                    link(dve.tensor_tensor(new_shift[:, b:b + 1], page_ps, pages[:, b:b + 1], ALU.subtract))
                    link(dve.tensor_tensor(limit, old, pages[:, b:b + 1], ALU.add))
                    link(dve.tensor_tensor(change, new_shift[:, b:b + 1], old, ALU.subtract))
                    dve.tensor_tensor(shift_diag[:], ident[0:NE, 0:NE].unsqueeze(1).broadcast_to([NE, 3, NE]),
                                      shifts[:, b, :].unsqueeze(2).broadcast_to([NE, 3, NE]), ALU.mult)\
                       .then_inc(s_shift, 1)
                    link(dve.scalar_tensor_tensor(out=moved[:, b:b + 1], in0=new[:, b:b + 1], scalar=0.0,
                                                  in1=change, op0=ALU.is_gt, op1=ALU.mult))
                    link(dve.tensor_tensor(shifts[:, b + 1, 0:1], old, moved[:, b:b + 1], ALU.add))

                def place(b):
                    vec.wait_ge(s_shiftb, b + 1)
                    ts = slice(b * LB, (b + 1) * LB)
                    link(dve.tensor_tensor(picked[:], pick_ps, onehot[:, ts, :].unsqueeze(1)
                                           .broadcast_to([P, 3, LB, NE]), ALU.mult))
                    link(dve.tensor_reduce(per_token[:], picked[:], AX.X, ALU.add))
                    shifted, limit, change = (per_token[:, i, :] for i in range(3))
                    link(dve.tensor_tensor(beyond[:], shifted, limit, ALU.is_ge))
                    link(dve.tensor_tensor(beyond[:], beyond[:], change, ALU.mult))
                    dve.tensor_tensor(row[:, ts], shifted, beyond[:], ALU.add).then_inc(s_row, 1)

                vec.wait_ge(s_c, 11)
                residual(0)
                rstd_of(0)
                for b in range(NB):
                    if b + 1 < NB:
                        residual(b + 1)
                    if b >= 1:
                        new_pages(b - 1)
                    if b + 1 < NB:
                        rstd_of(b + 1)
                    choose_start(b)
                    if b >= 1:
                        shifts_of(b - 1)
                    choose(b)
                    if b >= 1:
                        place(b - 1)
                new_pages(NB - 1)
                shifts_of(NB - 1)
                place(NB - 1)
                link(dve.tensor_tensor(first_new[:], new_shift[:], pages[:, 0:NB], ALU.add))
                link(dve.tensor_tensor(new_end[:], first_new[:], new[:], ALU.add))
                page = page_id[:].unsqueeze(1).broadcast_to([NE, NB, CHUNKS])
                link(dve.tensor_tensor(from_first[:], page, first_new[:].unsqueeze(2)
                                       .broadcast_to([NE, NB, CHUNKS]), ALU.is_ge))
                link(dve.tensor_tensor(to_end[:], page, new_end[:].unsqueeze(2).broadcast_to([NE, NB, CHUNKS]),
                                       ALU.is_lt))
                link(dve.tensor_tensor(from_first[:], from_first[:], to_end[:], ALU.mult))
                dve.tensor_reduce(owned[:], from_first[:].rearrange("e b q -> e q b"), AX.X, ALU.add)\
                   .then_inc(s_owned, 1)
                vec.wait_ge(s_exp, 1)
                dve.tensor_copy(expert[:], expert_ps)

        SLOTS = 8
        PARTS = 4
        PART = SLOTS // PARTS
        WS = 4
        RC = CHUNKS // SLOTS
        assert CHUNKS % SLOTS == 0
        page_bound = [((b + 1) * BN_ + NE * (P - 1)) // P for b in range(NB)]
        with ExitStack() as ctx:
            xg = sb("xg", [P, SLOTS, D], F32, ctx)
            wc = sb("wc", [P, WS, EWC], F32, ctx)
            xgT = sb("xgT", [P, 2, KD, P], F32, ctx)
            hg = sb("hg", [EH + 1, 2, P], F32, ctx)
            og = sb("og", [P, SLOTS, D], F32, ctx)
            t_ps = psum("t_ps", [P, 2, 512], F32, ctx)
            u_ps = psum("u_ps", [P, 2, 512], F32, ctx)
            d_ps = psum("d_ps", [P, 2, 512], F32, ctx)
            s_in = [sem(f"pages_in{h}", ctx) for h in range(PARTS)]
            s_st = [sem(f"pages_out{h}", ctx) for h in range(PARTS)]
            s_wc = sem("expert_copied", ctx)
            s_t = sem("page_turned", ctx)
            s_tk = sem("page_turned_kept", ctx)
            s_u = sem("expert_up", ctx)
            s_uk = sem("expert_relu", ctx)
            s_d = sem("expert_down", ctx)
            s_dk = sem("expert_kept", ctx)
            s_one = sem("ones_row", ctx)
            s_taken = [sem(f"tokens_taken{b}", ctx) for b in range(NB - 1)]
            s_last = [sem(f"last_tokens_taken{j}", ctx) for j in range(LB)]
            s_add = sem("added", ctx)
            s_o = sem("stored", ctx)
            block = ctx.enter_context(nc.Block())

            def take_batch(pool, b):
                parts = ceil_div(page_bound[b], PART)
                for h in range(PARTS):
                    pool.wait_ge(s_st[h], 16 * ceil_div(parts - h, PARTS))
                for t in range(b * LB, (b + 1) * LB):
                    n = P if t < T - 1 else LAST
                    pool_.indirect_dma_start(
                        xs[0:n, t, :], None, slots_out[0:min(parts * PART, CHUNKS) * P, :],
                        bass.IndirectOffsetOnAxis(ap=row[0:n, t:t + 1], axis=0)
                    ).then_inc(s_taken[b] if b < NB - 1 else s_last[t - b * LB], 16)

            @block.gpsimd
            def _(pool):
                pool_.memset(hg[EH:EH + 1], 1.0).then_inc(s_one, 1)
                for b in range(NB):
                    take_batch(pool, b)
                for b in range(NB - 1):
                    pool.wait_ge(s_taken[b], 16 * LB)
                for s in s_last:
                    pool.wait_ge(s, 16)

            @block.sync
            def _(sp):
                def pages_of(dram, r, h):
                    return dram.rearrange("(q p) d -> p q d", p=P)[:, bass.ds(r * SLOTS + h * PART, PART), :]

                def load(r, h, later):
                    if later:
                        sp.wait_ge(s_t, r * SLOTS + (h + 1) * PART - SLOTS)
                    sp.dma_start(xg[:, h * PART:(h + 1) * PART, :], pages_of(by_expert, r, h))\
                      .then_inc(s_in[h], 16)

                def store(r, h):
                    sp.wait_ge(s_dk, r * SLOTS + (h + 1) * PART)
                    sp.dma_start(pages_of(slots_out, r, h), og[:, h * PART:(h + 1) * PART, :])\
                      .then_inc(s_st[h], 16)

                for h in range(PARTS):
                    load(0, h, False)
                with sp.Fori(0, RC - 1) as r:
                    for h in range(PARTS):
                        load(r + 1, h, True)
                        store(r, h)
                for h in range(PARTS):
                    store(RC - 1, h)
                for b in range(NB - 1):
                    sp.wait_ge(s_add, b + 1)
                    sp.dma_start(out[b * BN_:(b + 1) * BN_, :].rearrange("(t p) d -> p t d", p=P),
                                 xt[:, b * LB:(b + 1) * LB, :]).then_inc(s_o, 16)
                for t in range(T - LB, T):
                    n = P if t < T - 1 else LAST
                    sp.wait_ge(s_add, t - (T - LB) + NB)
                    sp.dma_start(out[t * P:t * P + n, :], xt[0:n, t, :]).then_inc(s_o, 16)
                sp.wait_ge(s_o, 16 * (NB - 1 + LB))

            @block.tensor
            def _(pe):
                def turn(c, i, later):
                    if i % PART == 0:
                        pe.wait_ge(s_in[i // PART], (c - i) * (16 // SLOTS) + 16)
                    if later or i >= 2:
                        pe.wait_ge(s_tk, c - 1)
                    for k in range(KD):
                        last = pe_.transpose(t_ps[:, i % 2, k * P:(k + 1) * P],
                                             xg[:, i, :].rearrange("p (d k) -> p k d", k=KD)[:, k, :], ident[:])
                    last.then_inc(s_t, 1)

                def up(c, i, later):
                    pe.wait_ge(s_tk, c + 1)
                    pe.wait_ge(s_wc, c + 1)
                    if later or i >= 2:
                        pe.wait_ge(s_uk, c - 1)
                    for k in range(KD):
                        last = pe_.matmul(u_ps[0:EH, i % 2, 0:P], wc[:, i % WS, k * EH:(k + 1) * EH],
                                          xgT[:, i % 2, k, :], start=(k == 0), stop=(k == KD - 1))
                    last.then_inc(s_u, 1)

                def down(c, i, later):
                    pe.wait_ge(s_uk, c + 1)
                    if later or i >= 2:
                        pe.wait_ge(s_dk, c - 1)
                    pe_.matmul(d_ps[:, i % 2, 0:D], hg[:, i % 2, :], wc[0:EH + 1, i % WS, C1:C2], start=True,
                               stop=True).then_inc(s_d, 1)

                turn(0, 0, False)
                turn(1, 1, False)
                up(0, 0, False)
                for i in range(2, SLOTS):
                    turn(i, i, False)
                    up(i - 1, i - 1, False)
                    down(i - 2, i - 2, False)
                with pe.Fori(1, RC) as r:
                    c = r * SLOTS
                    for i in range(SLOTS):
                        turn(c + i, i, True)
                        up(c + i - 1, (i - 1) % SLOTS, True)
                        down(c + i - 2, (i - 2) % SLOTS, True)
                up(CHUNKS - 1, SLOTS - 1, True)
                down(CHUNKS - 2, SLOTS - 2, True)
                down(CHUNKS - 1, SLOTS - 1, True)

            @block.scalar
            def _(act):
                act.wait_ge(s_one, 1)

                def keep_turned(c, i, later):
                    act.wait_ge(s_t, c + 1)
                    if later or i >= 2:
                        act.wait_ge(s_u, c - 1)
                    act_.activation(xgT[:, i % 2].rearrange("p k n -> p (k n)"), t_ps[:, i % 2, 0:KD * P],
                                    ACT.Copy).then_inc(s_tk, 1)

                def relu(c, i, later):
                    act.wait_ge(s_u, c + 1)
                    if later or i >= 2:
                        act.wait_ge(s_d, c - 1)
                    act_.activation(hg[0:EH, i % 2, :], u_ps[0:EH, i % 2, 0:P], ACT.Relu,
                                    bias=wc[0:EH, i % WS, C2:C2 + 1]).then_inc(s_uk, 1)

                keep_turned(0, 0, False)
                for i in range(1, SLOTS):
                    keep_turned(i, i, False)
                    relu(i - 1, i - 1, False)
                with act.Fori(1, RC) as r:
                    c = r * SLOTS
                    for i in range(SLOTS):
                        keep_turned(c + i, i, True)
                        relu(c + i - 1, (i - 1) % SLOTS, True)
                relu(CHUNKS - 1, SLOTS - 1, True)

            @block.vector
            def _(vec):
                def experts_of(r):
                    return nc.values_load_multi_w_load_instructions(
                        expert[0:1, bass.ds(r * WS, WS)], engines=[mybir.EngineType.DVE], min_val=0,
                        max_val=NE - 1, skip_runtime_bounds_check_because="an expert is always one of the NE")[1]

                def fetch(e, c, i, later):
                    if later or i >= WS:
                        vec.wait_ge(s_d, c - WS + 1)
                    dve.tensor_copy(wc[:, i % WS, :], ew[:, bass.ds(e, 1), :].rearrange("p a n -> p (a n)"))\
                       .then_inc(s_wc, 1)

                def keep(c, i, later):
                    vec.wait_ge(s_d, c + 1)
                    if later and i % PART == 0:
                        vec.wait_ge(s_st[i // PART], (c - i) * (16 // SLOTS))
                    dve.tensor_scalar(og[:, i, :], d_ps[:, i % 2, 0:D], 0.0, None, ALU.max).then_inc(s_dk, 1)

                for i in range(SLOTS):
                    if i % WS == 0:
                        es_ = experts_of(i // WS)
                    fetch(es_[i % WS], i, i, False)
                    if i >= 2:
                        keep(i - 2, i - 2, False)
                with vec.Fori(1, RC) as r:
                    c = r * SLOTS
                    for i in range(SLOTS):
                        if i % WS == 0:
                            es_ = experts_of(r * (SLOTS // WS) + i // WS)
                        fetch(es_[i % WS], c + i, i, True)
                        keep(c + i - 2, (i - 2) % SLOTS, i >= 2)
                keep(CHUNKS - 2, SLOTS - 2, True)
                keep(CHUNKS - 1, SLOTS - 1, True)
                for b in range(NB - 1):
                    vec.wait_ge(s_taken[b], 16 * LB)
                    ts = slice(b * LB, (b + 1) * LB)
                    dve.tensor_tensor(xt[:, ts, :], xt[:, ts, :], xs[:, ts, :], ALU.add).then_inc(s_add, 1)
                for t in range(T - LB, T):
                    n = P if t < T - 1 else LAST
                    vec.wait_ge(s_last[t - (T - LB)], 16)
                    dve.tensor_tensor(xt[0:n, t, :], xt[0:n, t, :], xs[0:n, t, :], ALU.add).then_inc(s_add, 1)


_INS = ["x", "src", "dst", "L0_gnn_eps", "L0_gnn_W1", "L0_gnn_b1", "L0_gnn_W2", "L0_gnn_b2", "L0_gnn_gamma",
        "L0_gnn_beta", "L0_ffn_router_w", "L0_ffn_router_b", "L0_ffn_W1", "L0_ffn_b1", "L0_ffn_W2", "L0_ffn_b2"]


def kernel(**inputs):
    import numpy as _np
    import concourse.bacc as _bacc
    from concourse import mybir as _mybir
    from concourse.bass_utils import run_bass_kernel_spmd as _run

    nc = _bacc.Bacc("TRN2", target_bir_lowering=False, num_devices=1)
    arrays, args = {}, []
    for name in _INS:
        a = _np.ascontiguousarray(inputs[name])
        arrays[f"in_{name}_dram"] = a
        args.append(nc.dram_tensor(f"in_{name}_dram", a.shape, _mybir.dt.from_np(a.dtype), kind="ExternalInput").ap())
    args.append(nc.dram_tensor("out_dram", arrays["in_x_dram"].shape, _mybir.dt.float32, kind="ExternalOutput").ap())
    gnn_moe_kernel(nc, *args)
    r = _run(nc, [arrays], core_ids=[0])
    return r.results[0]["out_dram"]
```

```python
from contextlib import ExitStack

import concourse.bass as bass
from concourse import mybir

ALU = mybir.AluOpType
ACT = mybir.ActivationFunctionType
AX = mybir.AxisListType
F32 = mybir.dt.float32
F16 = mybir.dt.float16
I32 = mybir.dt.int32

P = 128
LN_EPS = 1e-5
BN_EPS = 1e-5
WSCALE = 256.0
HSCALE = 16.0
W_BOUND = 120.0
H_BOUND = 2000.0
XSCALE = 2048.0

EPART = 125

W = 5
QUAD = 4
BPS = 2 * QUAD
STEPS = 10
GN = STEPS * BPS * W

SLOTS = 8
SPARE_ROWS = SLOTS * P


def ceil_div(a, b):
    return -(-a // b)


def chained(eng, sem):
    count = [0]

    def link(ins):
        count[0] += 1
        ins.then_inc(sem, 1)
        eng.wait_ge(sem, count[0])

    return link


def rsqrt(link, vec, r, root, var, t):
    link(vec.reciprocal(r, root))
    link(vec.scalar_tensor_tensor(out=t, in0=r, scalar=-0.5, in1=var, op0=ALU.mult, op1=ALU.mult))
    link(vec.tensor_tensor(t, t, r, ALU.mult))
    link(vec.scalar_tensor_tensor(out=r, in0=t, scalar=1.5, in1=r, op0=ALU.add, op1=ALU.mult))


def gnn_moe_kernel(nc, x, src, dst, eps, gw1, gb1, gw2, gb2, gamma, beta, rw, rb, ew1, eb1, ew2, eb2, out):
    N, D = x.shape
    E = src.shape[0]
    H = gw1.shape[1]
    NE, _, EH = ew1.shape
    T = ceil_div(N, P)
    LAST = N - (T - 1) * P
    KD = D // P
    KH = H // P
    EK = E // EPART
    GROUPS = ceil_div(N, GN)
    NP = GROUPS * GN
    BLOCKS = NP // W
    BC = ceil_div(BLOCKS, P)
    Z = T * W
    ZP = Z + 1
    CHUNKS = (N + NE * (P - 1)) // P
    TPP = T // (STEPS // 2)
    XG = 5
    XT = T // XG
    assert NP == T * P and D == 2 * P and EPART * EK == E and T % XG == 0 and QUAD * ZP <= 512

    DW = D + 1
    by_expert = nc.dram_tensor("by_expert", [CHUNKS * P, DW], F32, kind="Internal").ap()

    top = ExitStack()

    def sb(name, shape, dt, ctx=top):
        return ctx.enter_context(nc.sbuf_tensor(name, shape, dt))

    def psum(name, shape, dt, ctx):
        return ctx.enter_context(nc.psum_tensor(name, shape, dt))

    def sem(name, ctx):
        return ctx.enter_context(nc.semaphore(name))

    with top:
        ident = sb("ident", [P, P], F32)
        ones16 = sb("ones16", [P, P], F16)
        xt = sb("xt", [P, T, D], F32)
        xs = sb("xs", [P, T, DW], F32)
        hT = sb("hT", [P, KD, NP], F32)
        page_total = sb("page_total", [1, 1], I32)
        overflow = sb("overflow", [1, 1], I32)
        w1s = sb("w1s", [P, 2, KD, H], F16)
        w2s = sb("w2s", [P, 2, KH, D], F16)
        ones32 = sb("ones32", [P, 1], F32)
        wst = sb("wst", [P, 4, 6], F32)
        total = sb("total", [1, 1], I32)
        w1 = sb("w1", [P, KD, H], F32)
        w2 = sb("w2", [P, KH, D], F32)
        b1 = sb("b1", [P, KH], F32)
        b2 = sb("b2", [P, KD], F32)
        gam = sb("gam", [P, KD], F32)
        bet = sb("bet", [P, KD], F32)
        rwT = sb("rwT", [P, KD, NE], F32)
        rbT = sb("rbT", [NE, 1], F32)
        agg = top.enter_context(ExitStack())
        iota16 = sb("iota16", [P, P], F16, agg)
        xhl = sb("xhl", [P, T, 2, D], F16, agg)
        z2 = sb("z2", [P, BC * P, 2], F16, agg)
        slo2 = sb("slo2", [P, BC * P, 2], F16, agg)
        epsT = sb("epsT", [P, 1], F32, agg)
        selfw = sb("selfw", [P, 1], F32, agg)
        idx = sb("idx", [P, BC], I32, agg)
        thr = sb("thr", [P, BC * P], F32, agg)
        rows = sb("rows", [P, BC, 2, P], I32, agg)
        rowsf = sb("rowsf", [P, BC, 2, P], F32, agg)
        dstT = sb("dstT", [P, BC * P], F32, agg)
        srcT = sb("srcT", [P, BC * P], I32, agg)
        ti = sb("ti", [P, BC * P], I32, agg)
        f1 = sb("f1", [P, BC * P], F32, agg)
        f2 = sb("f2", [P, BC * P], F32, agg)
        found = sb("found", [P, BC], F32, agg)

        dve, act_, pe_, pool_ = nc.vector, nc.scalar, nc.tensor, nc.gpsimd

        def gather_row(pool, c, gathered):
            for i, edges in enumerate((dst, src)):
                pool_.indirect_dma_start(
                    rows[:, c, i, :], None, edges.rearrange("(e a) -> e a", a=1),
                    bass.IndirectOffsetOnAxis(ap=idx[:, c:c + 1], axis=0)
                ).then_inc(gathered, 16)

        def turn_row(c, turned_ps):
            for i in range(2):
                last = pe_.transpose(turned_ps[:, i, c * P:(c + 1) * P], rowsf[:, c, i, :], ident[:])
            return last

        def unpack_rows(link, c0, c1, counted=None):
            n = (c1 - c0) * P
            s = slice(c0 * P, c1 * P)
            link(dve.tensor_scalar(ti[:, s], srcT[:, s], P - 1, None, ALU.bitwise_and))
            link(dve.tensor_copy(slo2[:, s], ti[:, s].unsqueeze(2).broadcast_to([P, n, 2])))
            link(dve.tensor_scalar(ti[:, s], srcT[:, s], P.bit_length() - 1, None, ALU.arith_shift_right))
            link(dve.tensor_tensor(f1[:, s], dstT[:, s], thr[:, s], ALU.subtract))
            link(dve.tensor_scalar(f2[:, s], f1[:, s], 0.0, None, ALU.is_ge))
            link(dve.scalar_tensor_tensor(out=f2[:, s], in0=f1[:, s], scalar=float(W), in1=f2[:, s],
                                          op0=ALU.is_lt, op1=ALU.mult))
            if counted is not None:
                link(dve.tensor_scalar(f2[:, s], f2[:, s], counted, None, ALU.mult))
            link(dve.tensor_reduce(found[:, c0:c1], f2[:, s].rearrange("p (c b) -> p c b", b=P), AX.X, ALU.add))
            link(dve.scalar_tensor_tensor(out=f1[:, s], in0=ti[:, s], scalar=float(W), in1=f1[:, s],
                                          op0=ALU.mult, op1=ALU.add))
            link(dve.scalar_tensor_tensor(out=f1[:, s], in0=f1[:, s], scalar=1.0, in1=f2[:, s],
                                          op0=ALU.add, op1=ALU.mult))
            link(dve.tensor_scalar(z2[:, s], f1[:, s].unsqueeze(2).broadcast_to([P, n, 2]), -1.0, None, ALU.add))

        BATCH = 4
        batches = [(t, min(BATCH, T - t)) for t in range(0, T, BATCH)]

        def turn_self(pe, i, selfT, self_turned, self_kept, xs_ready=None):
            t0, n = batches[i]
            if xs_ready is not None:
                pe.wait_ge(xs_ready, t0 + n)
            if i >= 1:
                pe.wait_ge(self_kept, KD * i)
            for k in range(KD):
                for j in range(n):
                    last = pe_.transpose(selfT[:, k, j * P:(j + 1) * P], xs[:, t0 + j, k * P:(k + 1) * P], ident[:])
            last.then_inc(self_turned, 1)

        def keep_self(act, i, selfT, self_turned, self_kept):
            t0, n = batches[i]
            act.wait_ge(self_turned, i + 1)
            for k in range(KD):
                act_.activation(hT[:, k, t0 * P:(t0 + n) * P], selfT[:, k, 0:n * P], ACT.Copy,
                                scale=selfw[:]).then_inc(self_kept, 1)

        class Pass:

            def __init__(self, tag, ctx):
                self.zoh = sb(f"zoh{tag}", [P, 2, BPS, ZP], F16, ctx)
                self.soh = sb(f"soh{tag}", [P, 2, BPS, P], F16, ctx)
                self.at = sb(f"at{tag}", [P, 2, T, GN], F16, ctx)
                self.build_ps = psum(f"build_ps{tag}", [P, 2, 2, 512], F32, ctx)
                self.h_ps = psum(f"h_ps{tag}", [P, 2, KD, 512], F32, ctx)
                names = ("onehots_ready", "built", "at_ready", "ax_done", "h_added")
                self.sems = [nc.alloc_semaphore(f"{n}{tag}") for n in names]
                self.s_oh, self.s_built, self.s_at, self.s_ax, self.s_h = self.sems

            def onehots(self, vec, step, u, wait):
                if wait:
                    vec.wait_ge(self.s_built, step - 1)
                for to, n, vals in ((self.zoh, ZP, z2), (self.soh, P, slo2)):
                    dve.tensor_tensor(
                        to[:, u].rearrange("p b (i two) -> p b i two", two=2),
                        iota16[:, 0:n].rearrange("p (i two) -> p i two", two=2).unsqueeze(1)
                        .broadcast_to([P, BPS, n // 2, 2]),
                        vals[:, bass.ds(step * BPS, BPS), :].unsqueeze(2).broadcast_to([P, BPS, n // 2, 2]),
                        ALU.is_equal).then_inc(self.s_oh, 1)

            def add(self, vec, g):
                vec.wait_ge(self.s_ax, g + 1)
                for k in range(KD):
                    cols = hT[:, k, g * GN:(g + 1) * GN]
                    dve.scalar_tensor_tensor(out=cols, in0=self.h_ps[:, g % 2, k, 0:GN], scalar=1.0 / XSCALE,
                                             in1=cols, op0=ALU.mult, op1=ALU.add).then_inc(self.s_h, 1)

            def vector_group(self, vec, g, self_kept=None):
                self.onehots(vec, g * STEPS, 0, g > 0)
                self.onehots(vec, g * STEPS + 1, 1, g > 0)
                if g == 2 and self_kept is not None:
                    vec.wait_ge(self_kept, KD * len(batches))
                if g >= 2:
                    self.add(vec, g - 2)
                with vec.Fori(1, STEPS // 2) as i:
                    self.onehots(vec, i * 2 + g * STEPS, 0, True)
                    self.onehots(vec, i * 2 + g * STEPS + 1, 1, True)

            def build(self, pe, step, u, wait):
                pe.wait_ge(self.s_oh, 2 * step + 2)
                if wait:
                    pe.wait_ge(self.s_at, 2 * step - 2)
                for b in range(BPS):
                    last = pe_.matmul(self.build_ps[:, u, b // QUAD, (b % QUAD) * ZP:(b % QUAD + 1) * ZP],
                                      self.soh[:, u, b, :], self.zoh[:, u, b, :], start=True, stop=True)
                last.then_inc(self.s_built, 1)

            def sums(self, g, t, start, stop):
                for k in range(KD):
                    for part in range(2):
                        last = pe_.matmul(
                            self.h_ps[:, g % 2, k, 0:GN],
                            xhl[:, bass.ds(t, 1), part, k * P:(k + 1) * P].rearrange("p a b -> p (a b)"),
                            self.at[:, g % 2, bass.ds(t, 1), :].rearrange("p a b -> p (a b)"),
                            start=start and part == 0, stop=stop and part == 1, skip_group_check=True)
                return last

            def pair(self, pe, g, i, first, final, split_ready=None, between=None):
                for u in range(2):
                    if g < GROUPS:
                        self.build(pe, g * STEPS + 2 * i + u, u, not (g == 0 and first))
                    if g >= 1:
                        if u == 0:
                            if first:
                                pe.wait_ge(self.s_at, 2 * STEPS * g)
                            if first and g >= 3:
                                pe.wait_ge(self.s_h, KD * (g - 2))
                            if g == 1 and split_ready is not None:
                                pe.wait_ge(split_ready, i + 1)
                        for j in range(3 * u, 3 + 2 * u):
                            last = self.sums(g - 1, i * TPP + j, first and j == 0, final and j == TPP - 1)
                    if between is not None:
                        between(2 * i + u)
                if g >= 1 and final:
                    last.then_inc(self.s_ax, 1)

            def tensor_group(self, pe, g, split_ready=None):
                self.pair(pe, g, 0, True, False, split_ready)
                with pe.Fori(1, STEPS // 2 - 1) as i:
                    self.pair(pe, g, i, False, False, split_ready)
                self.pair(pe, g, STEPS // 2 - 1, False, True, split_ready)

            def keep(self, act, g, i, u):
                act.wait_ge(self.s_built, g * STEPS + 2 * i + u + 1)
                for q in range(2):
                    to = self.at[:, g % 2, :, bass.ds((2 * i + u) * BPS * W + q * QUAD * W, QUAD * W)]
                    fr = self.build_ps[:, u, q, 0:QUAD * ZP].rearrange("p (b z) -> p b z", z=ZP)[:, :, 0:Z]
                    act_.activation(to.rearrange("p t (b r) -> p b t r", r=W),
                                    fr.rearrange("p b (t r) -> p b t r", r=W), ACT.Copy).then_inc(self.s_at, 1)

            def scalar_group(self, act, g):
                if g >= 2:
                    act.wait_ge(self.s_ax, g - 1)
                with act.Fori(0, STEPS // 2) as i:
                    self.keep(act, g, i, 0)
                    self.keep(act, g, i, 1)

        with ExitStack() as ctx:
            headi = sb("headi", [EPART, 1], I32, ctx)
            head = sb("head", [EPART, 1], F32, ctx)
            heads_below = sb("heads_below", [EPART, BC * P], F16, ctx)
            thrc = sb("thrc", [P, BC], F32, ctx)
            line = sb("line", [P, BC], F32, ctx)
            linei = sb("linei", [P, BC], I32, ctx)
            lines = sb("lines", [P, BC, EK], I32, ctx)
            junk = sb("junk", [P, EK], F16, ctx)
            below = sb("below", [P, BC], F32, ctx)
            start = sb("start", [P, BC], F32, ctx)
            foundp = sb("foundp", [P, 1], F32, ctx)
            stats = sb("stats", [P, T, 6], F32, ctx)
            mv = sb("mv", [P, T, 2], F32, ctx)
            var = sb("var", [P, T], F32, ctx)
            root = sb("root", [P, T], F32, ctx)
            rstd = sb("rstd", [P, T], F32, ctx)
            tmp = sb("tmp", [P, T], F32, ctx)
            one = Pass("", ctx)
            counts_ps = one.h_ps[:, 0, 1, 256:512]
            turned_ps = one.h_ps[:].rearrange("p i k n -> p i (k n)")
            selfT = one.h_ps[:, 1]

            s_heads = sem("heads_in", ctx)
            s_x = [sem(f"x_in{g}", ctx) for g in range(XG)]
            s_eps = sem("eps_in", ctx)
            s_w = sem("weights_in", ctx)
            s_tail = sem("tail_zeroed", ctx)
            s_const = sem("constants_made", ctx)
            s_hb = sem("heads_compared", ctx)
            s_hc = sem("heads_counted", ctx)
            s_line = sem("lines_known", ctx)
            s_lines = [sem(f"lines_gathered{c}", ctx) for c in range(BC)]
            s_late = sem("later_constants_made", ctx)
            s_cnt = sem("below_counted", ctx)
            s_idx = sem("rows_known", ctx)
            s_rows = [sem(f"rows_gathered{c}", ctx) for c in range(BC)]
            s_rowsf = sem("rows_as_float", ctx)
            s_turned = sem("rows_turned", ctx)
            s_turnedk = sem("turned_rows_kept", ctx)
            s_found = sem("found_per_partition", ctx)
            s_sum = sem("found_summed", ctx)
            s_totalled = sem("total_kept", ctx)
            s_stats = sem("stats_done", ctx)
            s_dve = sem("vector_chain", ctx)
            s_var = sem("var_ready", ctx)
            s_root = sem("root_ready", ctx)
            s_xs = sem("xs_ready", ctx)
            s_hi = sem("hi_ready", ctx)
            s_lo = sem("lo_ready", ctx)
            s_selfw = sem("self_weight_ready", ctx)
            s_selfT = sem("self_turned", ctx)
            s_self = sem("self_kept", ctx)
            s_pool = sem("pool_chain", ctx)
            s_split = sem("weights_high_ready", ctx)

            block = ctx.enter_context(nc.Block())

            EARLY = 2

            def self_of(step):
                i = step - (STEPS - len(batches))
                return i if i >= 0 else None

            @block.sync
            def _(sp):
                sp.dma_start(headi[:], dst.rearrange("(p k) -> p k", k=EK)[:, 0:1], allow_slow_non_contiguous=True)\
                  .then_inc(s_heads, 16)
                xv = x[0:(T - 1) * P, :].rearrange("(t p) d -> p t d", p=P)
                for g in range(XG):
                    a, b = g * XT, min((g + 1) * XT, T - 1)
                    if g >= 2:
                        sp.wait_ge(s_lines[(g - 2) * 2], 16)
                    sp.dma_start(xt[:, a:b, :], xv[:, a:b, :]).then_inc(s_x[g], 16)
                sp.wait_ge(s_tail, 1)
                sp.dma_start(xt[0:LAST, T - 1, :], x[(T - 1) * P:N, :]).then_inc(s_x[XG - 1], 16)
                sp.dma_start(epsT[:], eps.rearrange("(a b) -> a b", a=1).broadcast_to([P, 1])).then_inc(s_eps, 16)
                for sbuf, dram in (
                    (w1[:], gw1.rearrange("(k p) h -> p k h", p=P)),
                    (w2[:], gw2.rearrange("(k p) h -> p k h", p=P)),
                    (b1[:], gb1.rearrange("(k p) -> p k", p=P)),
                    (b2[:], gb2.rearrange("(k p) -> p k", p=P)),
                    (gam[:], gamma.rearrange("(k p) -> p k", p=P)),
                    (bet[:], beta.rearrange("(k p) -> p k", p=P)),
                    (rbT[:], rb.rearrange("(e a) -> e a", a=1)),
                    (rwT[:, 0, :], rw[:, 0:P].rearrange("e p -> p e")),
                    (rwT[:, 1, :], rw[:, P:D].rearrange("e p -> p e")),
                ):
                    sp.dma_start(sbuf, dram, allow_slow_non_contiguous=True).then_inc(s_w, 16)
                sp.wait_ge(s_w, 16 * 9)

            @block.gpsimd
            def _(pool):
                link = chained(pool, s_pool)
                pool_.iota(thr[:], [[W, BC * P]], base=0, channel_multiplier=0,
                           allow_small_or_imprecise_dtypes=True).then_inc(s_const, 1)
                pool_.memset(ones16[:], 1.0).then_inc(s_const, 1)
                pool_.memset(xt[:, T - 1, :], 0.0).then_inc(s_tail, 1)
                pool_.iota(thrc[:], [[W * P, BC]], base=0, channel_multiplier=W,
                           allow_small_or_imprecise_dtypes=True).then_inc(s_const, 1)
                pool.wait_ge(s_line, 1)
                dl = dst.rearrange("(p k) -> p k", k=EK)
                for c in range(BC):
                    pool_.indirect_dma_start(
                        lines[:, c, :], None, dl, bass.IndirectOffsetOnAxis(ap=linei[:, c:c + 1], axis=0)
                    ).then_inc(s_lines[c], 16)
                pool_.iota(iota16[:], [[1, P]], base=0, channel_multiplier=0,
                           allow_small_or_imprecise_dtypes=True).then_inc(s_late, 1)
                link(pool_.memset(ident[:], 0.0))
                pool_.affine_select(out=ident[:], in_=ident[:], compare_op=ALU.not_equal, fill=1.0, base=0,
                                    pattern=[[-1, P]], channel_multiplier=1).then_inc(s_late, 1)
                pool_.memset(ones32[:], 1.0).then_inc(s_late, 1)
                for c in range(BC):
                    pool.wait_ge(s_idx, c + 1)
                    gather_row(pool, c, s_rows[c])
                for i in range(XG):
                    pool.wait_ge(s_hi, i + 1)
                    t, n = i * XT, XT
                    pool_.tensor_tensor(xhl[:, t:t + n, 1, :], xs[:, t:t + n, 0:D], xhl[:, t:t + n, 0, :],
                                        ALU.subtract).then_inc(s_lo, 1)

            @block.tensor
            def _(pe):
                pe.wait_ge(s_hb, 1)
                pe.wait_ge(s_const, 3)
                for c in range(BC):
                    last = pe_.matmul(counts_ps[:, c:c + 1], heads_below[:, c * P:(c + 1) * P],
                                      ones16[0:EPART, 0:1], start=True, stop=True)
                last.then_inc(s_hc, 1)
                pe.wait_ge(s_late, 3)
                for c in range(BC):
                    pe.wait_ge(s_rowsf, c + 1)
                    turn_row(c, turned_ps).then_inc(s_turned, 1)
                one.tensor_group(pe, 0)
                pe.wait_ge(s_turnedk, 2 * BC)

                def between(step):
                    if self_of(step) is not None:
                        turn_self(pe, self_of(step), selfT, s_selfT, s_self, s_xs)

                for i in range(STEPS // 2):
                    one.pair(pe, 1, i, i == 0, i == STEPS // 2 - 1, s_lo, between)
                pe.wait_ge(s_self, KD * len(batches))
                for g in range(2, GROUPS):
                    one.tensor_group(pe, g)
                pe.wait_ge(s_found, 1)
                pe.wait_ge(one.s_at, 2 * STEPS * GROUPS)
                pe_.matmul(one.build_ps[0:1, 0, 0, 0:1], foundp[:], ones32[:], start=True, stop=True)\
                   .then_inc(s_sum, 1)
                one.tensor_group(pe, GROUPS)

            @block.scalar
            def _(act):
                def keep_row(c):
                    act.wait_ge(s_rows[c], 32)
                    act_.activation(rowsf[:, c], rows[:, c], ACT.Copy).then_inc(s_rowsf, 1)
                    act.wait_ge(s_turned, c + 1)
                    s = slice(c * P, (c + 1) * P)
                    act_.activation(dstT[:, s], turned_ps[:, 0, s], ACT.Copy).then_inc(s_turnedk, 1)
                    act_.activation(srcT[:, s], turned_ps[:, 1, s], ACT.Copy).then_inc(s_turnedk, 1)

                def split(g):
                    act.wait_ge(s_xs, (g + 1) * XT)
                    act_.activation(xhl[:, g * XT:(g + 1) * XT, 0, :], xs[:, g * XT:(g + 1) * XT, 0:D],
                                    ACT.Copy).then_inc(s_hi, 1)

                keep_row(0)
                act.wait_ge(s_var, 1)
                act_.activation(root[:], var[:], ACT.Sqrt).then_inc(s_root, 1)
                keep_row(1)
                for g in range(EARLY):
                    split(g)
                for c in range(2, BC):
                    keep_row(c)
                one.scalar_group(act, 0)
                act.wait_ge(s_selfw, 1)
                for step in range(STEPS):
                    one.keep(act, 1, step // 2, step % 2)
                    if step % 2 == 1 and step // 2 + EARLY < XG:
                        split(step // 2 + EARLY)
                    if self_of(step) is not None:
                        keep_self(act, self_of(step), selfT, s_selfT, s_self)
                for g in range(2, GROUPS):
                    one.scalar_group(act, g)

            @block.vector
            def _(vec):
                link = chained(vec, s_dve)

                def split_weights(j):
                    if j == 0:
                        vec.wait_ge(s_w, 16 * 9)
                    i, what = divmod(j, 3)
                    w, ws, n = ((w1, w1s, KD * H), (w2, w2s, KH * D))[i]
                    w, hi, lo = (v.rearrange("p a b -> p (a b)") for v in (w[:], ws[:, 0], ws[:, 1]))
                    if what == 0:
                        dve.tensor_scalar(hi, w, WSCALE, None, ALU.mult).then_inc(s_split, 1)
                    elif what == 1:
                        vec.wait_ge(s_split, i + 1)
                        dve.scalar_tensor_tensor(out=lo, in0=w, scalar=WSCALE, in1=hi, op0=ALU.mult,
                                                 op1=ALU.subtract)
                    else:
                        for h in range(2):
                            dve.bn_stats(wst[:, 2 * i + h, :], w[:, h * (n // 2):(h + 1) * (n // 2)])

                def group_stats(g):
                    vec.wait_ge(s_x[g], 16 if g < XG - 1 else 32)
                    for t in range(g * XT, (g + 1) * XT):
                        dve.bn_stats(stats[:, t, :], xt[:, t, :]).then_inc(s_stats, 1)

                vec.wait_ge(s_heads, 16)
                link(dve.tensor_copy(head[:], headi[:]))
                vec.wait_ge(s_const, 3)
                dve.tensor_scalar(heads_below[:], thr[0:EPART, :], head[:], None, ALU.is_gt).then_inc(s_hb, 1)
                vec.wait_ge(s_hc, 1)
                link(dve.tensor_scalar(line[:], counts_ps[:, 0:BC], -1.0, 0.0, ALU.add, ALU.max))
                dve.tensor_copy(linei[:], line[:]).then_inc(s_line, 1)
                group_stats(0)
                for c in range(BC):
                    vec.wait_ge(s_lines[c], 16)
                    dve.tensor_scalar(junk[:], lines[:, c, :], thrc[:, c:c + 1], 0.0, ALU.is_lt, ALU.add,
                                      accum_out=below[:, c:c + 1]).then_inc(s_cnt, 1)
                    vec.wait_ge(s_cnt, c + 1)
                    link(dve.scalar_tensor_tensor(out=start[:, c:c + 1], in0=line[:, c:c + 1], scalar=float(EK),
                                                  in1=below[:, c:c + 1], op0=ALU.mult, op1=ALU.add))
                    dve.tensor_scalar(idx[:, c:c + 1], start[:, c:c + 1], float(E - P), None, ALU.min)\
                       .then_inc(s_idx, 1)
                for g in range(1, XG):
                    group_stats(g)
                vec.wait_ge(s_stats, T)
                for t in range(T):
                    last = dve.bn_aggr(mv[:, t, :], stats[:, t, :])
                link(last)
                dve.tensor_scalar(var[:], mv[:, :, 1], LN_EPS, None, ALU.add).then_inc(s_var, 1)
                vec.wait_ge(s_eps, 16)
                dve.tensor_scalar(selfw[:], epsT[:], 1.0, 1.0 / XSCALE, ALU.add, ALU.mult).then_inc(s_selfw, 1)
                vec.wait_ge(s_root, 1)
                rsqrt(link, dve, rstd[:], root[:], var[:], tmp[:])
                link(dve.tensor_scalar(rstd[:], rstd[:], XSCALE, None, ALU.mult))

                def layernorm(a, b):
                    for t in range(a, b):
                        dve.tensor_scalar(xs[:, t, 0:D], xt[:, t, :], mv[:, t, 0:1], rstd[:, t:t + 1],
                                          ALU.subtract, ALU.mult).then_inc(s_xs, 1)

                layernorm(0, EARLY * XT)
                vec.wait_ge(s_turnedk, 2)
                unpack_rows(link, 0, 1)
                vec.wait_ge(s_late, 3)
                one.vector_group(vec, 0)
                done = EARLY
                unpacked = 1
                for i in range(STEPS // 2):
                    for u in range(2):
                        step = STEPS + 2 * i + u
                        if (step + 1) * BPS > unpacked * P:
                            unpacked += 1
                            vec.wait_ge(s_turnedk, 2 * unpacked)
                            unpack_rows(link, unpacked - 1, unpacked)
                        one.onehots(vec, step, u, True)
                    if done < XG:
                        layernorm(done * XT, (done + 1) * XT)
                        done += 1
                vec.wait_ge(s_turnedk, 2 * BC)
                unpack_rows(link, unpacked, BC)
                dve.tensor_reduce(foundp[:], found[:], AX.X, ALU.add).then_inc(s_found, 1)
                for g in range(2, GROUPS):
                    one.vector_group(vec, g, s_self)
                    split_weights(g - 2)
                vec.wait_ge(s_sum, 1)
                dve.tensor_copy(total[:], one.build_ps[0:1, 0, 0, 0:1]).then_inc(s_totalled, 1)
                one.add(vec, GROUPS - 2)
                one.add(vec, GROUPS - 1)

        wanted = sb("wanted", [P, 1], F32, agg)
        skipped = sb("skipped", [P, 1], F32, agg)
        counted = sb("counted", [P, 1], F32, agg)
        edge_id = sb("edge_id", [P, 1], F32, agg)
        everything = nc.values_load(total[0:1, 0:1], min_val=0, max_val=E)
        with nc.If(everything != E):
            nc.all_engine_barrier()
            with ExitStack() as ctx:
                selfT = psum("selfT_again", [P, KD, 512], F32, ctx)
                s_selfT = sem("self_turned_again", ctx)
                s_self = sem("self_kept_again", ctx)
                block = ctx.enter_context(nc.Block())

                @block.tensor
                def _(pe):
                    for i in range(len(batches)):
                        turn_self(pe, i, selfT, s_selfT, s_self)

                @block.scalar
                def _(act):
                    for i in range(len(batches)):
                        keep_self(act, i, selfT, s_selfT, s_self)

                @block.vector
                def _(vec):
                    dve.memset(wanted[:], 0.0)
                    dve.memset(idx[:], 0)
                    dve.memset(counted[:], 1.0)

                @block.gpsimd
                def _(pool):
                    pool_.iota(edge_id[:], [[0, 1]], base=0, channel_multiplier=1,
                               allow_small_or_imprecise_dtypes=True)

            s_rows = nc.alloc_semaphore("rows_gathered_g")
            with nc.Fori(0, ceil_div(E, P)) as i:
                with ExitStack() as ctx:
                    turned_ps = psum("turned_ps_g", [P, 2, 1024], F32, ctx)
                    s_rowsf = nc.alloc_semaphore("rows_as_float_g")
                    s_turned = nc.alloc_semaphore("rows_turned_g")
                    s_dve = nc.alloc_semaphore("vector_chain_g")
                    with nc.Block() as block:

                        @block.gpsimd
                        def _(pool):
                            for c in range(BC):
                                gather_row(pool, c, s_rows)
                            pool.wait_ge(s_rows, (i + 1) * 32 * BC)

                        @block.tensor
                        def _(pe):
                            pe.wait_ge(s_rowsf, 1)
                            for c in range(BC):
                                last = turn_row(c, turned_ps)
                            last.then_inc(s_turned, 1)

                        @block.vector
                        def _(vec):
                            link = chained(vec, s_dve)
                            vec.wait_ge(s_rows, (i + 1) * 32 * BC)
                            dve.tensor_copy(rowsf[:], rows[:]).then_inc(s_rowsf, 1)
                            vec.wait_ge(s_turned, 1)
                            link(dve.tensor_copy(dstT[:], turned_ps[:, 0, 0:BC * P]))
                            link(dve.tensor_copy(srcT[:], turned_ps[:, 1, 0:BC * P]))
                            unpack_rows(link, 0, BC, counted[:])
                            link(dve.tensor_scalar(wanted[:], wanted[:], float(P), None, ALU.add))
                            link(dve.tensor_scalar(idx[:], wanted[:].broadcast_to([P, BC]), float(E - P), None,
                                                   ALU.min))
                            link(dve.tensor_scalar(skipped[:], wanted[:], float(E - P), 0.0, ALU.subtract, ALU.max))
                            link(dve.tensor_tensor(counted[:], edge_id[:], skipped[:], ALU.is_ge))

                    for s in (s_rowsf, s_turned, s_dve):
                        nc.all_engine_barrier(sems_to_clear=s)
                with ExitStack() as ctx:
                    again = Pass("_g", ctx)
                    with nc.Block() as block:

                        @block.vector
                        def _(vec):
                            for g in range(GROUPS):
                                again.vector_group(vec, g)
                            again.add(vec, GROUPS - 2)
                            again.add(vec, GROUPS - 1)

                        @block.tensor
                        def _(pe):
                            for g in range(GROUPS + 1):
                                again.tensor_group(pe, g)

                        @block.scalar
                        def _(act):
                            for g in range(GROUPS):
                                again.scalar_group(act, g)

                    for s in again.sems:
                        nc.all_engine_barrier(sems_to_clear=s)
        agg.close()

        yT = sb("yT", [P, KD, NP], F32)
        bstats = sb("bstats", [P, KD, GROUPS, 6], F32)
        EWC = KD * EH + D + 2
        ew = sb("ew", [P, NE, EWC], F32)
        C1, C2 = KD * EH, KD * EH + D
        with ExitStack() as ctx:
            hs = sb("hs", [P, 2, 2, KD, GN], F16, ctx)
            hid = sb("hid", [P, 2, KH, GN], F32, ctx)
            hids = sb("hids", [P, 2, 2, KH, GN], F16, ctx)
            hst = sb("hst", [P, GROUPS * KD, 6], F32, ctx)
            hidsum = sb("hidsum", [P, GROUPS * KH], F32, ctx)
            squares = sb("squares", [P, GROUPS * KD + 4, 2], F32, ctx)
            breaks = sb("breaks", [P, GROUPS * KH], F32, ctx)
            broken = sb("broken", [P, 5], F32, ctx)
            brokenp = sb("brokenp", [P, 1], F32, ctx)
            up_ps = psum("up_ps", [P, KH, 512], F32, ctx)
            down_ps = psum("down_ps", [P, 2, KD, 512], F32, ctx)
            s_hhi = sem("h_high_ready", ctx)
            s_hlo = sem("h_low_ready", ctx)
            s_up = sem("up_done", ctx)
            s_relu = sem("relu_done", ctx)
            s_hidhi = sem("hid_high_ready", ctx)
            s_hidlo = sem("hid_low_ready", ctx)
            s_down = sem("down_done", ctx)
            s_kept = sem("down_kept", ctx)
            s_stat = sem("statistics_done", ctx)
            s_dve = sem("mlp_chain", ctx)
            s_broken = sem("breaks_counted", ctx)
            s_over = sem("breaks_summed", ctx)
            s_ew0 = sem("expert_padding_zeroed", ctx)
            s_ew = sem("expert_weights_in", ctx)
            zeros = sb("zeros", [P, D], F32, ctx)
            nobody = sb("nobody", [P, CHUNKS], I32, ctx)
            s_zeros = sem("zeros_made", ctx)
            s_zeroed = sem("pages_zeroed", ctx)
            block = ctx.enter_context(nc.Block())

            @block.gpsimd
            def _(pool):
                pool_.iota(nobody[:].rearrange("p (r i) -> p r i", i=SLOTS), [[0, CHUNKS // SLOTS], [P, SLOTS]], base=N,
                           channel_multiplier=1).then_inc(s_zeros, 1)
                pool_.memset(zeros[:], 0.0).then_inc(s_zeros, 1)
                pool.wait_ge(s_zeros, 2)
                pool_.memset(ew[EH:P, :, C1:EWC], 0.0).then_inc(s_ew0, 1)
                pool.wait_ge(s_ew0, 1)
                pool_.memset(ew[0:EH, :, C2:EWC], 0.0).then_inc(s_ew0, 1)

            @block.sync
            def _(sp):
                sp.dma_start(ew[:, :, 0:C1], ew1.rearrange("e (p k) h -> p e (k h)", k=KD)).then_inc(s_ew, 16)
                sp.dma_start(ew[0:EH, :, C1:C2], ew2.rearrange("e h d -> h e d")).then_inc(s_ew, 16)
                sp.wait_ge(s_ew0, 2)
                sp.dma_start(ew[EH:EH + 1, :, C1:C2], eb2.rearrange("(a e) d -> a e d", a=1)).then_inc(s_ew, 16)
                sp.dma_start(ew[0:EH, :, C2], eb1.rearrange("e h -> h e"), allow_slow_non_contiguous=True)\
                  .then_inc(s_ew, 16)
                sp.wait_ge(s_zeros, 2)
                pages_of = by_expert.rearrange("(c p) d -> p c d", p=P)
                sp.dma_start(pages_of[:, :, 0:D], zeros[:].unsqueeze(1).broadcast_to([P, CHUNKS, D]))\
                  .then_inc(s_zeroed, 16)
                sp.dma_start(pages_of[:, :, D], nobody[:].bitcast(F32), allow_slow_non_contiguous=True).then_inc(s_zeroed, 16)
                sp.dma_start(out[N:N + SPARE_ROWS, :].rearrange("(c p) d -> p c d", p=P),
                             zeros[:].unsqueeze(1).broadcast_to([P, SLOTS, D])).then_inc(s_zeroed, 16)
                sp.wait_ge(s_ew, 64)
                sp.wait_ge(s_zeroed, 48)

            PRODUCTS = ((0, 0), (0, 1), (1, 0))

            @block.tensor
            def _(pe):
                def up(g, u, wait):
                    pe.wait_ge(s_hlo, g + 1)
                    for m in range(KH):
                        if wait:
                            pe.wait_ge(s_relu, (g - 1) * KH + m + 1)
                        for k in range(KD):
                            for i, (a, b) in enumerate(PRODUCTS):
                                last = pe_.matmul(up_ps[:, m, 0:GN], w1s[:, a, k, m * P:(m + 1) * P],
                                                  hs[:, u, b, k, :], start=(k == 0 and i == 0),
                                                  stop=(k == KD - 1 and i == 2))
                        last.then_inc(s_up, 1)

                def down(g, u, wait):
                    if wait:
                        pe.wait_ge(s_kept, (g - 1) * KD)
                    for f in range(KD):
                        for m in range(KH):
                            if f == 0:
                                pe.wait_ge(s_hidlo, g * KH + m + 1)
                            for i, (a, b) in enumerate(PRODUCTS):
                                last = pe_.matmul(down_ps[:, u, f, 0:GN], w2s[:, a, m, f * P:(f + 1) * P],
                                                  hids[:, u, b, m, :], start=(m == 0 and i == 0),
                                                  stop=(m == KH - 1 and i == 2))
                        last.then_inc(s_down, 1)

                up(0, 0, False)
                up(1, 1, True)
                down(0, 0, False)
                up(2, 0, True)
                down(1, 1, False)
                with pe.Fori(1, GROUPS // 2 - 1) as i:
                    up(i * 2 + 1, 1, True)
                    down(i * 2, 0, True)
                    up(i * 2 + 2, 0, True)
                    down(i * 2 + 1, 1, True)
                up(GROUPS - 1, 1, True)
                down(GROUPS - 2, 0, True)
                pe.wait_ge(s_broken, 1)
                pe_.matmul(up_ps[0:1, 0, 0:1], brokenp[:], ones32[:], start=True, stop=True).then_inc(s_over, 1)
                down(GROUPS - 1, 1, True)

            @block.scalar
            def _(act):
                def high(g, u, wait):
                    if wait:
                        act.wait_ge(s_up, (g - 1) * KH)
                    act_.activation(hs[:, u, 0], hT[:, :, bass.ds(g * GN, GN)], ACT.Copy,
                                    scale=HSCALE).then_inc(s_hhi, 1)

                def relu(g, u, wait):
                    if wait:
                        act.wait_ge(s_hidlo, (g - 1) * KH)
                        act.wait_ge(s_down, (g - 1) * KD)

                    def high_part(m):
                        act.wait_ge(s_relu, g * KH + m + 1)
                        act_.activation(hids[:, u, 0, m, :], hid[:, u, m, :], ACT.Copy,
                                        scale=HSCALE).then_inc(s_hidhi, 1)

                    for m in range(KH):
                        act.wait_ge(s_up, g * KH + m + 1)
                        act_.activation(hid[:, u, m, :], up_ps[:, m, 0:GN], ACT.Relu, bias=b1[:, m:m + 1],
                                        scale=1.0 / (WSCALE * HSCALE),
                                        accum_out=hidsum[:, bass.ds(g * KH + m, 1)]).then_inc(s_relu, 1)
                        if m >= 1:
                            high_part(m - 1)
                    high_part(KH - 1)

                high(0, 0, False)
                high(1, 1, False)
                relu(0, 0, False)
                high(2, 0, True)
                relu(1, 1, False)
                high(3, 1, True)
                with act.Fori(1, GROUPS // 2 - 1) as i:
                    relu(i * 2, 0, True)
                    high(i * 2 + 2, 0, True)
                    relu(i * 2 + 1, 1, True)
                    high(i * 2 + 3, 1, True)
                relu(GROUPS - 2, 0, True)
                relu(GROUPS - 1, 1, True)

            @block.vector
            def _(vec):
                link = chained(vec, s_dve)

                def low(g, u):
                    vec.wait_ge(s_hhi, g + 1)
                    dve.scalar_tensor_tensor(out=hs[:, u, 1], in0=hT[:, :, bass.ds(g * GN, GN)], scalar=HSCALE,
                                             in1=hs[:, u, 0], op0=ALU.mult, op1=ALU.subtract).then_inc(s_hlo, 1)
                    for k in range(KD):
                        dve.bn_stats(hst[:, bass.ds(g * KD + k, 1), :].rearrange("p a b -> p (a b)"),
                                     hT[:, k, bass.ds(g * GN, GN)]).then_inc(s_stat, 1)

                def low_hid(g, u):
                    for m in range(KH):
                        vec.wait_ge(s_hidhi, g * KH + m + 1)
                        dve.scalar_tensor_tensor(out=hids[:, u, 1, m, :], in0=hid[:, u, m, :], scalar=HSCALE,
                                                 in1=hids[:, u, 0, m, :], op0=ALU.mult,
                                                 op1=ALU.subtract).then_inc(s_hidlo, 1)

                def keep(g, u, n):
                    for f in range(KD):
                        vec.wait_ge(s_down, g * KD + f + 1)
                        dve.tensor_scalar(yT[:, f, bass.ds(g * GN, GN)], down_ps[:, u, f, 0:GN],
                                          1.0 / (WSCALE * HSCALE), b2[:, f:f + 1], ALU.mult,
                                          ALU.add).then_inc(s_kept, 1)
                    for f in range(KD):
                        vec.wait_ge(s_kept, g * KD + f + 1)
                        dve.bn_stats(bstats[:, f, bass.ds(g, 1), :].rearrange("p a b -> p (a b)"),
                                     yT[:, f, bass.ds(g * GN, n)]).then_inc(s_stat, 1)

                def check_bounds():
                    NH = GROUPS * KD
                    vec.wait_ge(s_relu, GROUPS * KH)
                    vec.wait_ge(s_stat, KD * (2 * GROUPS - 2))
                    both = hst[:].rearrange("p a (h s) -> p a h s", s=3)
                    bothw = wst[:].rearrange("p a (h s) -> p a h s", s=3)
                    link(dve.tensor_tensor(squares[:, 0:NH, :], both[:, :, :, 1], both[:, :, :, 1], ALU.mult))
                    link(dve.tensor_tensor(squares[:, NH:NH + 4, :], bothw[:, :, :, 1], bothw[:, :, :, 1],
                                           ALU.mult))
                    for i, (v, bound, n) in enumerate((
                        (squares[:, 0:NH, :], H_BOUND ** 2, (NH, 2)),
                        (both[:, :, :, 2], H_BOUND ** 2, (NH, 2)),
                        (squares[:, NH:NH + 4, :], W_BOUND ** 2, (4, 2)),
                        (bothw[:, :, :, 2], W_BOUND ** 2, (4, 2)),
                        (hidsum[:], 2 * H_BOUND, (GROUPS * KH,)),
                    )):
                        to = breaks[:, 0:n[0] * (n[1] if len(n) > 1 else 1)]
                        if len(n) > 1:
                            to = to.rearrange("p (a b) -> p a b", b=n[1])
                        link(dve.tensor_scalar(to, v, bound, 0.0, ALU.is_ge, ALU.add,
                                               accum_out=broken[:, i:i + 1]))
                    dve.tensor_reduce(brokenp[:], broken[:], AX.X, ALU.add).then_inc(s_broken, 1)

                low(0, 0)
                low(1, 1)
                low_hid(0, 0)
                low(2, 0)
                low_hid(1, 1)
                keep(0, 0, GN)
                low(3, 1)
                with vec.Fori(1, GROUPS // 2 - 1) as i:
                    low_hid(i * 2, 0)
                    keep(i * 2 - 1, 1, GN)
                    low(i * 2 + 2, 0)
                    low_hid(i * 2 + 1, 1)
                    keep(i * 2, 0, GN)
                    low(i * 2 + 3, 1)
                low_hid(GROUPS - 2, 0)
                keep(GROUPS - 3, 1, GN)
                low_hid(GROUPS - 1, 1)
                check_bounds()
                keep(GROUPS - 2, 0, GN)
                vec.wait_ge(s_over, 1)
                dve.tensor_copy(overflow[:], up_ps[0:1, 0, 0:1])
                keep(GROUPS - 1, 1, N - (GROUPS - 1) * GN)

        breaches = nc.values_load(overflow[0:1, 0:1], min_val=0, max_val=P * 5 * GROUPS * KH)
        with nc.If(breaches != 0):
            nc.all_engine_barrier()
            with ExitStack() as ctx:
                hid = sb("hid_f", [P, 2, KH, GN], F32, ctx)
                up_ps = psum("up_ps_f", [P, KH, 512], F32, ctx)
                down_ps = psum("down_ps_f", [P, 2, KD, 512], F32, ctx)
                s_up = sem("up_done_f", ctx)
                s_relu = sem("relu_done_f", ctx)
                s_down = sem("down_done_f", ctx)
                s_kept = sem("down_kept_f", ctx)
                s_stat = sem("bn_stats_done_f", ctx)
                block = ctx.enter_context(nc.Block())

                @block.tensor
                def _(pe):
                    def up(g, wait):
                        for m in range(KH):
                            if wait:
                                pe.wait_ge(s_relu, (g - 1) * KH + m + 1)
                            for k in range(KD):
                                last = pe_.matmul(up_ps[:, m, 0:GN], w1[:, k, m * P:(m + 1) * P],
                                                  hT[:, k, bass.ds(g * GN, GN)], start=(k == 0), stop=(k == KD - 1))
                            last.then_inc(s_up, 1)

                    def down(g, u, wait):
                        if wait:
                            pe.wait_ge(s_kept, (g - 1) * KD)
                        for f in range(KD):
                            for m in range(KH):
                                if f == 0:
                                    pe.wait_ge(s_relu, g * KH + m + 1)
                                last = pe_.matmul(down_ps[:, u, f, 0:GN], w2[:, m, f * P:(f + 1) * P],
                                                  hid[:, u, m, :], start=(m == 0), stop=(m == KH - 1))
                            last.then_inc(s_down, 1)

                    up(0, False)
                    up(1, True)
                    down(0, 0, False)
                    up(2, True)
                    down(1, 1, False)
                    with pe.Fori(1, GROUPS // 2 - 1) as i:
                        up(i * 2 + 1, True)
                        down(i * 2, 0, True)
                        up(i * 2 + 2, True)
                        down(i * 2 + 1, 1, True)
                    up(GROUPS - 1, True)
                    down(GROUPS - 2, 0, True)
                    down(GROUPS - 1, 1, True)

                @block.scalar
                def _(act):
                    def relu(g, u, wait):
                        if wait:
                            act.wait_ge(s_down, (g - 1) * KD)
                        for m in range(KH):
                            act.wait_ge(s_up, g * KH + m + 1)
                            act_.activation(hid[:, u, m, :], up_ps[:, m, 0:GN], ACT.Relu,
                                            bias=b1[:, m:m + 1]).then_inc(s_relu, 1)

                    relu(0, 0, False)
                    relu(1, 1, False)
                    with act.Fori(1, GROUPS // 2) as i:
                        relu(i * 2, 0, True)
                        relu(i * 2 + 1, 1, True)

                @block.vector
                def _(vec):
                    def keep(g, u, n):
                        for f in range(KD):
                            vec.wait_ge(s_down, g * KD + f + 1)
                            dve.tensor_scalar(yT[:, f, bass.ds(g * GN, GN)], down_ps[:, u, f, 0:GN], b2[:, f:f + 1],
                                              None, ALU.add).then_inc(s_kept, 1)
                        for f in range(KD):
                            vec.wait_ge(s_kept, g * KD + f + 1)
                            dve.bn_stats(bstats[:, f, bass.ds(g, 1), :].rearrange("p a b -> p (a b)"),
                                         yT[:, f, bass.ds(g * GN, n)]).then_inc(s_stat, 1)

                    with vec.Fori(0, GROUPS // 2 - 1) as i:
                        keep(i * 2, 0, GN)
                        keep(i * 2 + 1, 1, GN)
                    keep(GROUPS - 2, 0, GN)
                    keep(GROUPS - 1, 1, N - (GROUPS - 1) * GN)

        onehot = sb("onehot", [P, T, NE], F16)
        row = sb("row", [P, T], I32)
        expert = sb("expert", [1, CHUNKS], I32)
        LB = 5
        NB = T // LB
        BN_ = LB * P
        HB = BN_ // 2
        UNITS = ceil_div(LB, 2)

        def unit_tiles(u):
            b, j = divmod(u, UNITS)
            return b * LB + 2 * j, min(2, LB - 2 * j)

        with ExitStack() as ctx:
            mvB = sb("mvB", [P, KD, 2], F32, ctx)
            varB = sb("varB", [P, KD], F32, ctx)
            rootB = sb("rootB", [P, KD], F32, ctx)
            scaleB = sb("scaleB", [P, KD], F32, ctx)
            shiftB = sb("shiftB", [P, KD], F32, ctx)
            tmpB = sb("tmpB", [P, KD], F32, ctx)
            st2 = sb("st2", [P, T, 6], F32, ctx)
            mv2 = sb("mv2", [P, T, 2], F32, ctx)
            var2 = sb("var2", [P, T], F32, ctx)
            root2 = sb("root2", [P, T], F32, ctx)
            rstd2 = sb("rstd2", [P, T], F32, ctx)
            tmp2 = sb("tmp2", [P, T], F32, ctx)
            xT = sb("xT", [P, 2, KD, BN_], F32, ctx)
            lT = sb("lT", [NE, 2, BN_], F32, ctx)
            lmax = sb("lmax", [P, LB], F32, ctx)
            is_max = sb("is_max", [P, LB, NE], F32, ctx)
            lfirst = sb("lfirst", [P, LB], F32, ctx)
            down32 = sb("down32", [P, NE], F32, ctx)
            valid = sb("valid", [P, NE], F16, ctx)
            upper = sb("upper", [P, P], F16, ctx)
            before = sb("before", [P, T - LB + 1, NE], F16, ctx)
            picked = sb("picked", [P, 3, LB, NE], F32, ctx)
            per_token = sb("per_token", [P, 3, LB], F32, ctx)
            beyond = sb("beyond", [P, LB], F32, ctx)
            nmr2 = sb("nmr2", [P, T], F32, ctx)
            page_id = sb("page_id", [NE, CHUNKS], F32, ctx)
            first_new = sb("first_new", [NE, NB], F32, ctx)
            new_end = sb("new_end", [NE, NB], F32, ctx)
            from_first = sb("from_first", [NE, NB, CHUNKS], F32, ctx)
            to_end = sb("to_end", [NE, NB, CHUNKS], F32, ctx)
            owned = sb("owned", [NE, CHUNKS], F32, ctx)
            eid = sb("eid", [NE, 1], F32, ctx)
            full_at = sb("full_at", [NE, T + 1], F32, ctx)
            full = sb("full", [NE, T + 1], F32, ctx)
            pages = sb("pages", [NE, NB + 1], F32, ctx)
            new = sb("new", [NE, NB], F32, ctx)
            new_shift = sb("new_shift", [NE, NB], F32, ctx)
            moved = sb("moved", [NE, NB], F32, ctx)
            shifts = sb("shifts", [NE, NB + 1, 3], F32, ctx)
            shift_diag = sb("shift_diag", [NE, 3, NE], F16, ctx)
            upper32 = sb("upper32", [NE, NE], F32, ctx)
            ones_e = sb("ones_e", [NE, NE], F32, ctx)
            page_e = sb("page_e", [NE, P], F16, ctx)
            y_ps = psum("y_ps", [P, 2, 512], F32, ctx)
            x_ps = psum("x_ps", [P, 2, 512], F32, ctx)
            l_ps = psum("l_ps", [NE, 2, 512], F32, ctx)
            lt_ps = psum("lt_ps", [P, 512], F32, ctx)
            m_ps = psum("m_ps", [P, 512], F32, ctx)
            pick_ps = m_ps[:, 0:3 * LB * NE].rearrange("p (a t e) -> p a t e", a=3, e=NE)
            count_ps = m_ps[0:NE, 480:481]
            page_ps = m_ps[0:NE, 484:485]
            expert_ps = m_ps[0:1, 0:CHUNKS]
            total_ps = m_ps[0:1, 488:489]

            s_c = sem("router_constants", ctx)
            s_dve = sem("bn_chain", ctx)
            s_varB = sem("bn_var", ctx)
            s_rootB = sem("bn_root", ctx)
            s_scale = sem("bn_scale", ctx)
            s_bn = sem("bn_applied", ctx)
            s_bn0 = sem("bn_applied_by_vector", ctx)
            s_yT = sem("y_turned", ctx)
            s_x1 = sem("x1_ready", ctx)
            s_st2 = sem("stats2", ctx)
            s_mv2 = sem("mv2_ready", ctx)
            s_var2 = sem("var2_ready", ctx)
            s_root2 = sem("root2_ready", ctx)
            s_r2 = sem("rstd2_ready", ctx)
            s_xn = sem("xn2_ready", ctx)
            s_xT = sem("xn2_turned", ctx)
            s_xTk = sem("xn2_turned_kept", ctx)
            s_l = sem("logits_done", ctx)
            s_lk = sem("logits_kept", ctx)
            s_lT = sem("logits_turned", ctx)
            s_oh = sem("onehot_ready", ctx)
            s_bef = sem("before_ready", ctx)
            s_count = sem("tokens_counted", ctx)
            s_new = sem("new_pages_known", ctx)
            s_first = sem("first_new_page_done", ctx)
            s_shift = sem("shifts_ready", ctx)
            s_shiftb = sem("shifts_broadcast", ctx)
            s_owned = sem("owned_ready", ctx)
            s_exp = sem("experts_done", ctx)
            s_row = sem("rows_ready", ctx)
            s_disp = sem("dispatched", ctx)

            s_id = sem("token_numbers_set", ctx)
            s_sum1 = sem("x1_stored", ctx)
            block = ctx.enter_context(nc.Block())

            @block.sync
            def _(sp):
                for b in range(NB):
                    sp.wait_ge(s_x1, (b + 1) * UNITS)
                    t0, t1 = b * LB, min((b + 1) * LB, T - 1)
                    sp.dma_start(out[t0 * P:t1 * P, :].rearrange("(t p) d -> p t d", p=P), xt[:, t0:t1, :])\
                      .then_inc(s_sum1, 16)
                sp.dma_start(out[(T - 1) * P:N, :], xt[0:LAST, T - 1, :]).then_inc(s_sum1, 16)
                sp.wait_ge(s_sum1, 16 * (NB + 1))

            @block.gpsimd
            def _(pool):
                pool_.iota(xs[:, :, D:DW].bitcast(I32), [[P, T], [1, 1]], base=0, channel_multiplier=1)\
                     .then_inc(s_id, 1)
                pool.wait_ge(s_id, 1)
                for to, pattern, base, mult in (
                    (down32[:], [[-1, NE]], NE, 0),
                    (full_at[:], [[P, T + 1]], 0, 0),
                    (page_id[:], [[1, CHUNKS]], 0, 0),
                    (eid[:], [[0, 1]], 0, 1),
                ):
                    pool_.iota(to, pattern, base=base, channel_multiplier=mult,
                               allow_small_or_imprecise_dtypes=True).then_inc(s_c, 1)
                pool_.affine_select(out=valid[:], in_=ones16[:, 0:NE], compare_op=ALU.is_gt, fill=0.0, base=LAST,
                                    pattern=[[0, NE]], channel_multiplier=-1).then_inc(s_c, 1)
                pool_.affine_select(out=upper[:], in_=ones16[:], compare_op=ALU.is_gt, fill=0.0, base=0,
                                    pattern=[[1, P]], channel_multiplier=-1).then_inc(s_c, 1)
                pool_.memset(ones_e[:], 1.0).then_inc(s_c, 1)
                pool_.memset(pages[:, 0:1], 0.0).then_inc(s_c, 1)
                pool_.memset(shifts[:, 0, 0:1], 0.0).then_inc(s_c, 1)
                pool_.memset(page_e[:], float(P)).then_inc(s_c, 1)
                pool.wait_ge(s_c, 10)
                pool_.affine_select(out=upper32[:], in_=ones_e[:], compare_op=ALU.is_gt, fill=0.0,
                                    base=0, pattern=[[1, NE]], channel_multiplier=-1).then_inc(s_c, 1)
                pool_.memset(before[:, 0, :], 0.0).then_inc(s_bef, 1)

                def count(b):
                    pool.wait_ge(s_oh, b + 1)
                    for t in range(b * LB, (b + 1) * LB):
                        pool.wait_ge(s_bef, t + 1)
                        pool_.tensor_tensor(before[:, t + 1, :], before[:, t, :], onehot[:, t, :],
                                            ALU.add).then_inc(s_bef, 1)

                def dispatch(b):
                    pool.wait_ge(s_row, b + 1)
                    for t in range(b * LB, (b + 1) * LB):
                        n = P if t < T - 1 else LAST
                        pool_.indirect_dma_start(
                            by_expert, bass.IndirectOffsetOnAxis(ap=row[0:n, t:t + 1], axis=0),
                            xs[0:n, t, :], None).then_inc(s_disp, 16)

                for b in range(NB - 1):
                    count(b)
                    if b >= 1:
                        dispatch(b - 1)
                dispatch(NB - 2)
                dispatch(NB - 1)
                pool.wait_ge(s_disp, 16 * T)

            @block.tensor
            def _(pe):
                def turn_y(u):
                    t0, n = unit_tiles(u)
                    pe.wait_ge(s_bn, KD * (u // UNITS) + 1)
                    pe.wait_ge(s_bn0, 1)
                    if u >= 2:
                        pe.wait_ge(s_x1, u - 1)
                    for i in range(n):
                        for k in range(KD):
                            last = pe_.transpose(y_ps[:, u % 2, (i * KD + k) * P:(i * KD + k + 1) * P],
                                                 yT[:, k, (t0 + i) * P:(t0 + i + 1) * P], ident[:])
                    last.then_inc(s_yT, 1)

                def turn_x(u):
                    t0, n = unit_tiles(u)
                    pe.wait_ge(s_xn, t0 + n)
                    if u >= 2:
                        pe.wait_ge(s_xTk, u - 1)
                    for i in range(n):
                        for k in range(KD):
                            last = pe_.transpose(x_ps[:, u % 2, (i * KD + k) * P:(i * KD + k + 1) * P],
                                                 xs[:, t0 + i, k * P:(k + 1) * P], ident[:])
                    last.then_inc(s_xT, 1)

                def logits(b, i):
                    pe.wait_ge(s_xTk, b * UNITS + ceil_div((i + 1) * HB, 2 * P))
                    if b >= 1:
                        pe.wait_ge(s_lk, b)
                    for k in range(KD):
                        last = pe_.matmul(l_ps[:, i, 0:HB], rwT[:, k, :], xT[:, b % 2, k, i * HB:(i + 1) * HB],
                                          start=(k == 0), stop=(k == KD - 1))
                    if i == 1:
                        last.then_inc(s_l, 1)

                def turn_logits(b):
                    pe.wait_ge(s_lk, b + 1)
                    if b >= 1:
                        pe.wait_ge(s_oh, b)
                    for j in range(LB):
                        last = pe_.transpose(lt_ps[:, j * NE:(j + 1) * NE], lT[:, b % 2, j * P:(j + 1) * P],
                                             ident[0:NE, 0:NE])
                    last.then_inc(s_lT, 1)

                def count_tokens(b):
                    pe.wait_ge(s_oh, b + 1)
                    pe.wait_ge(s_bef, b * LB + 1)
                    if b >= 1:
                        pe.wait_ge(s_row, b)
                    pe_.matmul(count_ps, before[:, b * LB, :], ones16[:, 0:1], start=True, stop=False,
                               skip_group_check=True)
                    for t in range(b * LB, (b + 1) * LB):
                        last = pe_.matmul(count_ps, onehot[:, t, :], ones16[:, 0:1], start=False,
                                          stop=(t == (b + 1) * LB - 1), skip_group_check=True)
                    last.then_inc(s_count, 1)

                def first_new_page(b):
                    pe.wait_ge(s_new, b + 1)
                    pe_.matmul(page_ps, ones_e[:], pages[:, b:b + 1], start=True, stop=False, skip_group_check=True)
                    pe_.matmul(page_ps, upper32[:], new[:, b:b + 1], start=False, stop=True,
                               skip_group_check=True).then_inc(s_first, 1)

                def rank_and_shifts(b):
                    ts = slice(b * LB, (b + 1) * LB)
                    if b < NB - 1:
                        pe.wait_ge(s_bef, (b + 1) * LB)
                    pe.wait_ge(s_shift, b + 1)
                    pe_.matmul(pick_ps[:, 0], upper[:], onehot[:, ts, :], start=True, stop=False,
                               skip_group_check=True)
                    if b < NB - 1:
                        pe_.matmul(pick_ps[:, 0], ones16[:], before[:, ts, :], start=False, stop=False,
                                   skip_group_check=True)
                    else:
                        pe_.matmul(pick_ps[:, 0], ones16[:],
                                   before[:, b * LB, :].unsqueeze(1).broadcast_to([P, LB, NE]), start=False,
                                   stop=False, skip_group_check=True)
                        for j in range(LB - 1):
                            pe_.matmul(pick_ps[:, 0, j + 1:LB], ones16[:],
                                       onehot[:, b * LB + j, :].unsqueeze(1).broadcast_to([P, LB - 1 - j, NE]),
                                       start=False, stop=False, skip_group_check=True)
                    for i in range(3):
                        last = pe_.matmul(pick_ps[:, i], page_e[:],
                                          shift_diag[:, i, :].unsqueeze(1).broadcast_to([NE, LB, NE]),
                                          start=(i > 0), stop=True, skip_group_check=True)
                    last.then_inc(s_shiftb, 1)

                pe.wait_ge(s_c, 11)
                for u in range(UNITS):
                    turn_y(u)
                for b in range(NB):
                    ahead = range((b + 1) * UNITS, (b + 2) * UNITS) if b + 1 < NB else ()
                    for u in ahead[:-1]:
                        turn_y(u)
                    for u in range(b * UNITS, (b + 1) * UNITS):
                        turn_x(u)
                    if b >= 1:
                        count_tokens(b - 1)
                    for u in ahead[-1:]:
                        turn_y(u)
                    logits(b, 0)
                    if b == NB - 1:
                        first_new_page(b - 1)
                    logits(b, 1)
                    if b == NB - 1:
                        rank_and_shifts(b - 1)
                    turn_logits(b)
                    if 1 <= b < NB - 1:
                        first_new_page(b - 1)
                        rank_and_shifts(b - 1)
                count_tokens(NB - 1)
                first_new_page(NB - 1)
                rank_and_shifts(NB - 1)
                pe.wait_ge(s_row, NB)
                pe.wait_ge(s_owned, 1)
                pe_.matmul(total_ps, pages[:, NB:NB + 1], ones_e[:, 0:1], start=True, stop=True,
                           skip_group_check=True)
                pe_.matmul(expert_ps, eid[:], owned[:], start=True, stop=True, skip_group_check=True)\
                   .then_inc(s_exp, 1)

            @block.scalar
            def _(act):
                act.wait_ge(s_varB, 1)
                act_.activation(rootB[:], varB[:], ACT.Sqrt).then_inc(s_rootB, 1)
                act.wait_ge(s_scale, 1)

                def apply_bn(b):
                    for k in range(1 if b == 0 else KD):
                        cols = yT[:, k, b * BN_:(b + 1) * BN_]
                        act_.activation(cols, cols, ACT.Identity, bias=shiftB[:, k:k + 1],
                                        scale=scaleB[:, k:k + 1]).then_inc(s_bn, 1)

                def root(b):
                    act.wait_ge(s_var2, b + 1)
                    act_.activation(root2[:, b * LB:(b + 1) * LB], var2[:, b * LB:(b + 1) * LB],
                                    ACT.Sqrt).then_inc(s_root2, 1)

                def normalise(b):
                    act.wait_ge(s_r2, b + 1)
                    for t in range(b * LB, (b + 1) * LB):
                        act_.activation(xs[:, t, 0:D], xt[:, t, :], ACT.Identity, bias=nmr2[:, t:t + 1],
                                        scale=rstd2[:, t:t + 1]).then_inc(s_xn, 1)

                def keep_x(b):
                    for u in range(b * UNITS, (b + 1) * UNITS):
                        t0, n = unit_tiles(u)
                        act.wait_ge(s_xT, u + 1)
                        if b >= 2:
                            act.wait_ge(s_l, b - 1)
                        cols = xT[:, b % 2, :, (t0 - b * LB) * P:(t0 - b * LB + n) * P]
                        act_.activation(cols.rearrange("p k (i n) -> p i k n", n=P),
                                        x_ps[:, u % 2, 0:n * D].rearrange("p (i k n) -> p i k n", k=KD, n=P),
                                        ACT.Copy).then_inc(s_xTk, 1)

                def keep_logits(b):
                    act.wait_ge(s_l, b + 1)
                    if b >= 2:
                        act.wait_ge(s_lT, b - 1)
                    act_.activation(lT[:, b % 2, :].rearrange("p (i n) -> p i n", i=2), l_ps[:, :, 0:HB],
                                    ACT.Identity, bias=rbT[:]).then_inc(s_lk, 1)

                apply_bn(0)
                apply_bn(1)
                root(0)
                apply_bn(2)
                normalise(0)
                for b in range(NB):
                    keep_x(b)
                    if b + 3 < NB:
                        apply_bn(b + 3)
                    if b + 1 < NB:
                        root(b + 1)
                    keep_logits(b)
                    if b + 1 < NB:
                        normalise(b + 1)

            @block.vector
            def _(vec):
                link = chained(vec, s_dve)
                for k in range(KD):
                    last = dve.bn_aggr(mvB[:, k, :], bstats[:, k, :, :].rearrange("p g s -> p (g s)"))
                link(last)
                dve.tensor_scalar(varB[:], mvB[:, :, 1], BN_EPS, None, ALU.add).then_inc(s_varB, 1)
                vec.wait_ge(s_rootB, 1)
                rsqrt(link, dve, scaleB[:], rootB[:], varB[:], tmpB[:])
                link(dve.tensor_tensor(scaleB[:], scaleB[:], gam[:], ALU.mult))
                link(dve.tensor_tensor(tmpB[:], mvB[:, :, 0], scaleB[:], ALU.mult))
                dve.tensor_tensor(shiftB[:], bet[:], tmpB[:], ALU.subtract).then_inc(s_scale, 1)
                vec.wait_ge(s_scale, 1)
                cols = yT[:, 1, 0:BN_]
                dve.tensor_scalar(cols, cols, scaleB[:, 1:2], shiftB[:, 1:2], ALU.mult, ALU.add).then_inc(s_bn0, 1)

                def residual(b):
                    def stats_of(u):
                        t0, n = unit_tiles(u)
                        vec.wait_ge(s_x1, u + 1)
                        for t in range(t0, t0 + n):
                            dve.bn_stats(st2[:, t, :], xt[:, t, :]).then_inc(s_st2, 1)

                    for u in range(b * UNITS, (b + 1) * UNITS):
                        t0, n = unit_tiles(u)
                        vec.wait_ge(s_yT, u + 1)
                        dve.tensor_tensor(xt[:, t0:t0 + n, :], xt[:, t0:t0 + n, :],
                                          y_ps[:, u % 2, 0:n * D].rearrange("p (t d) -> p t d", d=D), ALU.add)\
                           .then_inc(s_x1, 1)
                        if u > b * UNITS:
                            stats_of(u - 1)
                    stats_of((b + 1) * UNITS - 1)
                    vec.wait_ge(s_st2, (b + 1) * LB)
                    for t in range(b * LB, (b + 1) * LB):
                        dve.bn_aggr(mv2[:, t, :], st2[:, t, :]).then_inc(s_mv2, 1)
                    vec.wait_ge(s_mv2, (b + 1) * LB)
                    ts = slice(b * LB, (b + 1) * LB)
                    dve.tensor_scalar(var2[:, ts], mv2[:, ts, 1], LN_EPS, None, ALU.add).then_inc(s_var2, 1)

                def rstd_of(b):
                    ts = slice(b * LB, (b + 1) * LB)
                    vec.wait_ge(s_root2, b + 1)
                    rsqrt(link, dve, rstd2[:, ts], root2[:, ts], var2[:, ts], tmp2[:, ts])
                    dve.scalar_tensor_tensor(out=nmr2[:, ts], in0=mv2[:, ts, 0], scalar=-1.0, in1=rstd2[:, ts],
                                             op0=ALU.mult, op1=ALU.mult).then_inc(s_r2, 1)

                def choose_start(b):
                    vec.wait_ge(s_lT, b + 1)
                    lg = lt_ps[:, 0:LB * NE].rearrange("p (t e) -> p t e", e=NE)
                    link(dve.tensor_reduce(lmax[:], lg, AX.X, ALU.max))
                    link(dve.tensor_tensor(is_max[:], lg, lmax[:].unsqueeze(2).broadcast_to([P, LB, NE]),
                                           ALU.is_ge))

                def choose(b):
                    down = down32[:].unsqueeze(1).broadcast_to([P, LB, NE])
                    link(dve.tensor_tensor(is_max[:], is_max[:], down, ALU.mult))
                    link(dve.tensor_reduce(lfirst[:], is_max[:], AX.X, ALU.max))
                    hits = dve.tensor_tensor(onehot[:, b * LB:(b + 1) * LB, :], down,
                                             lfirst[:].unsqueeze(2).broadcast_to([P, LB, NE]), ALU.is_equal)
                    if b < NB - 1:
                        hits.then_inc(s_oh, 1)
                    else:
                        link(hits)
                        dve.tensor_tensor(onehot[:, T - 1, :], onehot[:, T - 1, :], valid[:],
                                          ALU.mult).then_inc(s_oh, 1)

                def new_pages(b):
                    vec.wait_ge(s_count, b + 1)
                    link(dve.tensor_scalar(full[:], full_at[:], count_ps, 0.0, ALU.is_lt, ALU.add,
                                           accum_out=pages[:, b + 1:b + 2]))
                    dve.tensor_tensor(new[:, b:b + 1], pages[:, b + 1:b + 2], pages[:, b:b + 1],
                                      ALU.subtract).then_inc(s_new, 1)

                def shifts_of(b):
                    vec.wait_ge(s_first, b + 1)
                    old, limit, change = (shifts[:, b, i:i + 1] for i in range(3))
                    link(dve.tensor_tensor(new_shift[:, b:b + 1], page_ps, pages[:, b:b + 1], ALU.subtract))
                    link(dve.tensor_tensor(limit, old, pages[:, b:b + 1], ALU.add))
                    link(dve.tensor_tensor(change, new_shift[:, b:b + 1], old, ALU.subtract))
                    dve.tensor_tensor(shift_diag[:], ident[0:NE, 0:NE].unsqueeze(1).broadcast_to([NE, 3, NE]),
                                      shifts[:, b, :].unsqueeze(2).broadcast_to([NE, 3, NE]), ALU.mult)\
                       .then_inc(s_shift, 1)
                    link(dve.scalar_tensor_tensor(out=moved[:, b:b + 1], in0=new[:, b:b + 1], scalar=0.0,
                                                  in1=change, op0=ALU.is_gt, op1=ALU.mult))
                    link(dve.tensor_tensor(shifts[:, b + 1, 0:1], old, moved[:, b:b + 1], ALU.add))

                def place(b):
                    vec.wait_ge(s_shiftb, b + 1)
                    ts = slice(b * LB, (b + 1) * LB)
                    link(dve.tensor_tensor(picked[:], pick_ps, onehot[:, ts, :].unsqueeze(1)
                                           .broadcast_to([P, 3, LB, NE]), ALU.mult))
                    link(dve.tensor_reduce(per_token[:], picked[:], AX.X, ALU.add))
                    shifted, limit, change = (per_token[:, i, :] for i in range(3))
                    link(dve.tensor_tensor(beyond[:], shifted, limit, ALU.is_ge))
                    link(dve.tensor_tensor(beyond[:], beyond[:], change, ALU.mult))
                    dve.tensor_tensor(row[:, ts], shifted, beyond[:], ALU.add).then_inc(s_row, 1)

                vec.wait_ge(s_c, 11)
                residual(0)
                rstd_of(0)
                for b in range(NB):
                    if b + 1 < NB:
                        residual(b + 1)
                    if b >= 1:
                        new_pages(b - 1)
                    if b + 1 < NB:
                        rstd_of(b + 1)
                    if b == NB - 1:
                        shifts_of(b - 1)
                        place(b - 1)
                    choose_start(b)
                    if 1 <= b < NB - 1:
                        shifts_of(b - 1)
                    choose(b)
                    if 1 <= b < NB - 1:
                        place(b - 1)
                new_pages(NB - 1)
                shifts_of(NB - 1)
                place(NB - 1)
                link(dve.tensor_tensor(first_new[:], new_shift[:], pages[:, 0:NB], ALU.add))
                link(dve.tensor_tensor(new_end[:], first_new[:], new[:], ALU.add))
                page = page_id[:].unsqueeze(1).broadcast_to([NE, NB, CHUNKS])
                link(dve.tensor_tensor(from_first[:], page, first_new[:].unsqueeze(2)
                                       .broadcast_to([NE, NB, CHUNKS]), ALU.is_ge))
                link(dve.tensor_tensor(to_end[:], page, new_end[:].unsqueeze(2).broadcast_to([NE, NB, CHUNKS]),
                                       ALU.is_lt))
                link(dve.tensor_tensor(from_first[:], from_first[:], to_end[:], ALU.mult))
                dve.tensor_reduce(owned[:], from_first[:].rearrange("e b q -> e q b"), AX.X, ALU.add)\
                   .then_inc(s_owned, 1)
                vec.wait_ge(s_exp, 1)
                dve.tensor_copy(expert[:], expert_ps)
                dve.tensor_copy(page_total[:], total_ps)

        PARTS = 4
        PART = SLOTS // PARTS
        WS = 4
        FIRST = ceil_div(NE, SLOTS) * SLOTS + SLOTS
        assert CHUNKS % SLOTS == 0 and FIRST < CHUNKS

        def run_pages(p0, p1, tag, ctx):
            NPG = p1 - p0
            RC = NPG // SLOTS
            xg = sb(f"xg{tag}", [P, SLOTS, DW], F32, ctx)
            wc = sb(f"wc{tag}", [P, WS, EWC], F32, ctx)
            xgT = sb(f"xgT{tag}", [P, 2, KD, P], F32, ctx)
            hg = sb(f"hg{tag}", [EH + 1, 2, P], F32, ctx)
            og = sb(f"og{tag}", [P, SLOTS, D], F32, ctx)
            ids = sb(f"ids{tag}", [P, SLOTS], I32, ctx)
            t_ps = psum(f"t_ps{tag}", [P, 2, 512], F32, ctx)
            u_ps = psum(f"u_ps{tag}", [P, 2, 512], F32, ctx)
            d_ps = psum(f"d_ps{tag}", [P, 2, 512], F32, ctx)
            s_in = [sem(f"pages_in{h}{tag}", ctx) for h in range(PARTS)]
            s_st = [sem(f"page_added{i}{tag}", ctx) for i in range(SLOTS)]
            s_wc = sem(f"expert_copied{tag}", ctx)
            s_t = sem(f"page_turned{tag}", ctx)
            s_tk = sem(f"page_turned_kept{tag}", ctx)
            s_u = sem(f"expert_up{tag}", ctx)
            s_uk = sem(f"expert_relu{tag}", ctx)
            s_d = sem(f"expert_down{tag}", ctx)
            s_dk = sem(f"expert_kept{tag}", ctx)
            s_one = sem(f"ones_row{tag}", ctx)
            block = ctx.enter_context(nc.Block())

            @block.gpsimd
            def _(pool):
                pool_.memset(hg[EH:EH + 1], 1.0).then_inc(s_one, 1)
                for q in range(p1 - p0):
                    i = q % SLOTS
                    pool.wait_ge(s_dk, 2 * (q + 1))
                    pool_.indirect_dma_start(
                        out, bass.IndirectOffsetOnAxis(ap=ids[:, i:i + 1], axis=0), og[:, i, :], None,
                        compute_op=ALU.add
                    ).then_inc(s_st[i], 16)
                for s in s_st:
                    pool.wait_ge(s, 16 * RC)

            @block.sync
            def _(sp):
                def load(r, h, later):
                    if later:
                        sp.wait_ge(s_dk, (r * SLOTS + (h + 1) * PART - SLOTS) * 2)
                    sp.dma_start(xg[:, h * PART:(h + 1) * PART, :],
                                 by_expert.rearrange("(q p) d -> p q d", p=P)
                                 [:, bass.ds(r * SLOTS + p0 + h * PART, PART), :]).then_inc(s_in[h], 16)

                for h in range(PARTS):
                    load(0, h, False)
                with sp.Fori(1, RC) as r:
                    for h in range(PARTS):
                        load(r, h, True)

            @block.tensor
            def _(pe):
                def turn(c, i, later):
                    if i % PART == 0:
                        pe.wait_ge(s_in[i // PART], (c - i) * (16 // SLOTS) + 16)
                    if later or i >= 2:
                        pe.wait_ge(s_tk, c - 1)
                    for k in range(KD):
                        last = pe_.transpose(t_ps[:, i % 2, k * P:(k + 1) * P],
                                             xg[:, i, 0:D].rearrange("p (d k) -> p k d", k=KD)[:, k, :], ident[:])
                    last.then_inc(s_t, 1)

                def up(c, i, later):
                    pe.wait_ge(s_tk, c + 1)
                    pe.wait_ge(s_wc, c + 1)
                    if later or i >= 2:
                        pe.wait_ge(s_uk, c - 1)
                    for k in range(KD):
                        last = pe_.matmul(u_ps[0:EH, i % 2, 0:P], wc[:, i % WS, k * EH:(k + 1) * EH],
                                          xgT[:, i % 2, k, :], start=(k == 0), stop=(k == KD - 1))
                    last.then_inc(s_u, 1)

                def down(c, i, later):
                    pe.wait_ge(s_uk, c + 1)
                    if later or i >= 2:
                        pe.wait_ge(s_dk, (c - 1) * 2)
                    pe_.matmul(d_ps[:, i % 2, 0:D], hg[:, i % 2, :], wc[0:EH + 1, i % WS, C1:C2], start=True,
                               stop=True).then_inc(s_d, 1)

                turn(0, 0, False)
                turn(1, 1, False)
                up(0, 0, False)
                for i in range(2, SLOTS):
                    turn(i, i, False)
                    up(i - 1, i - 1, False)
                    down(i - 2, i - 2, False)
                with pe.Fori(1, RC) as r:
                    c = r * SLOTS
                    for i in range(SLOTS):
                        turn(c + i, i, True)
                        up(c + i - 1, (i - 1) % SLOTS, True)
                        down(c + i - 2, (i - 2) % SLOTS, True)
                up(NPG - 1, SLOTS - 1, True)
                down(NPG - 2, SLOTS - 2, True)
                down(NPG - 1, SLOTS - 1, True)

            @block.scalar
            def _(act):
                act.wait_ge(s_one, 1)

                def keep_turned(c, i, later):
                    act.wait_ge(s_t, c + 1)
                    if later or i >= 2:
                        act.wait_ge(s_u, c - 1)
                    act_.activation(xgT[:, i % 2].rearrange("p k n -> p (k n)"), t_ps[:, i % 2, 0:KD * P],
                                    ACT.Copy).then_inc(s_tk, 1)

                def relu(c, i, later):
                    act.wait_ge(s_u, c + 1)
                    if later or i >= 2:
                        act.wait_ge(s_d, c - 1)
                    act_.activation(hg[0:EH, i % 2, :], u_ps[0:EH, i % 2, 0:P], ACT.Relu,
                                    bias=wc[0:EH, i % WS, C2:C2 + 1]).then_inc(s_uk, 1)

                keep_turned(0, 0, False)
                for i in range(1, SLOTS):
                    keep_turned(i, i, False)
                    relu(i - 1, i - 1, False)
                with act.Fori(1, RC) as r:
                    c = r * SLOTS
                    for i in range(SLOTS):
                        keep_turned(c + i, i, True)
                        relu(c + i - 1, (i - 1) % SLOTS, True)
                relu(NPG - 1, SLOTS - 1, True)

            @block.vector
            def _(vec):
                def experts_of(r):
                    return nc.values_load_multi_w_load_instructions(
                        expert[0:1, bass.ds(r * WS + p0, WS)], engines=[mybir.EngineType.DVE], min_val=0,
                        max_val=NE - 1, skip_runtime_bounds_check_because="an expert is always one of the NE")[1]

                def fetch(e, c, i, later):
                    if later or i >= WS:
                        vec.wait_ge(s_d, c - WS + 1)
                    dve.tensor_copy(wc[:, i % WS, :], ew[:, bass.ds(e, 1), :].rearrange("p a n -> p (a n)"))\
                       .then_inc(s_wc, 1)

                def keep(c, i, later):
                    vec.wait_ge(s_d, c + 1)
                    if later:
                        vec.wait_ge(s_st[i], (c - i) * (16 // SLOTS))
                    dve.tensor_scalar(og[:, i, :], d_ps[:, i % 2, 0:D], 0.0, None, ALU.max).then_inc(s_dk, 1)
                    dve.tensor_copy(ids[:, i:i + 1], xg[:, i, D:DW].bitcast(I32)).then_inc(s_dk, 1)

                for c in range(2 * SLOTS):
                    if c % WS == 0:
                        es_ = experts_of(c // WS)
                    fetch(es_[c % WS], c, c % SLOTS, c >= SLOTS)
                    if c >= 2:
                        keep(c - 2, (c - 2) % SLOTS, c - 2 >= SLOTS)

                def round_of(r):
                    for i in range(SLOTS):
                        if i % WS == 0:
                            es_ = experts_of(r * (SLOTS // WS) + i // WS)
                        fetch(es_[i % WS], r * SLOTS + i, i, True)
                        keep(r * SLOTS + i - 2, (i - 2) % SLOTS, True)

                if RC > 2:
                    with vec.Fori(2, RC) as r:
                        round_of(r)
                keep(NPG - 2, SLOTS - 2, True)
                keep(NPG - 1, SLOTS - 1, True)

        with ExitStack() as ctx:
            run_pages(0, FIRST, "", ctx)
        pages_used = nc.values_load(page_total[0:1, 0:1], min_val=0, max_val=CHUNKS)
        with nc.If(pages_used > FIRST):
            nc.all_engine_barrier()
            with ExitStack() as ctx:
                run_pages(FIRST, CHUNKS, "_more", ctx)


_INS = ["x", "src", "dst", "L0_gnn_eps", "L0_gnn_W1", "L0_gnn_b1", "L0_gnn_W2", "L0_gnn_b2", "L0_gnn_gamma",
        "L0_gnn_beta", "L0_ffn_router_w", "L0_ffn_router_b", "L0_ffn_W1", "L0_ffn_b1", "L0_ffn_W2", "L0_ffn_b2"]


def kernel(**inputs):
    import numpy as _np
    import concourse.bacc as _bacc
    from concourse import mybir as _mybir
    from concourse.bass_utils import run_bass_kernel_spmd as _run

    nc = _bacc.Bacc("TRN2", target_bir_lowering=False, num_devices=1)
    arrays, args = {}, []
    for name in _INS:
        a = _np.ascontiguousarray(inputs[name])
        arrays[f"in_{name}_dram"] = a
        args.append(nc.dram_tensor(f"in_{name}_dram", a.shape, _mybir.dt.from_np(a.dtype), kind="ExternalInput").ap())
    nodes, width = arrays["in_x_dram"].shape
    args.append(nc.dram_tensor("out_dram", (nodes + SPARE_ROWS, width), _mybir.dt.float32,
                               kind="ExternalOutput").ap())
    gnn_moe_kernel(nc, *args)
    r = _run(nc, [arrays], core_ids=[0])
    return r.results[0]["out_dram"][:nodes]
```
